# Optimizing a Trainium2 kernel written in Bass

```python
import numpy as np
import jax
import jax.numpy as jnp

def _softmax(x, axis=-1):
    return jax.nn.softmax(x, axis=axis)

def _gelu(x):
    return jax.nn.gelu(x, approximate=True)

def _silu(x):
    return jax.nn.silu(x)

def _sigmoid(x):
    return jax.nn.sigmoid(x)

def _layernorm(x, axis=-1, eps=1e-05):
    m = jnp.mean(x, axis=axis, keepdims=True)
    v = jnp.var(x, axis=axis, keepdims=True)
    return (x - m) / jnp.sqrt(v + eps)

def _scatter_add(tgt, idx, src, axis=0):
    return tgt.at[idx].add(src)

def _segment_sum(src, seg, n):
    return jax.ops.segment_sum(src, seg, n)
kernel_name = 'mk_flamingo_gated_d2_seqx_r8_84c07f'

def setup_inputs(seed: int=0):
    np.random.seed(seed)
    _w = jnp.asarray

    def _rec_inputs():
        import jax
        import jax.numpy as jnp
        _rk = jax.random.key(seed)
        x = 7.22e-05 + 1 * jax.random.normal(jax.random.fold_in(_rk, 1), (8, 256, 128), jnp.float32)
        _lenS = 256 - jax.random.randint(jax.random.fold_in(_rk, 7), (8,), 0, max(1, 256 // 4) + 1, jnp.int32)
        _lenS2 = 256 - jax.random.randint(jax.random.fold_in(_rk, 8), (8,), 0, max(1, 256 // 4) + 1, jnp.int32)
        _ctx_1024P = jax.random.normal(jax.random.fold_in(_rk, 11), (8, 16, 128), jnp.float32)
        _ctx_1024c = jax.random.dirichlet(jax.random.fold_in(_rk, 511), 0.3 * jnp.ones((16,), jnp.float32), (8, 256))
        _ctx_1024t = jnp.einsum('bsk,bkd->bsd', _ctx_1024c, _ctx_1024P)
        _ctx_1024t = _ctx_1024t * jax.lax.rsqrt(jnp.mean(jnp.square(_ctx_1024t)) + 1e-12) * 0.953939
        ctx_1024 = 4.13588e-05 + 0.999923 * (_ctx_1024t + 0.3 * jax.random.normal(jax.random.fold_in(_rk, 611), (8, 256, 128), jnp.float32))
        _g = jax.random.normal(jax.random.fold_in(_rk, 9001), (2, 2), jnp.float32)
        _g = jnp.sign(_g) * jnp.maximum(jnp.abs(_g), 1.0) + (_g == 0) * 1.0
        g_xattn = _g[0]
        g_ffn = _g[1]
        return (x, ctx_1024, g_xattn, g_ffn)
    x, ctx_1024, g_xattn, g_ffn = _rec_inputs()

    def _L0_xattn_setup():
        import jax, jax.numpy as jnp
        import numpy as np
        B, S, D_IN, D_OUT = (4, 256, 128, 128)
        key = jax.random.key(seed)
        ks = jax.random.split(key, 6)
        scale = 1.0 / np.sqrt(D_IN)
        return {'inputs_for_keys': jax.random.normal(ks[0], (B, S, D_IN), jnp.float32), 'inputs_for_values': jax.random.normal(ks[1], (B, S, D_IN), jnp.float32), 'inputs_for_queries': jax.random.normal(ks[2], (B, S, D_IN), jnp.float32), 'WK': jax.random.uniform(ks[3], (D_IN, D_OUT), jnp.float32, -scale, scale), 'WQ': jax.random.uniform(ks[4], (D_IN, D_OUT), jnp.float32, -scale, scale), 'WV': jax.random.uniform(ks[5], (D_IN, D_OUT), jnp.float32, -scale, scale)}
    _L0_xattn_all = _L0_xattn_setup()
    _L0_xattn_in = {k: v for k, v in _L0_xattn_all.items() if k in ('WK', 'WQ', 'WV')}
    del _L0_xattn_all

    def _L0_ffn_setup():
        import jax, jax.numpy as jnp
        import numpy as np
        QMAX = 127.0

        def _ste_round(v):
            return v + jax.lax.stop_gradient(jnp.round(v) - v)

        def _act_fake_quant(x, clip_factor):
            scale = jax.nn.sigmoid(clip_factor) * jnp.max(jnp.abs(x)) / QMAX
            return jnp.clip(_ste_round(x / scale), -QMAX - 1.0, QMAX) * scale

        def _weight_fake_quant(w):
            scale = jnp.max(jnp.abs(w), axis=1, keepdims=True) / QMAX
            return jnp.clip(_ste_round(w / scale), -QMAX - 1.0, QMAX) * scale
        key = jax.random.key(seed)
        k1, k2, k3, k4 = jax.random.split(key, 4)
        B, S, H, I = (8, 1024, 128, 352)
        return {'x': jax.random.normal(k1, (B, S, H), dtype=jnp.float32), 'clip_x': jnp.full((1,), 4.0, dtype=jnp.float32), 'clip_down': jnp.full((1,), 4.0, dtype=jnp.float32), 'w_gate': jax.random.normal(k2, (I, H), dtype=jnp.float32) * 0.02, 'w_up': jax.random.normal(k3, (I, H), dtype=jnp.float32) * 0.02, 'w_down': jax.random.normal(k4, (H, I), dtype=jnp.float32) * 0.02}
    _L0_ffn_all = _L0_ffn_setup()
    _L0_ffn_in = {k: v for k, v in _L0_ffn_all.items() if k in ('clip_x', 'clip_down', 'w_gate', 'w_up', 'w_down')}
    del _L0_ffn_all

    def _L1_xattn_setup():
        import jax, jax.numpy as jnp
        import numpy as np
        D_MODEL = 128
        N_HEADS = 16
        key = jax.random.key(seed)
        ks = jax.random.split(key, 11)
        B, L, S, D = (2, 256, 256, D_MODEL)
        s = 1.0 / np.sqrt(D)
        return {'Q': jax.random.normal(ks[0], (B, L, D), jnp.float32), 'K': jax.random.normal(ks[1], (B, S, D), jnp.float32), 'V': jax.random.normal(ks[2], (B, S, D), jnp.float32), 'Wq': jax.random.normal(ks[3], (D, D), jnp.float32) * s, 'bq': jnp.zeros((D,), jnp.float32), 'Wk': jax.random.normal(ks[4], (D, D), jnp.float32) * s, 'bk': jnp.zeros((D,), jnp.float32), 'Wv': jax.random.normal(ks[5], (D, D), jnp.float32) * s, 'bv': jnp.zeros((D,), jnp.float32), 'We': jax.random.normal(ks[6], (D, D), jnp.float32) * s, 'be': jnp.zeros((D,), jnp.float32)}
    _L1_xattn_all = _L1_xattn_setup()
    _L1_xattn_in = {k: v for k, v in _L1_xattn_all.items() if k in ('Wq', 'bq', 'Wk', 'bk', 'Wv', 'bv', 'We', 'be')}
    del _L1_xattn_all

    def _L1_ffn_setup():
        import jax, jax.numpy as jnp
        import numpy as np
        B, S, D, H, E, K = (4, 256, 128, 512, 8, 2)
        key = jax.random.key(seed)
        ks = jax.random.split(key, 8)
        scale = 0.02
        x = jax.random.normal(ks[0], (B, S, D), dtype=jnp.float32)
        gate_w = jax.random.normal(ks[1], (D, E), dtype=jnp.float32) * scale
        gate_b = jnp.zeros((E,), dtype=jnp.float32)
        w1 = jax.random.normal(ks[2], (E, D, H), dtype=jnp.float32) * scale
        b1 = jnp.zeros((E, H), dtype=jnp.float32)
        w2 = jax.random.normal(ks[3], (E, H, D), dtype=jnp.float32) * scale
        b2 = jnp.zeros((E, D), dtype=jnp.float32)
        return {'x': x, 'gate_w': gate_w, 'gate_b': gate_b, 'w1': w1, 'b1': b1, 'w2': w2, 'b2': b2}
    _L1_ffn_all = _L1_ffn_setup()
    _L1_ffn_in = {k: v for k, v in _L1_ffn_all.items() if k in ('gate_w', 'gate_b', 'w1', 'b1', 'w2', 'b2')}
    del _L1_ffn_all
    return {'x': x, 'ctx_1024': ctx_1024, 'g_xattn': g_xattn, 'g_ffn': g_ffn, 'L0_xattn_WK': _L0_xattn_in['WK'], 'L0_xattn_WQ': _L0_xattn_in['WQ'], 'L0_xattn_WV': _L0_xattn_in['WV'], 'L0_ffn_clip_x': _L0_ffn_in['clip_x'], 'L0_ffn_clip_down': _L0_ffn_in['clip_down'], 'L0_ffn_w_gate': _L0_ffn_in['w_gate'], 'L0_ffn_w_up': _L0_ffn_in['w_up'], 'L0_ffn_w_down': _L0_ffn_in['w_down'], 'L1_xattn_Wq': _L1_xattn_in['Wq'], 'L1_xattn_bq': _L1_xattn_in['bq'], 'L1_xattn_Wk': _L1_xattn_in['Wk'], 'L1_xattn_bk': _L1_xattn_in['bk'], 'L1_xattn_Wv': _L1_xattn_in['Wv'], 'L1_xattn_bv': _L1_xattn_in['bv'], 'L1_xattn_We': _L1_xattn_in['We'], 'L1_xattn_be': _L1_xattn_in['be'], 'L1_ffn_gate_w': _L1_ffn_in['gate_w'], 'L1_ffn_gate_b': _L1_ffn_in['gate_b'], 'L1_ffn_w1': _L1_ffn_in['w1'], 'L1_ffn_b1': _L1_ffn_in['b1'], 'L1_ffn_w2': _L1_ffn_in['w2'], 'L1_ffn_b2': _L1_ffn_in['b2']}

def reference(x, ctx_1024, g_xattn, g_ffn, L0_xattn_WK, L0_xattn_WQ, L0_xattn_WV, L0_ffn_clip_x, L0_ffn_clip_down, L0_ffn_w_gate, L0_ffn_w_up, L0_ffn_w_down, L1_xattn_Wq, L1_xattn_bq, L1_xattn_Wk, L1_xattn_bk, L1_xattn_Wv, L1_xattn_bv, L1_xattn_We, L1_xattn_be, L1_ffn_gate_w, L1_ffn_gate_b, L1_ffn_w1, L1_ffn_b1, L1_ffn_w2, L1_ffn_b2):
    import jax
    import jax.numpy as jnp

    def _L0_xattn_ref(inputs_for_keys, inputs_for_values, inputs_for_queries, WK, WQ, WV):
        import jax, jax.numpy as jnp
        import numpy as np
        B, S, D_IN, D_OUT = (4, 256, 128, 128)
        keys = jnp.einsum('bsd,de->bse', inputs_for_keys, WK)
        values = jnp.einsum('bsd,de->bse', inputs_for_values, WV)
        queries = jnp.einsum('bsd,de->bse', inputs_for_queries, WQ)
        d_k = keys.shape[-1]
        scores = jnp.einsum('bqe,bke->bqk', queries, keys) / jnp.sqrt(jnp.float32(d_k))
        q_idx = jnp.arange(S)[:, None]
        k_idx = jnp.arange(S)[None, :]
        scores = jnp.where(k_idx > q_idx, -jnp.inf, scores)
        att = jax.nn.softmax(scores, axis=-1)
        out = jnp.einsum('bqk,bke->bqe', att, values)
        return out

    def _L0_ffn_ref(x, clip_x, clip_down, w_gate, w_up, w_down):
        import jax, jax.numpy as jnp
        import numpy as np
        QMAX = 127.0

        def _ste_round(v):
            return v + jax.lax.stop_gradient(jnp.round(v) - v)

        def _act_fake_quant(x, clip_factor):
            scale = jax.nn.sigmoid(clip_factor) * jnp.max(jnp.abs(x)) / QMAX
            return jnp.clip(_ste_round(x / scale), -QMAX - 1.0, QMAX) * scale

        def _weight_fake_quant(w):
            scale = jnp.max(jnp.abs(w), axis=1, keepdims=True) / QMAX
            return jnp.clip(_ste_round(w / scale), -QMAX - 1.0, QMAX) * scale
        xq = _act_fake_quant(x, clip_x[0])
        gate = jnp.einsum('bsh,ih->bsi', xq, _weight_fake_quant(w_gate))
        up = jnp.einsum('bsh,ih->bsi', xq, _weight_fake_quant(w_up))
        h = _act_fake_quant(jax.nn.silu(gate) * up, clip_down[0])
        return jnp.einsum('bsi,hi->bsh', h, _weight_fake_quant(w_down))

    def _L1_xattn_ref(Q, K, V, Wq, bq, Wk, bk, Wv, bv, We, be):
        import jax, jax.numpy as jnp
        import numpy as np
        D_MODEL = 128
        N_HEADS = 16
        B, L, D = Q.shape
        S = K.shape[1]
        H = N_HEADS
        E = D // H
        q = (Q @ Wq + bq).reshape(B, L, H, E)
        k = (K @ Wk + bk).reshape(B, S, H, E)
        v = (V @ Wv + bv).reshape(B, S, H, E)
        scale = 1.0 / np.sqrt(E)
        scores = jnp.einsum('blhe,bshe->bhls', q, k)
        A = jax.nn.softmax(scale * scores, axis=-1)
        out = jnp.einsum('bhls,bshd->blhd', A, v).reshape(B, L, H * E)
        return out @ We + be

    def _L1_ffn_ref(x, gate_w, gate_b, w1, b1, w2, b2):
        import jax, jax.numpy as jnp
        import numpy as np
        B, S, D, H, E, K = (4, 256, 128, 512, 8, 2)
        b, s, d = x.shape
        xf = x.reshape(-1, d)
        T = xf.shape[0]
        gates = xf @ gate_w + gate_b
        scores, idx = jax.lax.top_k(gates, K)
        g = jax.nn.softmax(scores, axis=-1)
        Wte = jnp.zeros((T, E), dtype=xf.dtype).at[jnp.arange(T)[:, None], idx].add(g)

        def body(acc, p):
            w1e, b1e, w2e, b2e, we = p
            h = jax.nn.gelu(xf @ w1e + b1e, approximate=False)
            y = h @ w2e + b2e
            return (acc + we[:, None] * y, None)
        out, _ = jax.lax.scan(body, jnp.zeros_like(xf), (w1, b1, w2, b2, Wte.T))
        return out.reshape(b, s, d)
    x = x + jnp.tanh(g_xattn[0]) * _L0_xattn_ref(_layernorm(x, axis=-1), ctx_1024, ctx_1024, L0_xattn_WK, L0_xattn_WQ, L0_xattn_WV)
    x = x + jnp.tanh(g_ffn[0]) * _L0_ffn_ref(_layernorm(x, axis=-1), L0_ffn_clip_x, L0_ffn_clip_down, L0_ffn_w_gate, L0_ffn_w_up, L0_ffn_w_down)
    x = x + jnp.tanh(g_xattn[1]) * _L1_xattn_ref(_layernorm(x, axis=-1), ctx_1024, ctx_1024, L1_xattn_Wq, L1_xattn_bq, L1_xattn_Wk, L1_xattn_bk, L1_xattn_Wv, L1_xattn_bv, L1_xattn_We, L1_xattn_be)
    x = x + jnp.tanh(g_ffn[1]) * _L1_ffn_ref(_layernorm(x, axis=-1), L1_ffn_gate_w, L1_ffn_gate_b, L1_ffn_w1, L1_ffn_b1, L1_ffn_w2, L1_ffn_b2)
    return x

_drawn_inputs = setup_inputs


def setup_inputs(seed=0):
    import zlib

    import numpy as np

    out = dict(_drawn_inputs(seed))
    spreads = {'g_ffn': (-1.0, 0.6),
     'L1_xattn_bq': (0.0, 1.148),
     'L1_xattn_bk': (0.0, 2.0),
     'L1_xattn_bv': (0.0, 0.268),
     'L1_xattn_be': (0.0, 0.1),
     'L1_ffn_gate_b': (0.0, 0.328),
     'L1_ffn_b1': (0.0, 0.64),
     'L1_ffn_b2': (0.0, 0.371)}
    factors = {'L0_xattn_WK': 3.396,
     'L0_xattn_WQ': 3.479,
     'L0_ffn_w_gate': 6.754,
     'L0_ffn_w_up': 6.645,
     'L0_ffn_w_down': 6.543,
     'L1_ffn_w1': 4.185}
    for name, (base, spread) in spreads.items():
        noise = np.random.default_rng([zlib.crc32(name.encode()), seed]).standard_normal(out[name].shape)
        drawn = base * np.exp(spread * noise) if base else spread * noise
        out[name] = jnp.asarray(drawn.astype(out[name].dtype))
    for name, factor in factors.items():
        out[name] = (out[name] * factor).astype(out[name].dtype)
    return out
```

```python
from contextlib import ExitStack

import numpy as np

import concourse.bass as bass
from concourse import mybir

F32, F32R, BF16 = mybir.dt.float32, mybir.dt.float32r, mybir.dt.bfloat16
U32 = mybir.dt.uint32
ACT = mybir.ActivationFunctionType
ALU = mybir.AluOpType
AX = mybir.AxisListType
ds = bass.ds

P = 128
BATCH, SEQ, DM = 8, 256, 128
TOK = BATCH * SEQ
TILES = TOK // P
HEADS, HD = 16, 8
FF0 = 352
CH = 3
CHW = [128, 128, FF0 - 256]
EXPERTS, HID = 8, 512
HC = HID // P
BLK = 512
NBLK = TOK // BLK
BT = BLK // P
LN1, LN2, LN3, LN4 = 0, 4, 4 + BATCH, 4 + BATCH + NBLK

EPS = 1e-5
QMAX = 127.0
MAGIC = 1.5 * 2.0 ** 23
MASKED = -1e30
SC0 = float(1.0 / np.sqrt(np.float32(DM)))
SC1 = float(1.0 / np.sqrt(HD))

QUADS, GROUPS = 4, 4
Q_HI, Q_LO = (0, 1), (2,)
K_HI, K_LO = (0, 2), (1,)
MROW = 24


class Step:

    def __init__(self, it, c, count):
        self.it, self.c, self.count = it, c, count
        self.par = c % 2

    @property
    def n(self):
        return 2 * self.it + self.c

    @property
    def half(self):
        return self.it + self.c // 2

    def __add__(self, k):
        return Step(self.it, self.c + k, self.count)

    @property
    def valid(self):
        return not isinstance(self.it, int) or 0 <= self.n < self.count


def wait(eng, sem, value):
    if not isinstance(value, int) or value > 0:
        eng.wait_ge(sem, value)


def skewed(eng, step, count):
    step(Step(0, -1, count))
    step(Step(0, 0, count))
    with eng.Fori(0, (count - 2) // 2) as it:
        for u in range(2):
            step(Step(it, 1 + u, count))
    step(Step(0, count - 1, count))
    step(Step(0, count, count))


def paired(eng, body, count):
    body(Step(0, 0, count), Step(0, 1, count))
    with eng.Fori(0, (count - 2) // 2) as it:
        body(Step(it, 2, count), Step(it, 3, count))


def flamingo(nc, t):
    ctx = ExitStack()
    with ctx:
        def sb(name, shape, dt=F32, scope=ctx):
            return scope.enter_context(nc.sbuf_tensor(name, shape, dt))

        sems = {}

        def sem(name):
            if name not in sems:
                sems[name] = ctx.enter_context(nc.semaphore(name))
            return sems[name]

        bank = [ctx.enter_context(nc.psum_tensor(f"bank{i}", [P, 512], F32)) for i in range(8)]

        x = sb("x", [P, TOK])
        ident = sb("ident", [P, P])
        ident_r = sb("ident_r", [P, P], F32R)
        ident_b = sb("ident_b", [P, P], BF16)
        wk0, wq0, wv0 = (sb(n, [P, DM]) for n in ("wk0", "wq0", "wv0"))
        wk1, wq1, wv1 = (sb(n, [P, DM]) for n in ("wk1", "wq1", "wv1"))
        bv1 = sb("bv1", [P, DM])
        rows = sb("rows", [64, P])
        cols = sb("cols", [P, 64])
        B1C, BQC, BKC = 0, 32, 33
        causal = sb("causal", [P, 384])
        g_in = sb("g_in", [P, 4])
        tg = sb("tg", [P, 4])
        clip = sb("clip", [P, 2])
        sig = sb("sig", [P, 2])
        magic = sb("magic", [P, 1])
        half_neg = sb("half_neg", [P, BT])
        eps = sb("eps_row", [P, BT])
        ones = sb("ones", [P, P])
        sel = {n: sb(f"sel_{n}", [P, GROUPS, P], F32R) for n in ("qhi", "qlo")}
        den_perm = sb("den_perm", [P, P])
        we_pad = sb("we_pad", [P, 2, DM])
        neg_max_pad = [sb(f"neg_max_pad{i}", [P, 2, GROUPS, P], F32R) for i in range(2)]
        stats = [sb(f"stats{i}", [P, BT, 6]) for i in range(2)]
        mv = [sb(f"mv_{i}", [P, BT, 2]) for i in range(2)]
        var_eps = [sb(f"var_eps{i}", [P, BT]) for i in range(2)]
        rstd = [sb(f"rstd_{i}", [P, BT]) for i in range(2)]
        wait_taker = sb("wait_taker", [P, 4])
        mv1 = sb("mv_first", [P, TILES, 2])
        rstd1 = sb("rstd_first", [P, TILES])
        wq_in = sb("wq_in", [P, 2 * CH, DM])
        wd_in = sb("wd_in", [P, FF0])
        w_amax = sb("w_amax", [P, 8])
        w_scale = sb("w_scale", [P, 8])
        w_inv = sb("w_inv", [P, 8])
        wgu_t = sb("wgu_t", [P, 2 * CH, P], BF16)
        wd_t = sb("wd_t", [P, CH, DM], BF16)
        sd_row = sb("sd_row", [P, DM])
        sd_all = sb("sd_all", [P, DM])
        gate_w = sb("gate_w", [P, EXPERTS])
        gate_hi = sb("gate_hi", [P, EXPERTS], F32R)
        gate_lo = sb("gate_lo", [P, EXPERTS], F32R)
        gate_b = sb("gate_b", [EXPERTS, 1])
        b2 = sb("b2", [EXPERTS, DM])
        xt_hi = sb("xt_hi", [P, TOK], F32R)
        xt_lo = sb("xt_lo", [P, TOK], F32R)
        smalls = sb("smalls", [P, 32])

        mid = ExitStack()
        v_wide = sb("v_wide", [P, TILES, BLK], scope=mid)
        q_hi = sb("q_hi", [P, TOK], F32R, mid)
        q_lo = sb("q_lo", [P, TOK], F32R, mid)
        k_all = sb("k_all", [P, GROUPS, TOK], F32R, mid)

        ab = ExitStack()
        k_hi = sb("k_hi", [P, TOK], F32R, ab)
        k_lo = sb("k_lo", [P, TOK], F32R, ab)
        xn2_t = sb("xn2_t", [P, TOK], scope=ab)
        amax0 = sb("amax0", [P, BATCH + 8], scope=ab)
        a = ExitStack()
        w_tmp = sb("w_tmp", [P, 2 * CH * DM], scope=a)
        w_q8 = sb("w_q8", [P, 2 * CH, DM], BF16, a)
        wd_tmp = sb("wd_tmp", [P, FF0], scope=a)
        wd_q8 = sb("wd_q8", [P, FF0], BF16, a)
        ctx_in = [sb(f"ctx_in{i}", [P, 2, DM], scope=a) for i in range(2)]
        xn1 = [sb(f"xn1_{i}", [P, 2, DM], scope=a) for i in range(2)]
        cx_t = [sb(f"cx_t{i}", [P, 512], scope=a) for i in range(2)]
        qk0 = [sb(f"qk0_{i}", [P, 512], scope=a) for i in range(2)]
        v0 = [sb(f"v0_{i}", [P, 256], scope=a) for i in range(2)]
        scores0 = [sb(f"scores0_{i}", [P, 384], scope=a) for i in range(2)]
        probs0 = [sb(f"probs0_{i}", [P, 384], scope=a) for i in range(2)]
        probs0_t = [sb(f"probs0_t{i}", [P, 384], scope=a) for i in range(2)]
        xn2 = [sb(f"xn2_{i}", [P, 256], scope=a) for i in range(2)]
        nmax0 = [sb(f"nmax0_{i}", [P, 2], scope=a) for i in range(2)]
        rsum0 = [sb(f"rsum0_{i}", [P, 2], scope=a) for i in range(2)]
        rinv0 = [sb(f"rinv0_{i}", [P, 4], scope=a) for i in range(2)]
        a.close()
        b = ExitStack()
        h = sb("h", [P, CH, TOK], scope=b)
        xq_f = [sb(f"xq_f{i}", [P, BLK], scope=b) for i in range(2)]
        xq = sb("xq", [P, TOK], BF16, b)
        silu = xn3_t = [sb(f"silu{i}", [P, BLK], scope=b) for i in range(2)]
        hq = [sb(f"hq{i}", [P, CH, BLK], BF16, b) for i in range(2)]
        down = xn3 = [sb(f"down{i}", [P, BLK], scope=b) for i in range(2)]
        amax1 = sb("amax1", [P, 8], scope=b)
        gu_scale = sb("gu_scale", [P, 2 * CH], scope=b)
        b.close()
        ab.close()

        c = ExitStack()
        q_st = [sb(f"q_st{i}", [P, GROUPS, SEQ], F32R, c) for i in range(2)]
        k_st = [sb(f"k_st{i}", [P, GROUPS, SEQ], F32R, c) for i in range(2)]
        v_st = [sb(f"v_st{i}", [P, 2, BLK], scope=c) for i in range(2)]
        probs = [sb(f"probs{i}", [P, QUADS, 2, SEQ], scope=c) for i in range(2)]
        nmax = [sb(f"nmax{i}", [P, 2, GROUPS, QUADS], scope=c) for i in range(2)]
        av = sb("av", [P, 512], scope=c)
        dinv = sb("dinv", [P, 512], scope=c)
        on = sb("on", [P, 512], scope=c)
        xn4 = sb("xn4", [P, SEQ], scope=c)
        c.close()
        mid.close()

        d = ctx
        gates_t = sb("gates_t", [EXPERTS, TOK], scope=d)
        gates = sb("gates", [P, TILES, EXPERTS], scope=d)
        top = sb("top", [P, TILES, 8], scope=d)
        top_i = sb("top_i", [P, TILES, 8], U32, d)
        top_f = sb("top_f", [P, TILES, 2], scope=d)
        soft = sb("soft", [P, 4, TILES], scope=d)
        eidx = sb("eidx", [P, EXPERTS], scope=d)
        pick = [sb(f"pick{i}", [P, TILES, EXPERTS], scope=d) for i in range(2)]
        wte = sb("wte", [P, TILES, EXPERTS], scope=d)
        wte_t = sb("wte_t", [EXPERTS, TOK], scope=d)
        w1_in = [sb(f"w1_in{i}", [P, HID], scope=d) for i in range(2)]
        w1_hi = [sb(f"w1_hi{i}", [P, HID], F32R, d) for i in range(2)]
        w1_lo = [sb(f"w1_lo{i}", [P, HID], F32R, d) for i in range(2)]
        b1_cols = [sb(f"b1_cols{i}", [P, HC], scope=d) for i in range(2)]
        w2_in = [sb(f"w2_in{i}", [P, HC, DM], scope=d) for i in range(2)]
        w_tok = [sb(f"w_tok{i}", [P, TOK], scope=d) for i in range(2)]
        hid = [sb(f"hid{i}", [P, HC, BLK], scope=d) for i in range(2)]
        ytmp = [sb(f"ytmp{i}", [P, BLK], scope=d) for i in range(2)]
        acc = sb("acc", [P, TOK], scope=d)
        wte_dram = nc.dram_tensor("wte_scratch", (EXPERTS, TOK), F32, kind="Internal").ap()

        x_tiles = t["x"].rearrange("b (i p) d -> p (b i) d", p=P)
        ctx_tiles = t["ctx_1024"].rearrange("b (i p) d -> p (b i) d", p=P)
        out_tiles = t["out"].rearrange("b (i p) d -> p (b i) d", p=P)
        x3d = x[:, :].rearrange("p (i d) -> p i d", d=DM)

        block = ctx.enter_context(nc.Block())

        @block.sync
        def _(sp):
            def load_ctx(s):
                wait(sp, sem("cx_turned"), s.n - 1)
                sp.dma_start(ctx_in[s.par][:, :, :], ctx_tiles[:, ds(2 * s.n, 2), :])\
                  .then_inc(sem(f"ctx_landed{s.par}"), 16)

            load_ctx(Step(0, 0, BATCH))
            for i in range(4):
                sp.dma_start(x3d[:, 4 * i:4 * i + 4, :], x_tiles[:, 4 * i:4 * i + 4, :])\
                  .then_inc(sem(f"x_landed{i}"), 16)
                if i == 0:
                    for dst, src in ((wq0, "L0_xattn_WQ"), (wk0, "L0_xattn_WK"), (wv0, "L0_xattn_WV"),
                                     (wk1, "L1_xattn_Wk"), (wv1, "L1_xattn_Wv")):
                        sp.dma_start(dst[:, :], t[src]).then_inc(sem("wa_landed"), 16)
                    sp.wait_ge(sem("rows_set"), 1)
                    sp.dma_start(rows[0:32, :], t["L1_ffn_b1"].rearrange("e (c p) -> (e c) p", p=P))\
                      .then_inc(sem("rows_landed"), 16)
                    sp.dma_start(rows[BQC:BQC + 1, :], t["L1_xattn_bq"].rearrange("(o n) -> o n", o=1))\
                      .then_inc(sem("rows_landed"), 16)
                    sp.dma_start(rows[BKC:BKC + 1, :], t["L1_xattn_bk"].rearrange("(o n) -> o n", o=1))\
                      .then_inc(sem("rows_landed"), 16)
                    sp.dma_start(g_in[:, 0:2], t["g_xattn"].partition_broadcast(P)).then_inc(sem("g_landed"), 16)
                    sp.dma_start(g_in[:, 2:4], t["g_ffn"].partition_broadcast(P)).then_inc(sem("g_landed"), 16)
                    sp.dma_start(clip[:, 0:1], t["L0_ffn_clip_x"].partition_broadcast(P)).then_inc(sem("g_landed"), 16)
                    sp.dma_start(clip[:, 1:2], t["L0_ffn_clip_down"].partition_broadcast(P)).then_inc(sem("g_landed"), 16)
                    sp.dma_start(bv1[:, :], t["L1_xattn_bv"].partition_broadcast(P)).then_inc(sem("wa_landed"), 16)
            sp.wait_ge(sem("wq_in_set"), 1)
            for k, name in enumerate(("L0_ffn_w_gate", "L0_ffn_w_up")):
                sp.dma_start(wq_in[:, CH * k:CH * k + 2, :], t[name][0:256, :].rearrange("(c p) n -> p c n", p=P))\
                  .then_inc(sem("wffn_landed"), 16)
                sp.dma_start(wq_in[0:CHW[2], CH * k + 2, :], t[name][256:FF0, :]).then_inc(sem("wffn_landed"), 16)
            sp.dma_start(wd_in[:, :], t["L0_ffn_w_down"]).then_inc(sem("wffn_landed"), 16)
            load_ctx(Step(0, 1, BATCH))
            with sp.Fori(0, (BATCH - 2) // 2) as it:
                load_ctx(Step(it, 2, BATCH))
                load_ctx(Step(it, 3, BATCH))
            for dst, src in ((wq1, "L1_xattn_Wq"), (gate_w, "L1_ffn_gate_w"), (b2, "L1_ffn_b2")):
                sp.dma_start(dst[:, :], t[src]).then_inc(sem("wc_landed"), 16)
            sp.dma_start(gate_b[:, :], t["L1_ffn_gate_b"].rearrange("(n o) -> n o", o=1)).then_inc(sem("wc_landed"), 16)
            sp.wait_ge(sem("we_pad_set"), 1)
            we_rows = t["L1_xattn_We"].rearrange("(u r j e) n -> r j e u n", u=2, r=2, j=QUADS, e=HD)
            for r in range(2):
                for j in range(QUADS):
                    p0 = 32 * j + 16 * r
                    sp.dma_start(we_pad[p0:p0 + HD, :, :], we_rows[r, j]).then_inc(sem("wc_landed"), 16)
            sp.dma_start(we_pad[HD:HD + 1, 0, :], t["L1_xattn_be"].rearrange("(o n) -> o n", o=1))\
              .then_inc(sem("wc_landed"), 16)

            sp.wait_ge(sem("k_split"), 2 * BATCH)
            sp.wait_ge(sem("k_all_set"), 1)
            for s in range(3):
                src = k_hi if s in K_HI else k_lo
                for g in range(GROUPS):
                    for j in range(QUADS):
                        r0 = HD * (4 * g + j)
                        sp.dma_start(k_all[32 * j + 8 * s:32 * j + 8 * s + 8, g, :].bitcast(F32),
                                     src[r0:r0 + 8, :].bitcast(F32)).then_inc(sem("k_slotted"), 16)

            def stage_kv(s):
                wait(sp, sem("attended"), 4 * s.n - 4)
                sp.dma_start(k_st[s.par][:, :, :].bitcast(F32), k_all[:, :, ds(s.n * SEQ, SEQ)].bitcast(F32))\
                  .then_inc(sem(f"kv_staged{s.par}"), 16)
                sp.dma_start(v_st[s.par][:, :, :], v_wide[:, ds(2 * s.n, 2), :])\
                  .then_inc(sem(f"kv_staged{s.par}"), 16)

            sp.wait_ge(sem("k_slotted"), 16 * 3 * HEADS)
            sp.wait_ge(sem("v_widened"), BATCH)
            sp.wait_ge(sem("q_split"), 2 * NBLK)
            stage_kv(Step(0, 0, BATCH))
            stage_kv(Step(0, 1, BATCH))
            with sp.Fori(0, (BATCH - 2) // 2) as it:
                stage_kv(Step(it, 2, BATCH))
                stage_kv(Step(it, 3, BATCH))

            sp.wait_ge(sem("attended"), 4 * BATCH)
            sp.wait_ge(sem("xt_split"), 2 * BATCH)

            def load_expert(s):
                wait(sp, sem("w1_cut"), 2 * s.n - 2)
                sp.dma_start(w1_in[s.par][:, :], t["L1_ffn_w1"][ds(s.n, 1)].rearrange("o p n -> (o p) n"))\
                  .then_inc(sem(f"w1_landed{s.par}"), 16)
                wait(sp, sem("y_done"), NBLK * (s.n - 1))
                sp.dma_start(w2_in[s.par][:, :, :],
                             t["L1_ffn_w2"][ds(s.n, 1)].rearrange("o (c p) n -> p (o c) n", p=P))\
                  .then_inc(sem(f"w2_landed{s.par}"), 16)

            def load_token_weights(s):
                wait(sp, sem("y_weighed"), NBLK * (s.n - 1))
                sp.dma_start(w_tok[s.par][:, :],
                             wte_dram[ds(s.n, 1), :].rearrange("o n -> (o n)").partition_broadcast(P))\
                  .then_inc(sem(f"wtok_landed{s.par}"), 16)

            load_expert(Step(0, 0, EXPERTS))
            load_expert(Step(0, 1, EXPERTS))
            sp.wait_ge(sem("wte_turned"), NBLK)
            sp.dma_start(wte_dram, wte_t[:, :]).then_inc(sem("wte_stored"), 16)
            sp.wait_ge(sem("wte_stored"), 16)
            load_token_weights(Step(0, 0, EXPERTS))
            load_token_weights(Step(0, 1, EXPERTS))
            with sp.Fori(0, (EXPERTS - 2) // 2) as it:
                for u in range(2):
                    load_expert(Step(it, 2 + u, EXPERTS))
                    load_token_weights(Step(it, 2 + u, EXPERTS))
            for k in range(NBLK):
                sp.wait_ge(sem("x_final"), k + 1)
                sp.dma_start(out_tiles[:, BT * k:BT * k + BT, :], x3d[:, BT * k:BT * k + BT, :])\
                  .then_inc(sem("stored"), 16)
            sp.wait_ge(sem("stored"), 16 * NBLK)

        @block.gpsimd
        def _(pool):
            pool.memset(ident[:, :], 0.0).then_inc(sem("p_zero"), 1)
            pool.memset(causal[:, :], 0.0).then_inc(sem("p_zero"), 1)
            pool.memset(half_neg[:, :], -0.5).then_inc(sem("p_zero"), 1)
            pool.memset(eps[:, :], EPS).then_inc(sem("p_zero"), 1)
            pool.wait_ge(sem("p_zero"), 4)
            pool.affine_select(out=ident[:, :], in_=ident[:, :], compare_op=ALU.not_equal, fill=1.0,
                               base=0, pattern=[[-1, P]], channel_multiplier=1).then_inc(sem("ident_set"), 1)
            for c0 in (0, 256):
                pool.affine_select(out=causal[:, c0:c0 + P], in_=causal[:, c0:c0 + P], compare_op=ALU.is_ge,
                                   fill=MASKED, base=0, pattern=[[-1, P]], channel_multiplier=1)\
                    .then_inc(sem("causal_set"), 1)
            pool.memset(wq_in[:, :, :], 1.0).then_inc(sem("wq_in_set"), 1)
            pool.memset(magic[:, :], MAGIC).then_inc(sem("magic_set"), 1)
            pool.memset(ones[:, :], 1.0).then_inc(sem("ones_set"), 1)

            def rstd_of(n, mean_var, eps_sum, out, tiles):
                pool.wait_ge(sem("var_done"), n)
                pool.tensor_tensor(eps_sum[:, 0:tiles], mean_var[:, 0:tiles, 1], eps[:, 0:tiles], ALU.add)\
                    .then_inc(sem("eps_added"), 1)
                pool.wait_ge(sem("eps_added"), n)
                pool.tensor_tensor(out[:, 0:tiles], eps_sum[:, 0:tiles], half_neg[:, 0:tiles], ALU.pow)\
                    .then_inc(sem("rstd_done"), 1)

            def rstd_loop(base, tiles, count):
                with pool.Fori(0, count // 2) as it:
                    for u in range(2):
                        rstd_of(2 * it + (base + u + 1), mv[u], var_eps[u], rstd[u], tiles)

            for k in range(TILES // BT):
                rstd_of(LN1 + k + 1, mv1[:, BT * k:BT * k + BT, :], var_eps[k % 2], rstd1[:, BT * k:BT * k + BT], BT)
            pool.memset(we_pad[:, :, :], 0.0).then_inc(sem("we_pad_set"), 1)
            pool.memset(v_wide[:, :, :], 0.0).then_inc(sem("v_zero"), 1)
            pool.wait_ge(sem("v_zero"), 1)
            pool.memset(v_wide[:, :, :].rearrange("p i (w r c) -> p i w r c", r=2, c=32)[:, :, :, 0, 8:16], 1.0)\
                .then_inc(sem("v_ones"), 1)
            pool.memset(v_wide[:, :, :].rearrange("p i (w r c) -> p i w r c", r=2, c=32)[:, :, :, 1, 24:32], 1.0)\
                .then_inc(sem("v_ones"), 1)
            pool.memset(k_all[:, :, :].bitcast(F32), 1.0).then_inc(sem("k_all_set"), 1)
            pool.wait_ge(sem("w_inv_set"), 1)
            for k in range(2 * CH):
                pool.tensor_scalar(w_tmp[:, k * DM:(k + 1) * DM], wq_in[:, k, :], w_inv[:, k:k + 1], MAGIC,
                                   ALU.mult, ALU.add).then_inc(sem("p_w"), 1)
            pool.tensor_scalar(wd_tmp[:, :], wd_in[:, :], w_inv[:, 6:7], MAGIC, ALU.mult, ALU.add)\
                .then_inc(sem("p_w"), 1)
            pool.wait_ge(sem("p_w"), 7)
            pool.tensor_scalar(w_tmp[:, :], w_tmp[:, :], MAGIC + QMAX, MAGIC - QMAX - 1.0, ALU.min, ALU.max)\
                .then_inc(sem("p_w"), 1)
            pool.tensor_scalar(wd_tmp[:, :], wd_tmp[:, :], MAGIC + QMAX, MAGIC - QMAX - 1.0, ALU.min, ALU.max)\
                .then_inc(sem("p_w"), 1)
            pool.wait_ge(sem("p_w"), 9)
            pool.tensor_scalar(w_q8[:, :, :].rearrange("p c n -> p (c n)"), w_tmp[:, :], -MAGIC, 1.0,
                               ALU.add, ALU.mult).then_inc(sem("w_rounded"), 1)
            pool.tensor_scalar(wd_q8[:, :], wd_tmp[:, :], -MAGIC, 1.0, ALU.add, ALU.mult)\
                .then_inc(sem("w_rounded"), 1)

            rstd_loop(LN2, 2, BATCH)
            pool.wait_ge(sem("amax0_done"), 1)
            pool.partition_all_reduce(amax0[:, 9:10], amax0[:, 8:9], P, bass.bass_isa.ReduceOp.max)\
                .then_inc(sem("gmax0"), 1)
            pool.wait_ge(sem("amax1_done"), 1)
            pool.partition_all_reduce(amax1[:, 5:6], amax1[:, 4:5], P, bass.bass_isa.ReduceOp.max)\
                .then_inc(sem("gmax1"), 1)
            rstd_loop(LN3, BT, NBLK)
            rstd_loop(LN4, 2, BATCH)
            pool.wait_ge(sem("attended"), 4 * BATCH)
            pool.wait_ge(sem("xt_split"), 2 * BATCH)
            pool.iota(eidx[:, :], pattern=[[1, EXPERTS]], base=0, channel_multiplier=0,
                      allow_small_or_imprecise_dtypes=True).then_inc(sem("eidx_set"), 1)
            pool.memset(acc[:, :], 0.0).then_inc(sem("acc_zero"), 1)

        @block.scalar
        def _(act):
            act.wait_ge(sem("g_landed"), 64)
            act.activation(tg[:, :], g_in[:, :], ACT.Tanh).then_inc(sem("tg_set"), 1)
            act.activation(sig[:, :], clip[:, :], ACT.Exp, scale=-1.0).then_inc(sem("sig_exp"), 1)

            def step_a(s):
                m, o = s + 1, s + (-1)
                if m.valid:
                    act.wait_ge(sem("cx_turned"), m.n + 1)
                    wait(act, sem("k1_projected"), m.n - 1)
                    act.activation(cx_t[m.par][:, :], bank[0][:, :], ACT.Copy).then_inc(sem("cx_ready"), 1)
                if s.valid:
                    act.wait_ge(sem("scored"), s.n + 1)
                    wait(act, sem("probs0_turned"), s.n - 1)
                    act.wait_ge(sem("nmax0_done"), s.n + 1)
                    act.activation(probs0[s.par][:, 0:128], scores0[s.par][:, 0:128], ACT.Exp,
                                   bias=nmax0[s.par][:, 0:1], accum_out=rsum0[s.par][:, 0:1])
                    act.activation(probs0[s.par][:, 128:384], scores0[s.par][:, 128:384], ACT.Exp,
                                   bias=nmax0[s.par][:, 1:2], accum_out=rsum0[s.par][:, 1:2])\
                       .then_inc(sem("probs0_done"), 1)
                if m.valid:
                    act.wait_ge(sem("v_projected"), m.n + 1)
                    wait(act, sem("attended0"), m.n - 1)
                    act.activation(v0[m.par][:, :], bank[2][:, 0:256], ACT.Copy).then_inc(sem("v0_ready"), 1)
                    act.wait_ge(sem("k1_projected"), m.n + 1)
                    act.activation(k_hi[:, ds(m.n * SEQ, SEQ)], bank[3][:, 0:256], ACT.Identity,
                                   bias=cols[:, BKC:BKC + 1]).then_inc(sem("k_hi_done"), 1)
                if s.valid:
                    act.wait_ge(sem("probs0_turned"), s.n + 1)
                    wait(act, sem("attended0"), s.n - 1)
                    act.activation(probs0_t[s.par][:, :], bank[5][:, 0:384], ACT.Copy)\
                       .then_inc(sem("probs0_t_ready"), 1)
                if o.valid:
                    act.wait_ge(sem("xn2_turned"), o.n + 1)
                    act.activation(xn2_t[:, ds(o.n * SEQ, SEQ)], bank[7][:, 0:256], ACT.Copy)\
                       .then_inc(sem("xn2_t_ready"), 1)

            act.wait_ge(sem("cols_set"), 1)
            skewed(act, step_a, BATCH)

            act.wait_ge(sem("x_inv"), 1)
            act.wait_ge(sem("magic_set"), 1)
            act.wait_ge(sem("xn2_t_ready"), BATCH)
            act.wait_ge(sem("wd_turned"), 1)

            def scale_x(s):
                wait(act, sem("x_rounded"), s.n - 1)
                act.activation(xq_f[s.par][:, :], xn2_t[:, ds(s.n * BLK, BLK)], ACT.Identity,
                               bias=magic[:, 0:1], scale=smalls[:, 1:2]).then_inc(sem("x_scaled"), 1)

            def both_scale_x(s0, s1):
                scale_x(s0)
                scale_x(s1)

            paired(act, both_scale_x, NBLK)

            def silu_block(s):
                for ch in range(CH):
                    w = CHW[ch]
                    k = CH * s.n + ch
                    act.wait_ge(sem("gated"), k + 1)
                    wait(act, sem("h_done"), k - 1)
                    par = (CH * s.c + ch) % 2
                    act.activation(silu[par][0:w, :], bank[2 * ch][0:w, :], ACT.Silu,
                                   scale=gu_scale[0:w, ch:ch + 1]).then_inc(sem("silued"), 1)

            def both_silu(s0, s1):
                silu_block(s0)
                silu_block(s1)

            act.wait_ge(sem("gu_scaled"), 1)
            paired(act, both_silu, NBLK)
            act.wait_ge(sem("h_inv"), 1)

            def finish_ffn(s0, s1):
                for s in (s0, s1):
                    act.activation(h[:, :, ds(s.n * BLK, BLK)], h[:, :, ds(s.n * BLK, BLK)], ACT.Identity,
                                   bias=magic[:, 0:1], scale=smalls[:, 3:4]).then_inc(sem("h_scaled"), 1)
                for s in (s0, s1):
                    act.wait_ge(sem("xn3_turned"), s.n + 1)
                    wait(act, sem("q_projected"), s.n - 1)
                    act.activation(xn3_t[s.par][:, :], bank[2 + s.par][:, :], ACT.Copy).then_inc(sem("xn3_t_ready"), 1)
                for s in (s0, s1):
                    act.wait_ge(sem("q_projected"), s.n + 1)
                    act.activation(q_hi[:, ds(s.n * BLK, BLK)], bank[4 + s.par][:, :], ACT.Identity,
                                   bias=cols[:, BQC:BQC + 1]).then_inc(sem("q_hi_done"), 1)

            paired(act, finish_ffn, NBLK)

            def step_c(s):
                m, o = s + 1, s + (-1)

                def take_q(u):
                    act.wait_ge(sem("q_slotted"), 2 * m.n + u + 1)
                    if u == 0:
                        wait(act, sem("st_done"), 16 * (m.n - 1))
                    act.activation(q_st[m.par][:, 2 * u:2 * u + 2, :], bank[5 + u][:, :]
                                   .rearrange("p (g s) -> p g s", g=2), ACT.Copy).then_inc(sem("q_staged"), 1)

                def exps(quad):
                    wait(act, sem("attended"), 4 * s.n + quad - 1)
                    for j in range(QUADS):
                        act.wait_ge(sem("st_done"), 16 * s.n + 4 * quad + j + 1)
                        act.activation(probs[quad % 2][:, j, :, :], bank[2 + j % 2][:, :]
                                       .rearrange("p (r s) -> p r s", r=2), ACT.Exp, scale=SC1)\
                           .then_inc(sem("exped"), 1)

                if m.valid:
                    take_q(0)
                if s.valid:
                    exps(0)
                if m.valid:
                    take_q(1)
                if s.valid:
                    for quad in range(1, 4):
                        exps(quad)
                    act.wait_ge(sem("attended"), 4 * s.n + 4)
                    wait(act, sem("on_ready"), s.n)
                    act.activation(av[:, :], bank[4][:, :], ACT.Copy).then_inc(sem("av_ready"), 1)
                if o.valid:
                    act.wait_ge(sem("xn4_turned"), o.n + 1)
                    act.activation(xt_hi[:, ds(o.n * SEQ, SEQ)], bank[5][:, 0:256], ACT.Copy)\
                       .then_inc(sem("xt_hi_done"), 1)

            act.wait_ge(sem("k_slotted"), 16 * 3 * HEADS)
            skewed(act, step_c, BATCH)

            for k in range(NBLK):
                act.wait_ge(sem("gates_done"), k + 1)
                act.activation(gates_t[:, k * BLK:(k + 1) * BLK], bank[k][0:EXPERTS, :], ACT.Identity,
                               bias=gate_b[:, 0:1]).then_inc(sem("gates_t_ready"), 1)
            act.wait_ge(sem("top_gap"), 1)
            act.activation(soft[:, 1, :], soft[:, 0, :], ACT.Exp).then_inc(sem("top_exp"), 1)
            for k in range(NBLK):
                act.wait_ge(sem("wte_turning"), k + 1)
                act.activation(wte_t[:, k * BLK:(k + 1) * BLK], bank[4 + k][0:EXPERTS, :], ACT.Copy)\
                   .then_inc(sem("wte_turned"), 1)

            def gelus(s):
                for k in range(NBLK):
                    wait(act, sem("y_done"), NBLK * s.n + k - 1)
                    for ch in range(HC):
                        act.wait_ge(sem("hid_done"), HC * (NBLK * s.n + k) + ch + 1)
                        act.activation(hid[k % 2][:, ch, :], bank[ch][:, :], ACT.Gelu,
                                       bias=b1_cols[s.par][:, ch:ch + 1]).then_inc(sem("gelued"), 1)

            def both_gelus(s0, s1):
                gelus(s0)
                gelus(s1)

            paired(act, both_gelus, EXPERTS)

        @block.vector
        def _(dve):
            dve.memset(rows[:, :], 0.0).then_inc(sem("rows_set"), 1)
            for i in range(2):
                dve.memset(neg_max_pad[i][:, :, :, :].bitcast(F32), 0.0).then_inc(sem("v_pad"), 1)
            for n in ("qhi", "qlo"):
                dve.memset(sel[n][:, :, :].bitcast(F32), 0.0).then_inc(sem("v_pad"), 1)
            dve.wait_ge(sem("ident_set"), 1)
            dve.wait_ge(sem("v_pad"), 4)
            dve.tensor_copy(ident_b[:, :], ident[:, :]).then_inc(sem("v_const"), 1)
            dve.tensor_copy(ident_r[:, :], ident[:, :]).then_inc(sem("v_const"), 1)
            iv = ident[:, :].rearrange("p (g j e) -> p g j e", g=GROUPS, e=HD)
            for n, slots in (("qhi", Q_HI), ("qlo", Q_LO)):
                for s in slots:
                    dve.tensor_copy(sel[n][:, :, :].rearrange("p g (j s e) -> p g j s e", j=QUADS, s=4)[:, :, :, s, :],
                                    iv).then_inc(sem("v_const"), 1)
            for half in range(2):
                dve.tensor_copy(den_perm[:, :].rearrange("p (w c e) -> p w c e", c=2, e=HD)[:, :, half, :],
                                ident[:, :].rearrange("p (w c e) -> p w c e", c=2, e=HD)[:, :, 1, :])\
                   .then_inc(sem("v_const"), 1)

            for k in range(4):
                dve.wait_ge(sem(f"x_landed{k}"), 16)
                for i in range(BT):
                    ins = dve.bn_stats(stats[k % 2][:, i, :], x3d[:, BT * k + i, :])
                ins.then_inc(sem("halves_done"), 1)
                dve.wait_ge(sem("halves_done"), k + 1)
                for i in range(BT):
                    ins = dve.bn_aggr(mv1[:, BT * k + i, :], stats[k % 2][:, i, :])
                ins.then_inc(sem("var_done"), 1)
            dve.wait_ge(sem("sig_exp"), 1)
            dve.tensor_scalar(sig[:, :], sig[:, :], 1.0, QMAX, ALU.add, ALU.mult).then_inc(sem("v_sig"), 1)
            dve.wait_ge(sem("v_sig"), 1)
            dve.reciprocal(sig[:, :], sig[:, :]).then_inc(sem("v_sig"), 1)
            dve.wait_ge(sem("wffn_landed"), 80)
            dve.tensor_reduce(w_amax[:, 0:6], wq_in[:, :, :], AX.X, ALU.max, apply_absolute_value=True)\
               .then_inc(sem("v_w"), 1)
            dve.tensor_reduce(w_amax[:, 6:7], wd_in[:, :], AX.X, ALU.max, apply_absolute_value=True)\
               .then_inc(sem("v_w"), 1)
            dve.wait_ge(sem("v_w"), 2)
            dve.tensor_scalar(w_scale[:, 0:7], w_amax[:, 0:7], 1.0 / QMAX, None, ALU.mult).then_inc(sem("v_w"), 1)
            dve.wait_ge(sem("v_w"), 3)
            dve.reciprocal(w_inv[:, 0:7], w_scale[:, 0:7]).then_inc(sem("w_inv_set"), 1)
            dve.tensor_scalar(sd_row[:, :], ident[:, :], w_scale[:, 6:7], None, ALU.mult).then_inc(sem("sd_diag"), 1)
            dve.wait_ge(sem("cols_turned"), 1)
            dve.tensor_copy(cols[:, :], bank[6][:, 0:64]).then_inc(sem("cols_set"), 1)

            def norm(out, src, par, i):
                return dve.tensor_scalar(out, src, mv[par][:, i, 0:1], rstd[par][:, i:i + 1], ALU.subtract, ALU.mult)

            def halves_of(par, tiles, column0):
                dve.memset(wait_taker[:, par:par + 1], 0.0)
                for i in range(tiles):
                    ins = dve.bn_stats(stats[par][:, i, :], x[:, ds(column0 + i * P, P)])
                ins.then_inc(sem("halves_done"), 1)

            def variances_of(n, par, tiles):
                dve.wait_ge(sem("halves_done"), n)
                dve.memset(wait_taker[:, 2 + par:3 + par], 0.0)
                for i in range(tiles):
                    ins = dve.bn_aggr(mv[par][:, i, :], stats[par][:, i, :])
                ins.then_inc(sem("var_done"), 1)

            def step_a(s):
                m, o = s + 1, s + (-1)
                if m.valid:
                    dve.wait_ge(sem("rstd_done"), LN1 + 4)
                    wait(dve, sem("cx_turned"), m.n - 1)
                    mv1f = mv1[:, :, :].rearrange("p i c -> p (i c)")
                    for i in range(2):
                        ins = dve.tensor_scalar(xn1[m.par][:, i, :], x[:, ds(m.n * SEQ + i * P, P)],
                                                mv1f[:, ds(4 * m.n + 2 * i, 1)], rstd1[:, ds(2 * m.n + i, 1)],
                                                ALU.subtract, ALU.mult)
                    ins.then_inc(sem("xn1_ready"), 1)
                if s.valid:
                    dve.wait_ge(sem("causal_set"), 2)
                    dve.wait_ge(sem("scored"), s.n + 1)
                    wait(dve, sem("probs0_done"), s.n - 1)
                    dve.scalar_tensor_tensor(scores0[s.par][:, :], bank[4][:, 0:384], SC0, causal[:, :],
                                             ALU.mult, ALU.add).then_inc(sem("masked"), 1)
                if o.valid:
                    dve.wait_ge(sem("rstd_done"), o.n + (LN2 + 1))
                    wait(dve, sem("xn2_turned"), o.n)
                    for i in range(2):
                        ins = norm(xn2[o.par][:, i * P:(i + 1) * P], x[:, ds(o.n * SEQ + i * P, P)], o.par, i)
                    ins.then_inc(sem("xn2_ready"), 1)
                if s.valid:
                    dve.wait_ge(sem("masked"), s.n + 1)
                    dve.tensor_reduce(nmax0[s.par][:, 0:1], scores0[s.par][:, 0:128], AX.X, ALU.max, negate=True)
                    dve.tensor_reduce(nmax0[s.par][:, 1:2], scores0[s.par][:, 128:384], AX.X, ALU.max, negate=True)\
                       .then_inc(sem("nmax0_done"), 1)
                if o.valid:
                    dve.wait_ge(sem("xn2_ready"), o.n + 1)
                    dve.tensor_reduce(amax0[:, ds(o.n, 1)], xn2[o.par][:, :], AX.X, ALU.max,
                                      apply_absolute_value=True).then_inc(sem("amax0_part"), 1)
                if m.valid:
                    dve.wait_ge(sem("qk0_projected"), m.n + 1)
                    wait(dve, sem("scored"), m.n - 1)
                    dve.tensor_copy(qk0[m.par][:, :], bank[1][:, :]).then_inc(sem("qk0_ready"), 1)
                    dve.wait_ge(sem("v0_ready"), m.n + 1)
                    dve.wait_ge(sem("v_ones"), 2)
                    wide = v_wide[:, :, :].rearrange("p i n -> p (i n)")
                    for i in range(2):
                        for u in range(2):
                            dst = wide[:, ds((2 * m.n + i) * BLK + 256 * u, 256)]\
                                .rearrange("p (j c) -> p j c", c=64)
                            for r in range(2):
                                c0 = P * i + 64 * u + 32 * r
                                ins = dve.tensor_tensor(
                                    dst[:, :, 48 * r:48 * r + 8],
                                    bank[2][:, 256 + c0:256 + c0 + 32].rearrange("p (j e) -> p j e", e=HD),
                                    bv1[:, 64 * u + 32 * r:64 * u + 32 * r + 32].rearrange("p (j e) -> p j e", e=HD),
                                    ALU.add)
                    ins.then_inc(sem("v_widened"), 1)
                    dve.wait_ge(sem("k_hi_done"), m.n + 1)
                    dve.scalar_tensor_tensor(k_lo[:, ds(m.n * SEQ, SEQ)], bank[3][:, 0:256], cols[:, BKC:BKC + 1],
                                             k_hi[:, ds(m.n * SEQ, SEQ)].bitcast(F32), ALU.add, ALU.subtract)\
                       .then_inc(sem("k_split"), 2)
                if s.valid:
                    dve.wait_ge(sem("probs0_done"), s.n + 1)
                    dve.reciprocal(rinv0[s.par][:, 0:2], rsum0[s.par][:, :]).then_inc(sem("rinv0_done"), 1)
                    dve.wait_ge(sem("rinv0_done"), s.n + 1)
                    dve.tensor_scalar(rinv0[s.par][:, 2:4], rinv0[s.par][:, 0:2], tg[:, 0:1], None, ALU.mult)\
                       .then_inc(sem("rg0_done"), 1)
                    dve.wait_ge(sem("rg0_done"), s.n + 1)
                    dve.wait_ge(sem("attended0"), s.n + 1)
                    for i in range(2):
                        ins = dve.scalar_tensor_tensor(x[:, ds(s.n * SEQ + i * P, P)], bank[6][:, i * P:(i + 1) * P],
                                                       rinv0[s.par][:, 2 + i:3 + i], x[:, ds(s.n * SEQ + i * P, P)],
                                                       ALU.mult, ALU.add)
                    ins.then_inc(sem("x1_done"), 1)
                    dve.wait_ge(sem("x1_done"), s.n + 1)
                    halves_of(s.par, 2, s.n * SEQ)
                    variances_of(s.n + (LN2 + 1), s.par, 2)

            dve.wait_ge(sem("tg_set"), 1)
            dve.wait_ge(sem("wa_landed"), 96)
            skewed(dve, step_a, BATCH)

            dve.wait_ge(sem("wgu_turned"), 1)
            dve.tensor_copy(wgu_t[:, :, :].rearrange("p c n -> p (c n)"), bank[0][:, :].bitcast(BF16)[:, 0:2 * CH * P])\
               .then_inc(sem("ffn_w_ready"), 1)
            dve.wait_ge(sem("wd_turned"), 1)
            wd_ps = bank[1][:, :].bitcast(BF16)
            dve.tensor_copy(wd_t[:, 0:2, :].rearrange("p c n -> p (c n)"), wd_ps[:, 0:2 * P]).then_inc(sem("ffn_w_ready"), 1)
            dve.tensor_copy(wd_t[0:CHW[2], 2, :], wd_ps[0:CHW[2], 2 * P:3 * P]).then_inc(sem("ffn_w_ready"), 1)
            dve.wait_ge(sem("xn2_t_ready"), BATCH)
            dve.wait_ge(sem("amax0_part"), BATCH)
            dve.tensor_reduce(amax0[:, 8:9], amax0[:, 0:8], AX.X, ALU.max).then_inc(sem("amax0_done"), 1)
            dve.wait_ge(sem("v_sig"), 2)
            dve.wait_ge(sem("gmax0"), 1)
            dve.tensor_scalar(smalls[:, 0:1], amax0[:, 9:10], sig[:, 0:1], None, ALU.mult).then_inc(sem("v_sig"), 1)
            dve.wait_ge(sem("v_sig"), 3)
            dve.reciprocal(smalls[:, 1:2], smalls[:, 0:1]).then_inc(sem("x_inv"), 1)
            dve.tensor_scalar(gu_scale[:, :], w_scale[:, 0:6], smalls[:, 0:1], None, ALU.mult)\
               .then_inc(sem("gu_scaled"), 1)
            dve.memset(h[96:128, 2, :], 0.0).then_inc(sem("h_pad"), 1)

            def round_x(s):
                dve.wait_ge(sem("x_scaled"), s.n + 1)
                dve.tensor_scalar(xq_f[s.par][:, :], xq_f[s.par][:, :], MAGIC + QMAX, MAGIC - QMAX - 1.0,
                                  ALU.min, ALU.max).then_inc(sem("x_clipped"), 1)

            def both_round_x(s0, s1):
                round_x(s0)
                round_x(s1)
                for s in (s0, s1):
                    dve.wait_ge(sem("x_clipped"), s.n + 1)
                    dve.tensor_scalar(xq[:, ds(s.n * BLK, BLK)], xq_f[s.par][:, :], MAGIC, None, ALU.subtract)\
                       .then_inc(sem("x_rounded"), 1)

            paired(dve, both_round_x, NBLK)

            def products(s0, s1):
                for s in (s0, s1):
                    for ch in range(CH):
                        w = CHW[ch]
                        k = CH * s.n + ch
                        par = (CH * s.c + ch) % 2
                        dve.wait_ge(sem("upped"), k + 1)
                        dve.wait_ge(sem("silued"), k + 1)
                        dve.scalar_tensor_tensor(h[0:w, ch, ds(s.n * BLK, BLK)], bank[2 * ch + 1][0:w, :],
                                                 gu_scale[0:w, CH + ch:CH + ch + 1], silu[par][0:w, :],
                                                 ALU.mult, ALU.mult).then_inc(sem("h_done"), 1)
                    if s is s1:
                        dve.wait_ge(sem("h_done"), CH * s0.n + CH)
                        dve.tensor_reduce(amax1[:, ds(s0.n, 1)], h[:, :, ds(s0.n * BLK, BLK)], AX.XY, ALU.max,
                                          apply_absolute_value=True).then_inc(sem("amax1_part"), 1)
                dve.wait_ge(sem("h_done"), CH * s1.n + CH)
                dve.tensor_reduce(amax1[:, ds(s1.n, 1)], h[:, :, ds(s1.n * BLK, BLK)], AX.XY, ALU.max,
                                  apply_absolute_value=True).then_inc(sem("amax1_part"), 1)

            dve.wait_ge(sem("h_pad"), 1)
            dve.wait_ge(sem("gu_scaled"), 1)
            paired(dve, products, NBLK)
            dve.wait_ge(sem("amax1_part"), NBLK)
            dve.tensor_reduce(amax1[:, 4:5], amax1[:, 0:4], AX.X, ALU.max).then_inc(sem("amax1_done"), 1)
            dve.wait_ge(sem("gmax1"), 1)
            dve.tensor_scalar(smalls[:, 2:3], amax1[:, 5:6], sig[:, 1:2], None, ALU.mult).then_inc(sem("v_sig"), 1)
            dve.wait_ge(sem("v_sig"), 4)
            dve.reciprocal(smalls[:, 3:4], smalls[:, 2:3]).then_inc(sem("h_inv"), 1)
            dve.tensor_scalar(smalls[:, 4:5], smalls[:, 2:3], tg[:, 2:3], None, ALU.mult).then_inc(sem("v_sig"), 1)
            dve.wait_ge(sem("v_sig"), 5)
            dve.wait_ge(sem("sd_spread"), 1)
            dve.tensor_scalar(sd_all[:, :], bank[7][:, 0:DM], smalls[:, 4:5], None, ALU.mult).then_inc(sem("sd_set"), 1)
            dve.wait_ge(sem("sd_set"), 1)

            def finish_ffn(s0, s1):
                for s in (s0, s1):
                    dve.wait_ge(sem("h_scaled"), s.n + 1)
                    hb = h[:, :, ds(s.n * BLK, BLK)]
                    dve.tensor_scalar(hb, hb, MAGIC + QMAX, MAGIC - QMAX - 1.0, ALU.min, ALU.max)\
                       .then_inc(sem("h_clipped"), 1)
                for s in (s0, s1):
                    dve.wait_ge(sem("h_clipped"), s.n + 1)
                    wait(dve, sem("downed"), s.n - 1)
                    dve.tensor_scalar(hq[s.par][:, :, :], h[:, :, ds(s.n * BLK, BLK)], MAGIC, None, ALU.subtract)\
                       .then_inc(sem("h_rounded"), 1)
                for s in (s0, s1):
                    dve.wait_ge(sem("downed"), s.n + 1)
                    wait(dve, sem("xn3_turned"), s.n - 1)
                    dve.tensor_tensor(down[s.par][:, :].rearrange("p (i d) -> p i d", d=DM),
                                      bank[s.par][:, :].rearrange("p (i d) -> p i d", d=DM),
                                      sd_all[:, :].unsqueeze(1).broadcast_to([P, BT, DM]), ALU.mult)\
                       .then_inc(sem("down_scaled"), 1)
                for s in (s0, s1):
                    dve.wait_ge(sem("down_scaled"), s.n + 1)
                    xb = x[:, ds(s.n * BLK, BLK)]
                    dve.tensor_tensor(xb, down[s.par][:, :], xb, ALU.add).then_inc(sem("x2_done"), 1)
                for s in (s0, s1):
                    dve.wait_ge(sem("x2_done"), s.n + 1)
                    halves_of(s.par, BT, s.n * BLK)
                for s in (s0, s1):
                    variances_of(s.n + (LN3 + 1), s.par, BT)
                for s in (s0, s1):
                    dve.wait_ge(sem("rstd_done"), s.n + (LN3 + 1))
                    for i in range(BT):
                        ins = norm(xn3[s.par][:, i * P:(i + 1) * P], x[:, ds(s.n * BLK + i * P, P)], s.par, i)
                    ins.then_inc(sem("xn3_ready"), 1)
                for s in (s0, s1):
                    dve.wait_ge(sem("q_hi_done"), s.n + 1)
                    dve.scalar_tensor_tensor(q_lo[:, ds(s.n * BLK, BLK)], bank[4 + s.par][:, :], cols[:, BQC:BQC + 1],
                                             q_hi[:, ds(s.n * BLK, BLK)].bitcast(F32), ALU.add, ALU.subtract)\
                       .then_inc(sem("q_split"), 2)

            paired(dve, finish_ffn, NBLK)

            def step_c(s):
                m, o = s + 1, s + (-1)

                def maxima(first, last):
                    for u in range(first, last):
                        gp, qt, j = u // 8, u // 4 % 2, u % 4
                        dve.wait_ge(sem("s_done"), 16 * m.n + u + 1)
                        if u == 0:
                            wait(dve, sem("max_split"), m.n - 1)
                        dve.tensor_reduce(nmax[m.par][:, qt, 2 * gp:2 * gp + 2, j],
                                          bank[u % 2][:, :].rearrange("p (r s) -> p r s", r=2), AX.X, ALU.max,
                                          negate=True).then_inc(sem("s_maxed"), 1)

                if s.valid:
                    pad = neg_max_pad[s.par][:, :, :, :].rearrange("p t g (j c) -> p (t g j) c", c=32)
                    nm = nmax[s.par][:, :, :, :].rearrange("p t g j -> p (t g j)").unsqueeze(2)
                    dve.wait_ge(sem("s_maxed"), 16 * s.n + 16)
                    wait(dve, sem("max_turned"), 2 * s.n - 2)
                    dve.tensor_copy(pad[:, :, MROW:MROW + 1], nm).then_inc(sem("max_hi"), 1)
                    dve.wait_ge(sem("max_hi"), s.n + 1)
                    dve.tensor_tensor(pad[:, :, MROW + 1:MROW + 2], nm, pad[:, :, MROW:MROW + 1].bitcast(F32),
                                      ALU.subtract).then_inc(sem("max_split"), 1)
                    for u in range(2):
                        dve.wait_ge(sem("max_turned"), 2 * s.n + u + 1)
                        qs = q_st[s.par][:, 2 * u:2 * u + 2, :]
                        dve.tensor_tensor(qs, bank[5 + u][:, :].rearrange("p (g s) -> p g s", g=2),
                                          qs.bitcast(F32), ALU.add).then_inc(sem("q_shifted"), 1)
                if o.valid:
                    dve.wait_ge(sem("den_spread"), o.n + 1)
                    dve.reciprocal(dinv[:, :], bank[7][:, :]).then_inc(sem("den_inv"), 1)
                    dve.wait_ge(sem("den_inv"), o.n + 1)
                    wait(dve, sem("wo_done"), o.n)
                    dve.tensor_tensor(on[:, :], av[:, :], dinv[:, :], ALU.mult).then_inc(sem("on_ready"), 1)
                if m.valid:
                    maxima(0, 4)
                if o.valid:
                    dve.wait_ge(sem("wo_done"), o.n + 1)
                    xb = x[:, ds(o.n * SEQ, SEQ)]
                    dve.scalar_tensor_tensor(xb, bank[7][:, 0:256], tg[:, 1:2], xb, ALU.mult, ALU.add)\
                       .then_inc(sem("x3_done"), 1)
                if m.valid:
                    maxima(4, 8)
                if o.valid:
                    dve.wait_ge(sem("x3_done"), o.n + 1)
                    halves_of(o.par, 2, o.n * SEQ)
                if m.valid:
                    maxima(8, 10)
                if o.valid:
                    variances_of(o.n + (LN4 + 1), o.par, 2)
                if m.valid:
                    maxima(10, 14)
                if o.valid:
                    dve.wait_ge(sem("rstd_done"), o.n + (LN4 + 1))
                    wait(dve, sem("xn4_turned"), o.n)
                    for i in range(2):
                        ins = norm(xn4[:, i * P:(i + 1) * P], x[:, ds(o.n * SEQ + i * P, P)], o.par, i)
                    ins.then_inc(sem("xn4_ready"), 1)
                if m.valid:
                    maxima(14, 16)
                if o.valid:
                    dve.wait_ge(sem("xt_hi_done"), o.n + 1)
                    dve.tensor_tensor(xt_lo[:, ds(o.n * SEQ, SEQ)], bank[5][:, 0:256],
                                      xt_hi[:, ds(o.n * SEQ, SEQ)].bitcast(F32), ALU.subtract)\
                       .then_inc(sem("xt_split"), 2)

            skewed(dve, step_c, BATCH)

            dve.wait_ge(sem("wc_landed"), 16 * (4 + 2 * QUADS + 1))
            dve.tensor_copy(gate_hi[:, :], gate_w[:, :]).then_inc(sem("gw_hi"), 1)
            dve.wait_ge(sem("gw_hi"), 1)
            dve.tensor_tensor(gate_lo[:, :], gate_w[:, :], gate_hi[:, :].bitcast(F32), ALU.subtract)\
               .then_inc(sem("gw_split"), 1)

            def cut_w1(s):
                dve.wait_ge(sem(f"w1_landed{s.par}"), 16 * (s.half + 1))
                wait(dve, sem("hid_done"), HC * NBLK * (s.n - 1))
                wait(dve, sem("gelued"), HC * NBLK * (s.n - 1))
                dve.tensor_copy(b1_cols[s.par][:, :], cols[:, ds(HC * s.n, HC)])
                dve.tensor_copy(w1_hi[s.par][:, :], w1_in[s.par][:, :]).then_inc(sem("w1_cut"), 1)
                dve.wait_ge(sem("w1_cut"), 2 * s.n + 1)
                dve.tensor_tensor(w1_lo[s.par][:, :], w1_in[s.par][:, :], w1_hi[s.par][:, :].bitcast(F32),
                                  ALU.subtract).then_inc(sem("w1_cut"), 1)

            cut_w1(Step(0, 0, EXPERTS))
            dve.wait_ge(sem("gates_turned"), 1)
            dve.tensor_copy(gates[:, :, :], bank[4][:, 0:P].rearrange("p (i e) -> p i e", e=EXPERTS))\
               .then_inc(sem("v_top"), 1)
            dve.wait_ge(sem("v_top"), 1)
            for i in range(TILES):
                ins = dve.max(top[:, i, :], gates[:, i, :])
            ins.then_inc(sem("v_top"), 1)
            dve.wait_ge(sem("v_top"), 2)
            dve.tensor_tensor(soft[:, 0, :], top[:, :, 1], top[:, :, 0], ALU.subtract).then_inc(sem("top_gap"), 1)
            for i in range(TILES):
                ins = dve.max_index(top_i[:, i, :], top[:, i, :], gates[:, i, :])
            ins.then_inc(sem("v_top"), 1)
            dve.wait_ge(sem("top_exp"), 1)
            dve.tensor_scalar(soft[:, 2, :], soft[:, 1, :], 1.0, None, ALU.add).then_inc(sem("v_top"), 1)
            dve.wait_ge(sem("v_top"), 3)
            dve.tensor_copy(top_f[:, :, :], top_i[:, :, 0:2]).then_inc(sem("v_top"), 1)
            dve.wait_ge(sem("v_top"), 4)
            dve.reciprocal(soft[:, 2, :], soft[:, 2, :]).then_inc(sem("v_top"), 1)
            dve.wait_ge(sem("v_top"), 6)
            dve.tensor_tensor(soft[:, 3, :], soft[:, 2, :], soft[:, 1, :], ALU.mult).then_inc(sem("v_top"), 1)
            dve.wait_ge(sem("eidx_set"), 1)
            dve.wait_ge(sem("v_top"), 5)
            full = [P, TILES, EXPERTS]
            for k in range(2):
                dve.tensor_tensor(pick[k][:, :, :], eidx[:, :].unsqueeze(1).broadcast_to(full),
                                  top_f[:, :, k].unsqueeze(2).broadcast_to(full), ALU.is_equal)\
                   .then_inc(sem("v_top"), 1)
            dve.wait_ge(sem("v_top"), 7)
            dve.wait_ge(sem("v_top"), 9)
            for k in range(2):
                dve.tensor_tensor(pick[k][:, :, :], pick[k][:, :, :],
                                  soft[:, 2 + k, :].unsqueeze(2).broadcast_to(full), ALU.mult)\
                   .then_inc(sem("v_top"), 1)
            dve.wait_ge(sem("v_top"), 11)
            dve.tensor_tensor(wte[:, :, :], pick[0][:, :, :], pick[1][:, :, :], ALU.add).then_inc(sem("wte_ready"), 1)
            cut_w1(Step(0, 1, EXPERTS))

            def weigh(s):
                dve.wait_ge(sem(f"wtok_landed{s.par}"), 16 * (s.half + 1))
                for k in range(NBLK):
                    y = NBLK * s.n + k
                    dve.wait_ge(sem("y_done"), y + 1)
                    wait(dve, sem("acc_added"), y - 1)
                    dve.tensor_tensor(ytmp[k % 2][:, :], bank[4 + k % 2][:, :],
                                      w_tok[s.par][:, k * BLK:(k + 1) * BLK], ALU.mult).then_inc(sem("y_weighed"), 1)
                    dve.wait_ge(sem("y_weighed"), y + 1)
                    ab_ = acc[:, k * BLK:(k + 1) * BLK]
                    dve.tensor_tensor(ab_, ab_, ytmp[k % 2][:, :], ALU.add).then_inc(sem("acc_added"), 1)

            dve.wait_ge(sem("acc_zero"), 1)
            for n in range(2):
                weigh(Step(0, n, EXPERTS))
                cut_w1(Step(0, n + 2, EXPERTS))
            with dve.Fori(0, (EXPERTS - 4) // 2) as it:
                for u in range(2):
                    weigh(Step(it, 2 + u, EXPERTS))
                    cut_w1(Step(it, 4 + u, EXPERTS))
            weigh(Step(0, EXPERTS - 2, EXPERTS))
            weigh(Step(0, EXPERTS - 1, EXPERTS))
            for k in range(NBLK):
                dve.wait_ge(sem("out_done"), k + 1)
                xb = x[:, k * BLK:(k + 1) * BLK]
                dve.scalar_tensor_tensor(xb, bank[k][:, :], tg[:, 3:4], xb, ALU.mult, ALU.add)\
                   .then_inc(sem("x_final"), 1)

        @block.tensor
        def _(pe):
            def mm(out, lhsT, rhs, start=True, stop=True, **kw):
                return pe.matmul(out, lhsT, rhs, start=start, stop=stop, **kw)

            pe.wait_ge(sem("ident_set"), 1)
            pe.wait_ge(sem("rows_landed"), 48)
            pe.wait_ge(sem("rows_set"), 1)
            pe.transpose(bank[6][:, 0:64], rows[:, :], ident[0:64, 0:64]).then_inc(sem("cols_turned"), 1)
            pe.wait_ge(sem("cols_set"), 1)
            pe.wait_ge(sem("wa_landed"), 96)

            def step_a(s):
                m, o = s + 1, s + (-1)
                if s.valid:
                    wait(pe, sem("masked"), s.n)
                    pe.wait_ge(sem("qk0_ready"), s.n + 1)
                    mm(bank[4][:, 0:128], qk0[s.par][:, 0:128], qk0[s.par][:, 256:384])
                    mm(bank[4][:, 128:384], qk0[s.par][:, 128:256], qk0[s.par][:, 256:512])\
                        .then_inc(sem("scored"), 1)
                if m.valid:
                    pe.wait_ge(sem(f"ctx_landed{m.par}"), 16 * (m.half + 1))
                    pe.wait_ge(sem("xn1_ready"), m.n + 1)
                    wait(pe, sem("cx_ready"), m.n)
                    for i in range(2):
                        pe.transpose(bank[0][:, P * i:P * i + P], ctx_in[m.par][:, i, :], ident[:, :])
                    for i in range(2):
                        ins = pe.transpose(bank[0][:, 256 + P * i:256 + P * i + P], xn1[m.par][:, i, :], ident[:, :])
                    ins.then_inc(sem("cx_turned"), 1)
                if o.valid:
                    pe.wait_ge(sem("xn2_ready"), o.n + 1)
                    wait(pe, sem("xn2_t_ready"), o.n)
                    for i in range(2):
                        ins = pe.transpose(bank[7][:, P * i:P * i + P], xn2[o.par][:, P * i:P * i + P], ident[:, :])
                    ins.then_inc(sem("xn2_turned"), 1)
                if m.valid:
                    ct, xt = cx_t[m.par][:, 0:256], cx_t[m.par][:, 256:512]
                    pe.wait_ge(sem("cx_ready"), m.n + 1)
                    wait(pe, sem("qk0_ready"), m.n)
                    mm(bank[1][:, 0:256], wq0[:, :], ct)
                    mm(bank[1][:, 256:512], wk0[:, :], xt).then_inc(sem("qk0_projected"), 1)
                    wait(pe, sem("v0_ready"), m.n)
                    wait(pe, sem("v_widened"), m.n)
                    for i in range(2):
                        mm(bank[2][:, P * i:P * i + P], ct[:, P * i:P * i + P], wv0[:, :])
                    for i in range(2):
                        ins = mm(bank[2][:, 256 + P * i:256 + P * i + P], ct[:, P * i:P * i + P], wv1[:, :])
                    ins.then_inc(sem("v_projected"), 1)
                    wait(pe, sem("k_split"), 2 * m.n)
                    mm(bank[3][:, 0:256], wk1[:, :], ct).then_inc(sem("k1_projected"), 1)
                if s.valid:
                    pe.wait_ge(sem("probs0_done"), s.n + 1)
                    wait(pe, sem("probs0_t_ready"), s.n)
                    for i in range(3):
                        ins = pe.transpose(bank[5][:, P * i:P * i + P], probs0[s.par][:, P * i:P * i + P], ident[:, :])
                    ins.then_inc(sem("probs0_turned"), 1)
                    pe.wait_ge(sem("probs0_t_ready"), s.n + 1)
                    pe.wait_ge(sem("v0_ready"), s.n + 1)
                    wait(pe, sem("x1_done"), s.n)
                    pt, vv = probs0_t[s.par], v0[s.par]
                    mm(bank[6][:, 0:128], pt[:, 0:128], vv[:, 0:128])
                    mm(bank[6][:, 128:256], pt[:, 128:256], vv[:, 0:128], stop=False)
                    mm(bank[6][:, 128:256], pt[:, 256:384], vv[:, 128:256], start=False).then_inc(sem("attended0"), 1)

            skewed(pe, step_a, BATCH)

            pe.wait_ge(sem("w_rounded"), 2)
            pe.wait_ge(sem("v_const"), 7)
            pe.wait_ge(sem("cx_ready"), BATCH)
            pe.wait_ge(sem("qk0_ready"), BATCH)
            wg_ps = bank[0][:, :].bitcast(BF16)
            wd_ps = bank[1][:, :].bitcast(BF16)
            for k in range(2 * CH):
                ins = pe.transpose(wg_ps[:, k * P:(k + 1) * P], w_q8[:, k, :], ident_b[:, :])
            ins.then_inc(sem("wgu_turned"), 1)
            for k in range(CH):
                ins = pe.transpose(wd_ps[0:CHW[k], k * P:k * P + P], wd_q8[:, k * P:k * P + CHW[k]], ident_b[:, :])
            ins.then_inc(sem("wd_turned"), 1)
            pe.wait_ge(sem("sd_diag"), 1)
            pe.wait_ge(sem("ones_set"), 1)
            pe.wait_ge(sem("xn2_t_ready"), BATCH)
            mm(bank[7][:, 0:DM], ones[:, :], sd_row[:, :]).then_inc(sem("sd_spread"), 1)

            pe.wait_ge(sem("ffn_w_ready"), 3)
            pe.wait_ge(sem("v0_ready"), BATCH)
            pe.wait_ge(sem("k_split"), 2 * BATCH)
            pe.wait_ge(sem("masked"), BATCH)
            pe.wait_ge(sem("probs0_t_ready"), BATCH)

            def gate_up(s0, s1):
                for s in (s0, s1):
                    pe.wait_ge(sem("x_rounded"), s.n + 1)
                    for ch in range(CH):
                        w = CHW[ch]
                        wait(pe, sem("silued"), CH * s.n + ch - (CH - 1))
                        mm(bank[2 * ch][0:w, :], wgu_t[:, ch, 0:w], xq[:, ds(s.n * BLK, BLK)])\
                            .then_inc(sem("gated"), 1)
                        wait(pe, sem("h_done"), CH * s.n + ch - (CH - 1))
                        mm(bank[2 * ch + 1][0:w, :], wgu_t[:, CH + ch, 0:w], xq[:, ds(s.n * BLK, BLK)])\
                            .then_inc(sem("upped"), 1)

            paired(pe, gate_up, NBLK)
            pe.wait_ge(sem("h_done"), CH * NBLK)
            pe.wait_ge(sem("wc_landed"), 16 * (4 + 2 * QUADS + 1))

            def finish_ffn(s0, s1):
                for s in (s0, s1):
                    pe.wait_ge(sem("h_rounded"), s.n + 1)
                    wait(pe, sem("down_scaled"), s.n - 1)
                    for i in range(BT):
                        for ch in range(CH):
                            w = CHW[ch]
                            ins = mm(bank[s.par][:, i * P:(i + 1) * P], hq[s.par][0:w, ch, i * P:(i + 1) * P],
                                     wd_t[0:w, ch, :], start=(ch == 0), stop=(ch == CH - 1))
                    ins.then_inc(sem("downed"), 1)
                for s in (s0, s1):
                    pe.wait_ge(sem("xn3_ready"), s.n + 1)
                    wait(pe, sem("xn3_t_ready"), s.n - 1)
                    for i in range(BT):
                        ins = pe.transpose(bank[2 + s.par][:, P * i:P * i + P], xn3[s.par][:, P * i:P * i + P],
                                           ident[:, :])
                    ins.then_inc(sem("xn3_turned"), 1)
                for s in (s0, s1):
                    pe.wait_ge(sem("xn3_t_ready"), s.n + 1)
                    wait(pe, sem("q_split"), 2 * (s.n - 1))
                    mm(bank[4 + s.par][:, :], wq1[:, :], xn3_t[s.par][:, :]).then_inc(sem("q_projected"), 1)

            paired(pe, finish_ffn, NBLK)

            pe.wait_ge(sem("q_split"), 2 * NBLK)

            def step_c(s):
                m, o = s + 1, s + (-1)

                def slot_q(u):
                    if u == 0:
                        wait(pe, sem("q_shifted"), 2 * s.n + 1)
                        wait(pe, sem("xt_split"), 2 * (m.n - 2))
                    else:
                        wait(pe, sem("q_shifted"), 2 * s.n + 2)
                    for gg in range(2):
                        g = 2 * u + gg
                        mm(bank[5 + u][:, gg * SEQ:(gg + 1) * SEQ], sel["qhi"][:, g, :],
                           q_hi[:, ds(m.n * SEQ, SEQ)], stop=False)
                        ins = mm(bank[5 + u][:, gg * SEQ:(gg + 1) * SEQ], sel["qlo"][:, g, :],
                                 q_lo[:, ds(m.n * SEQ, SEQ)], start=False)
                    ins.then_inc(sem("q_slotted"), 1)

                def by_query(u):
                    gp, qt, j = u // 8, u // 4 % 2, u % 4
                    if u % 8 == 0:
                        pe.wait_ge(sem("q_staged"), 2 * m.n + gp + 1)
                    if u == 0:
                        pe.wait_ge(sem(f"kv_staged{m.par}"), 32 * (m.half + 1))
                    wait(pe, sem("s_maxed"), 16 * m.n + u - 1)
                    r0 = 32 * j
                    for r in range(2):
                        g = 2 * gp + r
                        ins = mm(bank[u % 2][:, r * SEQ:(r + 1) * SEQ],
                                 q_st[m.par][r0:r0 + 32, g, qt * P:(qt + 1) * P],
                                 k_st[m.par][r0:r0 + 32, g, :], tile_position=(r0, 0))
                    ins.then_inc(sem("s_done"), 1)

                def by_key(quad, j):
                    gp, kt = quad // 2, quad % 2
                    if kt == 0 and j == 0:
                        pe.wait_ge(sem("q_shifted"), 2 * s.n + gp + 1)
                    wait(pe, sem("exped"), 16 * s.n + 4 * quad + j - 1)
                    r0 = 32 * j
                    for r in range(2):
                        g = 2 * gp + r
                        ins = mm(bank[2 + j % 2][:, r * SEQ:(r + 1) * SEQ],
                                 k_st[s.par][r0:r0 + 32, g, kt * P:(kt + 1) * P],
                                 q_st[s.par][r0:r0 + 32, g, :], tile_position=(r0, 0))
                    ins.then_inc(sem("st_done"), 1)

                def attend(quad):
                    gp, kt = quad // 2, quad % 2
                    pe.wait_ge(sem("exped"), 16 * s.n + 4 * quad + 4)
                    if quad == 0:
                        wait(pe, sem("av_ready"), s.n)
                    for r in range(2):
                        for j in range(QUADS):
                            c0 = 32 * (2 * (4 * gp + j) + r)
                            ins = mm(bank[4][32 * j:32 * j + 32, gp * SEQ:(gp + 1) * SEQ],
                                     v_st[s.par][:, kt, c0:c0 + 32], probs[quad % 2][:, j, r, :],
                                     start=(kt == 0 and r == 0), stop=(kt == 1 and r == 1),
                                     tile_position=(0, 32 * j))
                    ins.then_inc(sem("attended"), 1)

                if s.valid:
                    pe.wait_ge(sem("max_split"), s.n + 1)
                    for u in range(2):
                        pe.wait_ge(sem("q_staged"), 2 * s.n + u + 1)
                        if u == 0:
                            wait(pe, sem("xt_split"), 2 * (s.n - 1))
                        for gg in range(2):
                            for qt in range(2):
                                ins = mm(bank[5 + u][:, gg * SEQ + qt * P:gg * SEQ + (qt + 1) * P],
                                         neg_max_pad[s.par][:, qt, 2 * u + gg, :], ident_r[:, :])
                        ins.then_inc(sem("max_turned"), 1)
                if o.valid:
                    pe.wait_ge(sem("av_ready"), o.n + 1)
                    wait(pe, sem("x3_done"), o.n)
                    mm(bank[7][:, :], den_perm[:, :], av[:, :]).then_inc(sem("den_spread"), 1)
                if m.valid:
                    slot_q(0)
                if s.valid:
                    by_key(0, 0)
                    by_key(0, 1)
                if o.valid:
                    pe.wait_ge(sem("on_ready"), o.n + 1)
                    for qt in range(2):
                        for u in range(2):
                            ins = mm(bank[7][:, qt * P:(qt + 1) * P], on[:, u * SEQ + qt * P:u * SEQ + (qt + 1) * P],
                                     we_pad[:, u, :], start=(u == 0), stop=(u == 1))
                    ins.then_inc(sem("wo_done"), 1)
                if m.valid:
                    slot_q(1)
                for quad in range(4):
                    if quad and s.valid:
                        by_key(quad, 0)
                        by_key(quad, 1)
                    if m.valid:
                        by_query(4 * quad)
                        by_query(4 * quad + 1)
                    if s.valid:
                        by_key(quad, 2)
                    if m.valid:
                        by_query(4 * quad + 2)
                    if s.valid:
                        by_key(quad, 3)
                    if m.valid:
                        by_query(4 * quad + 3)
                    if quad and s.valid:
                        attend(quad - 1)
                if o.valid:
                    pe.wait_ge(sem("xn4_ready"), o.n + 1)
                    if m.valid:
                        pe.wait_ge(sem("q_staged"), 2 * m.n + 1)
                    for i in range(2):
                        ins = pe.transpose(bank[5][:, P * i:P * i + P], xn4[:, P * i:P * i + P], ident[:, :])
                    ins.then_inc(sem("xn4_turned"), 1)
                if s.valid:
                    attend(3)

            skewed(pe, step_c, BATCH)

            pe.wait_ge(sem("gw_split"), 1)
            pe.wait_ge(sem("xt_split"), 2 * BATCH)
            for k in range(NBLK):
                cs = slice(k * BLK, (k + 1) * BLK)
                if k == 0:
                    pe.wait_ge(sem("s_maxed"), 16 * BATCH)
                if k == 2:
                    pe.wait_ge(sem("exped"), 16 * BATCH)
                mm(bank[k][0:EXPERTS, :], gate_hi[:, :], xt_hi[:, cs], stop=False)
                mm(bank[k][0:EXPERTS, :], gate_hi[:, :], xt_lo[:, cs], start=False, stop=False)
                mm(bank[k][0:EXPERTS, :], gate_lo[:, :], xt_hi[:, cs], start=False).then_inc(sem("gates_done"), 1)
            pe.wait_ge(sem("av_ready"), BATCH)
            pe.wait_ge(sem("gates_t_ready"), NBLK)
            for i in range(TILES):
                ins = pe.transpose(bank[4][:, EXPERTS * i:EXPERTS * (i + 1)], gates_t[:, i * P:(i + 1) * P],
                                   ident[0:EXPERTS, 0:EXPERTS])
            ins.then_inc(sem("gates_turned"), 1)
            pe.wait_ge(sem("wte_ready"), 1)
            for i in range(TILES):
                k = i // BT
                ins = pe.transpose(bank[4 + k][0:EXPERTS, (i % BT) * P:(i % BT + 1) * P], wte[:, i, :], ident[:, :])
                if i % BT == BT - 1:
                    ins.then_inc(sem("wte_turning"), 1)
            pe.wait_ge(sem("wte_turned"), NBLK)

            def expert(s):
                pe.wait_ge(sem("w1_cut"), 2 * s.n + 2)
                for k in range(NBLK):
                    cs = slice(k * BLK, (k + 1) * BLK)
                    y = NBLK * s.n + k
                    for ch in range(HC):
                        wait(pe, sem("gelued"), HC * y + ch - (HC - 1))
                        wc = slice(ch * P, (ch + 1) * P)
                        mm(bank[ch][:, :], w1_hi[s.par][:, wc], xt_hi[:, cs], stop=False)
                        mm(bank[ch][:, :], w1_hi[s.par][:, wc], xt_lo[:, cs], start=False, stop=False)
                        mm(bank[ch][:, :], w1_lo[s.par][:, wc], xt_hi[:, cs], start=False).then_inc(sem("hid_done"), 1)
                    if k == 0:
                        pe.wait_ge(sem(f"w2_landed{s.par}"), 16 * (s.half + 1))
                    wait(pe, sem("y_weighed"), y - 1)
                    for ch in range(HC):
                        pe.wait_ge(sem("gelued"), HC * y + ch + 1)
                        ins = mm(bank[4 + k % 2][:, :], w2_in[s.par][:, ch, :], hid[k % 2][:, ch, :],
                                 start=(ch == 0), stop=(ch == HC - 1))
                    ins.then_inc(sem("y_done"), 1)

            def both_experts(s0, s1):
                expert(s0)
                expert(s1)

            paired(pe, both_experts, EXPERTS)

            pe.wait_ge(sem("gelued"), HC * NBLK * EXPERTS)
            for k in range(NBLK):
                pe.wait_ge(sem("acc_added"), NBLK * (EXPERTS - 1) + k + 1)
                for i in range(BT):
                    tok = slice(k * BLK + i * P, k * BLK + (i + 1) * P)
                    mm(bank[k][:, i * P:(i + 1) * P], acc[:, tok], ident[:, :], stop=False)
                    ins = mm(bank[k][:, i * P:(i + 1) * P], wte_t[:, tok], b2[:, :], start=False)
                ins.then_inc(sem("out_done"), 1)


_INS = ["x", "ctx_1024", "g_xattn", "g_ffn", "L0_xattn_WK", "L0_xattn_WQ", "L0_xattn_WV", "L0_ffn_clip_x",
        "L0_ffn_clip_down", "L0_ffn_w_gate", "L0_ffn_w_up", "L0_ffn_w_down", "L1_xattn_Wq", "L1_xattn_bq",
        "L1_xattn_Wk", "L1_xattn_bk", "L1_xattn_Wv", "L1_xattn_bv", "L1_xattn_We", "L1_xattn_be",
        "L1_ffn_gate_w", "L1_ffn_gate_b", "L1_ffn_w1", "L1_ffn_b1", "L1_ffn_w2", "L1_ffn_b2"]


def kernel(**inputs):
    import concourse.bacc as bacc
    from concourse.bass_utils import run_bass_kernel_spmd

    nc = bacc.Bacc("TRN2", target_bir_lowering=False, num_devices=1)
    arrays, t = {}, {}
    for name in _INS:
        a = np.ascontiguousarray(inputs[name])
        arrays[f"in_{name}"] = a
        t[name] = nc.dram_tensor(f"in_{name}", a.shape, mybir.dt.from_np(a.dtype), kind="ExternalInput").ap()
    t["out"] = nc.dram_tensor("out_x", (BATCH, SEQ, DM), F32, kind="ExternalOutput").ap()
    flamingo(nc, t)
    r = run_bass_kernel_spmd(nc, [arrays], core_ids=[0])
    return r.results[0]["out_x"]
```

```python
from contextlib import ExitStack

import numpy as np

import concourse.bass as bass
from concourse import mybir

F32, F32R, BF16 = mybir.dt.float32, mybir.dt.float32r, mybir.dt.bfloat16
U32 = mybir.dt.uint32
ACT = mybir.ActivationFunctionType
ALU = mybir.AluOpType
AX = mybir.AxisListType
ds = bass.ds

P = 128
BATCH, SEQ, DM = 8, 256, 128
TOK = BATCH * SEQ
TILES = TOK // P
HEADS, HD = 16, 8
FF0 = 352
CH = 3
CHW = [128, 128, FF0 - 256]
EXPERTS, HID = 8, 512
HC = HID // P
BLK = 512
NBLK = TOK // BLK
BT = BLK // P
LN1, LN2, LN3, LN4 = 0, 4, 4 + BATCH, 4 + BATCH + NBLK

EPS = 1e-5
QMAX = 127.0
MAGIC = 1.5 * 2.0 ** 23
MASKED = -1e30
SC0 = float(1.0 / np.sqrt(np.float32(DM)))
SC1 = float(1.0 / np.sqrt(HD))

QUADS, GROUPS = 4, 4
Q_HI, Q_LO = (0, 1), (2,)
K_HI, K_LO = (0, 2), (1,)
C_SLOTS = 18
MROW = 24


class Step:

    def __init__(self, it, c, count):
        self.it, self.c, self.count = it, c, count
        self.par = c % 2

    @property
    def n(self):
        return 2 * self.it + self.c

    @property
    def half(self):
        return self.it + self.c // 2

    def __add__(self, k):
        return Step(self.it, self.c + k, self.count)

    @property
    def valid(self):
        return not isinstance(self.it, int) or 0 <= self.n < self.count


def wait(eng, sem, value):
    if not isinstance(value, int) or value > 0:
        eng.wait_ge(sem, value)


def skewed(eng, step, count, lag=1):
    first = 2 if lag == 2 else 1
    pairs = (count - 1 - first) // 2
    for n in range(-1, first):
        step(Step(0, n, count))
    with eng.Fori(0, pairs) as it:
        for u in range(2):
            step(Step(it, first + u, count))
    for n in range(first + 2 * pairs, count + lag):
        step(Step(0, n, count))


def paired(eng, body, count):
    body(Step(0, 0, count), Step(0, 1, count))
    with eng.Fori(0, (count - 2) // 2) as it:
        body(Step(it, 2, count), Step(it, 3, count))


def flamingo(nc, t):
    ctx = ExitStack()
    with ctx:
        def sb(name, shape, dt=F32, scope=ctx):
            return scope.enter_context(nc.sbuf_tensor(name, shape, dt))

        sems = {}

        def sem(name):
            if name not in sems:
                sems[name] = ctx.enter_context(nc.semaphore(name))
            return sems[name]

        bank = [ctx.enter_context(nc.psum_tensor(f"bank{i}", [P, 512], F32)) for i in range(8)]

        x = sb("x", [P, TOK])
        ident = sb("ident", [P, P])
        ident_r = sb("ident_r", [P, P], F32R)
        ident_b = sb("ident_b", [P, P], BF16)
        wk0, wq0, wv0 = (sb(n, [P, DM]) for n in ("wk0", "wq0", "wv0"))
        wk1, wq1, wv1 = (sb(n, [P, DM]) for n in ("wk1", "wq1", "wv1"))
        bv1 = sb("bv1", [P, DM])
        rows = sb("rows", [64, P])
        cols = sb("cols", [P, 64])
        B1C, BQC, BKC = 0, 32, 33
        causal = sb("causal", [P, 384])
        g_in = sb("g_in", [P, 4])
        tg = sb("tg", [P, 4])
        clip = sb("clip", [P, 2])
        sig = sb("sig", [P, 2])
        magic = sb("magic", [P, 1])
        half_neg = sb("half_neg", [P, BT])
        eps = sb("eps_row", [P, BT])
        ones = sb("ones", [P, P])
        sel = {n: sb(f"sel_{n}", [P, GROUPS, P], F32R) for n in ("qhi", "qlo")}
        sum_rows = sb("sum_rows", [P, 8])
        we_pad = sb("we_pad", [P, 2, DM])
        neg_max_pad = [sb(f"neg_max_pad{i}", [P, 2, 2, 2, P], F32R) for i in range(2)]
        stats = [sb(f"stats{i}", [P, BT, 6]) for i in range(2)]
        mv = [sb(f"mv_{i}", [P, BT, 2]) for i in range(2)]
        var_eps = [sb(f"var_eps{i}", [P, BT]) for i in range(2)]
        rstd = [sb(f"rstd_{i}", [P, BT]) for i in range(2)]
        wait_taker = sb("wait_taker", [P, 4])
        set_mark = sb("set_mark", [P, 2])
        mv1 = sb("mv_first", [P, TILES, 2])
        rstd1 = sb("rstd_first", [P, TILES])
        wq_in = sb("wq_in", [P, 2 * CH, DM])
        wd_in = sb("wd_in", [P, FF0])
        w_amax = sb("w_amax", [P, 8])
        w_scale = sb("w_scale", [P, 8])
        w_inv = sb("w_inv", [P, 8])
        wgu_t = sb("wgu_t", [P, 2 * CH, P], BF16)
        wd_t = sb("wd_t", [P, CH, DM], BF16)
        sd_row = sb("sd_row", [P, DM])
        sd_all = sb("sd_all", [P, DM])
        gate_w = sb("gate_w", [P, EXPERTS])
        gate_hi = sb("gate_hi", [P, EXPERTS], F32R)
        gate_lo = sb("gate_lo", [P, EXPERTS], F32R)
        gate_b = sb("gate_b", [EXPERTS, 1])
        b2 = sb("b2", [EXPERTS, DM])
        xt_hi = sb("xt_hi", [P, TOK], F32R)
        xt_lo = sb("xt_lo", [P, TOK], F32R)
        smalls = sb("smalls", [P, 32])

        mid = ExitStack()
        v1 = sb("v1", [P, TILES, DM], scope=mid)
        q_hi = sb("q_hi", [P, TOK], F32R, mid)
        q_lo = sb("q_lo", [P, TOK], F32R, mid)
        k_all = sb("k_all", [P, GROUPS, TOK], F32R, mid)

        ab = ExitStack()
        k_hi = sb("k_hi", [P, TOK], F32R, ab)
        k_lo = sb("k_lo", [P, TOK], F32R, ab)
        xn2_t = sb("xn2_t", [P, TOK], scope=ab)
        amax0 = sb("amax0", [P, BATCH + 8], scope=ab)
        a = ExitStack()
        w_tmp = sb("w_tmp", [P, 2 * CH * DM], scope=a)
        w_q8 = sb("w_q8", [P, 2 * CH, DM], BF16, a)
        wd_tmp = sb("wd_tmp", [P, FF0], scope=a)
        wd_q8 = sb("wd_q8", [P, FF0], BF16, a)
        ctx_in = [sb(f"ctx_in{i}", [P, 2, DM], scope=a) for i in range(2)]
        xn1 = [sb(f"xn1_{i}", [P, 2, DM], scope=a) for i in range(2)]
        cx_t = [sb(f"cx_t{i}", [P, 512], scope=a) for i in range(2)]
        qk0 = [sb(f"qk0_{i}", [P, 512], scope=a) for i in range(2)]
        v0 = [sb(f"v0_{i}", [P, 256], scope=a) for i in range(2)]
        scores0 = [sb(f"scores0_{i}", [P, 384], scope=a) for i in range(2)]
        probs0 = [sb(f"probs0_{i}", [P, 384], scope=a) for i in range(2)]
        probs0_t = [sb(f"probs0_t{i}", [P, 384], scope=a) for i in range(2)]
        xn2 = [sb(f"xn2_{i}", [P, 256], scope=a) for i in range(2)]
        nmax0 = [sb(f"nmax0_{i}", [P, 2], scope=a) for i in range(2)]
        rsum0 = [sb(f"rsum0_{i}", [P, 2], scope=a) for i in range(2)]
        rinv0 = [sb(f"rinv0_{i}", [P, 4], scope=a) for i in range(2)]
        a.close()
        b = ExitStack()
        h = sb("h", [P, CH, TOK], scope=b)
        xq_f = [sb(f"xq_f{i}", [P, BLK], scope=b) for i in range(2)]
        xq = sb("xq", [P, TOK], BF16, b)
        silu = xn3_t = [sb(f"silu{i}", [P, BLK], scope=b) for i in range(2)]
        hq = [sb(f"hq{i}", [P, CH, BLK], BF16, b) for i in range(2)]
        down = xn3 = [sb(f"down{i}", [P, BLK], scope=b) for i in range(2)]
        amax1 = sb("amax1", [P, 8], scope=b)
        gu_scale = sb("gu_scale", [P, 2 * CH], scope=b)
        b.close()
        ab.close()

        c = ExitStack()
        k_quad = [sb(f"k_quad{i}", [P, QUADS, GROUPS, SEQ], F32R, c) for i in range(2)]
        q_st = [sb(f"q_st{i}", [P, GROUPS, SEQ], F32R, c) for i in range(2)]
        v_st = [sb(f"v_st{i}", [P, 2, BLK], scope=c) for i in range(2)]
        probs = [sb(f"probs{i}", [P, QUADS, 2, SEQ], scope=c) for i in range(2)]
        nmax = [sb(f"nmax{i}", [P, 2, 2, 2, QUADS], scope=c) for i in range(2)]
        av = sb("av", [P, 512], scope=c)
        sums_inv = sb("sums_inv", [P, 2, 2, 8], scope=c)
        inv_wide = sb("inv_wide", [P, 2, 2, P], scope=c)
        on = sb("on", [P, 512], scope=c)
        xn4 = sb("xn4", [P, SEQ], scope=c)
        c.close()
        mid.close()

        d = ctx
        gates_t = sb("gates_t", [EXPERTS, TOK], scope=d)
        gates = sb("gates", [P, TILES, EXPERTS], scope=d)
        top = sb("top", [P, TILES, 8], scope=d)
        top_i = sb("top_i", [P, TILES, 8], U32, d)
        top_f = sb("top_f", [P, TILES, 2], scope=d)
        soft = sb("soft", [P, 4, TILES], scope=d)
        eidx = sb("eidx", [P, EXPERTS], scope=d)
        pick = [sb(f"pick{i}", [P, TILES, EXPERTS], scope=d) for i in range(2)]
        wte = sb("wte", [P, TILES, EXPERTS], scope=d)
        wte_t = sb("wte_t", [EXPERTS, TOK], scope=d)
        w1_in = [sb(f"w1_in{i}", [P, HID], scope=d) for i in range(2)]
        w1_hi = [sb(f"w1_hi{i}", [P, HID], F32R, d) for i in range(2)]
        w1_lo = [sb(f"w1_lo{i}", [P, HID], F32R, d) for i in range(2)]
        b1_cols = [sb(f"b1_cols{i}", [P, HC], scope=d) for i in range(2)]
        w2_in = [sb(f"w2_in{i}", [P, HC, DM], scope=d) for i in range(2)]
        w_tok = [sb(f"w_tok{i}", [P, TOK], scope=d) for i in range(2)]
        hid = [sb(f"hid{i}", [P, HC, BLK], scope=d) for i in range(2)]
        ytmp = [sb(f"ytmp{i}", [P, BLK], scope=d) for i in range(2)]
        acc = sb("acc", [P, TOK], scope=d)
        wte_dram = nc.dram_tensor("wte_scratch", (EXPERTS, TOK), F32, kind="Internal").ap()

        x_tiles = t["x"].rearrange("b (i p) d -> p (b i) d", p=P)
        ctx_tiles = t["ctx_1024"].rearrange("b (i p) d -> p (b i) d", p=P)
        out_tiles = t["out"].rearrange("b (i p) d -> p (b i) d", p=P)
        x3d = x[:, :].rearrange("p (i d) -> p i d", d=DM)

        block = ctx.enter_context(nc.Block())

        @block.sync
        def _(sp):
            def load_ctx(s):
                wait(sp, sem("cx_turned"), s.n - 1)
                sp.dma_start(ctx_in[s.par][:, :, :], ctx_tiles[:, ds(2 * s.n, 2), :])\
                  .then_inc(sem(f"ctx_landed{s.par}"), 16)

            def load_x(i):
                sp.dma_start(x3d[:, BT * i:BT * i + BT, :], x_tiles[:, BT * i:BT * i + BT, :])\
                  .then_inc(sem(f"x_landed{i}"), 16)

            load_ctx(Step(0, 0, BATCH))
            load_x(0)
            sp.wait_ge(sem("rows_set"), 1)
            sp.dma_start(rows[BKC:BKC + 1, :], t["L1_xattn_bk"].rearrange("(o n) -> o n", o=1))\
              .then_inc(sem("rows_landed"), 16)
            sp.dma_start(rows[BQC:BQC + 1, :], t["L1_xattn_bq"].rearrange("(o n) -> o n", o=1))\
              .then_inc(sem("rows_landed"), 16)
            sp.dma_start(rows[0:32, :], t["L1_ffn_b1"].rearrange("e (c p) -> (e c) p", p=P))\
              .then_inc(sem("rows_landed"), 16)
            load_ctx(Step(0, 1, BATCH))
            for i in range(1, 4):
                load_x(i)
            sp.dma_start(g_in[:, 0:2], t["g_xattn"].partition_broadcast(P)).then_inc(sem("g_landed"), 16)
            sp.dma_start(g_in[:, 2:4], t["g_ffn"].partition_broadcast(P)).then_inc(sem("g_landed"), 16)
            sp.dma_start(clip[:, 0:1], t["L0_ffn_clip_x"].partition_broadcast(P)).then_inc(sem("g_landed"), 16)
            sp.dma_start(clip[:, 1:2], t["L0_ffn_clip_down"].partition_broadcast(P)).then_inc(sem("g_landed"), 16)
            sp.wait_ge(sem("wq_in_set"), 1)
            for k, name in enumerate(("L0_ffn_w_gate", "L0_ffn_w_up")):
                sp.dma_start(wq_in[:, CH * k:CH * k + 2, :], t[name][0:256, :].rearrange("(c p) n -> p c n", p=P))\
                  .then_inc(sem("wffn_landed"), 16)
                sp.dma_start(wq_in[0:CHW[2], CH * k + 2, :], t[name][256:FF0, :]).then_inc(sem("wffn_landed"), 16)
            sp.dma_start(wd_in[:, :], t["L0_ffn_w_down"]).then_inc(sem("wffn_landed"), 16)
            sp.dma_start(bv1[:, :], t["L1_xattn_bv"].partition_broadcast(P)).then_inc(sem("bv1_landed"), 16)
            with sp.Fori(0, (BATCH - 2) // 2) as it:
                load_ctx(Step(it, 2, BATCH))
                load_ctx(Step(it, 3, BATCH))
            for dst, src in ((wq1, "L1_xattn_Wq"), (gate_w, "L1_ffn_gate_w"), (b2, "L1_ffn_b2")):
                sp.dma_start(dst[:, :], t[src]).then_inc(sem("wc_landed"), 16)
            sp.dma_start(gate_b[:, :], t["L1_ffn_gate_b"].rearrange("(n o) -> n o", o=1)).then_inc(sem("wc_landed"), 16)
            sp.wait_ge(sem("we_pad_set"), 1)
            we_rows = t["L1_xattn_We"].rearrange("(u r j e) n -> r j e u n", u=2, r=2, j=QUADS, e=HD)
            for r in range(2):
                for j in range(QUADS):
                    p0 = 32 * j + 16 * r
                    sp.dma_start(we_pad[p0:p0 + HD, :, :], we_rows[r, j]).then_inc(sem("wc_landed"), 16)
            sp.dma_start(we_pad[HD:HD + 1, 0, :], t["L1_xattn_be"].rearrange("(o n) -> o n", o=1))\
              .then_inc(sem("wc_landed"), 16)

            sp.wait_ge(sem("k_split"), 2 * BATCH)
            for s in range(3):
                src = k_hi if s in K_HI else k_lo
                for g in range(GROUPS):
                    for j in range(QUADS):
                        r0 = HD * (4 * g + j)
                        sp.dma_start(k_all[32 * j + 8 * s:32 * j + 8 * s + 8, g, :].bitcast(F32),
                                     src[r0:r0 + 8, :].bitcast(F32)).then_inc(sem("k_slotted"), 16)

            def stage_k(s, gp):
                wait(sp, sem("st_done"), 16 * s.n - 24 + 8 * gp)
                for j in range(QUADS):
                    r0 = 32 * j
                    sp.dma_start(k_quad[s.par][r0:r0 + MROW, j, 2 * gp:2 * gp + 2, :].bitcast(F32),
                                 k_all[r0:r0 + MROW, 2 * gp:2 * gp + 2, ds(s.n * SEQ, SEQ)].bitcast(F32))\
                      .then_inc(sem(f"k_staged{s.par}{gp}"), 16)

            sp.wait_ge(sem("k_slotted"), 16 * 3 * HEADS)
            sp.wait_ge(sem("k_quad_set"), 1)
            stage_k(Step(0, 0, BATCH), 0)
            stage_k(Step(0, 0, BATCH), 1)
            sp.wait_ge(sem("k_quad_set"), 2)
            stage_k(Step(0, 1, BATCH), 0)
            stage_k(Step(0, 1, BATCH), 1)
            with sp.Fori(0, (BATCH - 2) // 2) as it:
                for u in range(2):
                    stage_k(Step(it, 2 + u, BATCH), 0)
                    stage_k(Step(it, 2 + u, BATCH), 1)

            sp.wait_ge(sem("attended"), 4 * BATCH)
            sp.wait_ge(sem("xt_split"), 2 * BATCH)

            def load_expert(s):
                wait(sp, sem("w1_cut"), 2 * s.n - 2)
                sp.dma_start(w1_in[s.par][:, :], t["L1_ffn_w1"][ds(s.n, 1)].rearrange("o p n -> (o p) n"))\
                  .then_inc(sem(f"w1_landed{s.par}"), 16)
                wait(sp, sem("y_done"), NBLK * (s.n - 1))
                sp.dma_start(w2_in[s.par][:, :, :],
                             t["L1_ffn_w2"][ds(s.n, 1)].rearrange("o (c p) n -> p (o c) n", p=P))\
                  .then_inc(sem(f"w2_landed{s.par}"), 16)

            def load_token_weights(s):
                wait(sp, sem("y_weighed"), NBLK * (s.n - 1))
                sp.dma_start(w_tok[s.par][:, :],
                             wte_dram[ds(s.n, 1), :].rearrange("o n -> (o n)").partition_broadcast(P))\
                  .then_inc(sem(f"wtok_landed{s.par}"), 16)

            load_expert(Step(0, 0, EXPERTS))
            load_expert(Step(0, 1, EXPERTS))
            sp.wait_ge(sem("wte_turned"), NBLK)
            sp.dma_start(wte_dram, wte_t[:, :]).then_inc(sem("wte_stored"), 16)
            sp.wait_ge(sem("wte_stored"), 16)
            load_token_weights(Step(0, 0, EXPERTS))
            load_token_weights(Step(0, 1, EXPERTS))
            with sp.Fori(0, (EXPERTS - 2) // 2) as it:
                for u in range(2):
                    load_expert(Step(it, 2 + u, EXPERTS))
                    load_token_weights(Step(it, 2 + u, EXPERTS))
            for k in range(NBLK):
                sp.wait_ge(sem("x_final"), k + 1)
                sp.dma_start(out_tiles[:, BT * k:BT * k + BT, :], x3d[:, BT * k:BT * k + BT, :])\
                  .then_inc(sem("stored"), 16)
            sp.wait_ge(sem("stored"), 16 * NBLK)

        @block.gpsimd
        def _(pool):
            pool.memset(ident[:, :], 0.0).then_inc(sem("p_zero"), 1)
            pool.memset(causal[:, :], 0.0).then_inc(sem("p_zero"), 1)
            pool.memset(half_neg[:, :], -0.5).then_inc(sem("p_zero"), 1)
            pool.memset(eps[:, :], EPS).then_inc(sem("p_zero"), 1)
            pool.wait_ge(sem("p_zero"), 4)
            pool.affine_select(out=ident[:, :], in_=ident[:, :], compare_op=ALU.not_equal, fill=1.0,
                               base=0, pattern=[[-1, P]], channel_multiplier=1).then_inc(sem("ident_set"), 1)
            for c0 in (0, 256):
                pool.affine_select(out=causal[:, c0:c0 + P], in_=causal[:, c0:c0 + P], compare_op=ALU.is_ge,
                                   fill=MASKED, base=0, pattern=[[-1, P]], channel_multiplier=1)\
                    .then_inc(sem("causal_set"), 1)
            pool.memset(wq_in[:, :, :], 1.0).then_inc(sem("wq_in_set"), 1)
            pool.memset(magic[:, :], MAGIC).then_inc(sem("magic_set"), 1)
            pool.memset(ones[:, :], 1.0).then_inc(sem("ones_set"), 1)

            def rstd_of(n, mean_var, eps_sum, out, tiles):
                pool.wait_ge(sem("var_done"), n)
                pool.tensor_tensor(eps_sum[:, 0:tiles], mean_var[:, 0:tiles, 1], eps[:, 0:tiles], ALU.add)\
                    .then_inc(sem("eps_added"), 1)
                pool.wait_ge(sem("eps_added"), n)
                pool.tensor_tensor(out[:, 0:tiles], eps_sum[:, 0:tiles], half_neg[:, 0:tiles], ALU.pow)\
                    .then_inc(sem("rstd_done"), 1)

            def rstd_loop(base, tiles, count):
                with pool.Fori(0, count // 2) as it:
                    for u in range(2):
                        rstd_of(2 * it + (base + u + 1), mv[u], var_eps[u], rstd[u], tiles)

            for k in range(TILES // BT):
                rstd_of(LN1 + k + 1, mv1[:, BT * k:BT * k + BT, :], var_eps[k % 2], rstd1[:, BT * k:BT * k + BT], BT)
            pool.memset(we_pad[:, :, :], 0.0).then_inc(sem("we_pad_set"), 1)
            pool.wait_ge(sem("w_inv_set"), 1)
            for k in range(2 * CH):
                pool.tensor_scalar(w_tmp[:, k * DM:(k + 1) * DM], wq_in[:, k, :], w_inv[:, k:k + 1], MAGIC,
                                   ALU.mult, ALU.add).then_inc(sem("p_w"), 1)
            pool.tensor_scalar(wd_tmp[:, :], wd_in[:, :], w_inv[:, 6:7], MAGIC, ALU.mult, ALU.add)\
                .then_inc(sem("p_w"), 1)
            pool.wait_ge(sem("p_w"), 7)
            pool.tensor_scalar(w_tmp[:, :], w_tmp[:, :], MAGIC + QMAX, MAGIC - QMAX - 1.0, ALU.min, ALU.max)\
                .then_inc(sem("p_w"), 1)
            pool.tensor_scalar(wd_tmp[:, :], wd_tmp[:, :], MAGIC + QMAX, MAGIC - QMAX - 1.0, ALU.min, ALU.max)\
                .then_inc(sem("p_w"), 1)
            pool.wait_ge(sem("p_w"), 9)
            pool.tensor_scalar(w_q8[:, :, :].rearrange("p c n -> p (c n)"), w_tmp[:, :], -MAGIC, 1.0,
                               ALU.add, ALU.mult).then_inc(sem("w_rounded"), 1)
            pool.tensor_scalar(wd_q8[:, :], wd_tmp[:, :], -MAGIC, 1.0, ALU.add, ALU.mult)\
                .then_inc(sem("w_rounded"), 1)

            rstd_loop(LN2, 2, BATCH)
            pool.wait_ge(sem("amax0_done"), 1)
            pool.partition_all_reduce(amax0[:, 9:10], amax0[:, 8:9], P, bass.bass_isa.ReduceOp.max)\
                .then_inc(sem("gmax0"), 1)
            pool.wait_ge(sem("amax1_done"), 1)
            pool.partition_all_reduce(amax1[:, 5:6], amax1[:, 4:5], P, bass.bass_isa.ReduceOp.max)\
                .then_inc(sem("gmax1"), 1)
            def set_k_quad(i):
                pool.memset(k_quad[i][:, :, :, :].bitcast(F32), 0.0).then_inc(sem("k_quad_zero"), 1)
                pool.wait_ge(sem("k_quad_zero"), i + 1)
                for j in range(QUADS):
                    pool.memset(k_quad[i][32 * j:32 * j + 32, j, :, :].bitcast(F32), 1.0)\
                        .then_inc(sem("k_quad_ones"), 1)
                    pool.wait_ge(sem("k_quad_ones"), QUADS * i + j + 1)
                pool.memset(set_mark[:, i:i + 1], 0.0).then_inc(sem("k_quad_set"), 1)

            pool.wait_ge(sem("k_slotted"), 16 * 3 * HEADS)
            set_k_quad(0)
            rstd_loop(LN3, BT, NBLK)
            pool.wait_ge(sem("q_split"), 2 * NBLK)
            for i in range(2):
                pool.memset(v_st[i][:, :, :], 0.0).then_inc(sem("v_zero"), 1)
                pool.wait_ge(sem("v_zero"), i + 1)
                v4 = v_st[i][:, :, :].rearrange("p i (w r c) -> p i w r c", r=2, c=32)
                pool.memset(v4[:, :, :, 0, 8:16], 1.0).then_inc(sem("v_ones"), 1)
                pool.memset(v4[:, :, :, 1, 24:32], 1.0).then_inc(sem("v_ones"), 1)

            v1f = v1[:, :, :].rearrange("p i n -> p (i n)")

            def widen_v(s):
                wait(pool, sem("attended"), 4 * s.n - 4)
                for i in range(2):
                    for r in range(2):
                        def heads(tile):
                            return tile.rearrange("p (u r j e) -> p r u j e", u=2, r=2, e=HD)[:, r]
                        dst = v_st[s.par][:, i, :].rearrange("p (u j c) -> p u j c", u=2, c=64)
                        pool.tensor_tensor(dst[:, :, :, 48 * r:48 * r + 8],
                                           heads(v1f[:, ds(s.n * SEQ + i * P, P)]), heads(bv1[:, :]), ALU.add)\
                            .then_inc(sem("v_widened"), 1)

            def fourth_rstd(n, par):
                rstd_of(n, mv[par], var_eps[par], rstd[par], 2)

            pool.wait_ge(sem("bv1_landed"), 16)
            pool.wait_ge(sem("v_ones"), 4)
            widen_v(Step(0, 0, BATCH))
            set_k_quad(1)
            widen_v(Step(0, 1, BATCH))
            with pool.Fori(0, (BATCH - 2) // 2) as it:
                for u in range(2):
                    widen_v(Step(it, 2 + u, BATCH))
                    fourth_rstd(2 * it + (LN4 + u + 1), u)
            for u in range(2):
                fourth_rstd(LN4 + BATCH - 1 + u, u)
            pool.wait_ge(sem("attended"), 4 * BATCH)
            pool.wait_ge(sem("xt_split"), 2 * BATCH)
            pool.iota(eidx[:, :], pattern=[[1, EXPERTS]], base=0, channel_multiplier=0,
                      allow_small_or_imprecise_dtypes=True).then_inc(sem("eidx_set"), 1)
            pool.memset(acc[:, :], 0.0).then_inc(sem("acc_zero"), 1)

        @block.scalar
        def _(act):
            for dst, src in ((wq0, "L0_xattn_WQ"), (wk0, "L0_xattn_WK"), (wv0, "L0_xattn_WV"),
                             (wv1, "L1_xattn_Wv"), (wk1, "L1_xattn_Wk")):
                act.dma_start(dst[:, :], t[src]).then_inc(sem("wa_landed"), 16)

            def step_a(s):
                m, b, o = s + 1, s + (-1), s + (-2)
                if b.valid:
                    act.wait_ge(sem("probs0_turned"), b.n + 1)
                    wait(act, sem("attended0"), b.n - 1)
                    act.activation(probs0_t[b.par][:, :], bank[5][:, 0:384], ACT.Copy)\
                       .then_inc(sem("probs0_t_ready"), 1)
                if m.valid:
                    act.wait_ge(sem("cx_turned"), m.n + 1)
                    wait(act, sem("k1_projected"), m.n - 1)
                    act.activation(cx_t[m.par][:, :], bank[0][:, :], ACT.Copy).then_inc(sem("cx_ready"), 1)
                if s.valid:
                    act.wait_ge(sem("nmax0_done"), s.n + 1)
                    wait(act, sem("probs0_turned"), s.n - 1)
                    act.activation(probs0[s.par][:, 0:128], scores0[s.par][:, 0:128], ACT.Exp,
                                   bias=nmax0[s.par][:, 0:1], accum_out=rsum0[s.par][:, 0:1])
                    act.activation(probs0[s.par][:, 128:384], scores0[s.par][:, 128:384], ACT.Exp,
                                   bias=nmax0[s.par][:, 1:2], accum_out=rsum0[s.par][:, 1:2])\
                       .then_inc(sem("probs0_done"), 1)
                if o.valid:
                    act.wait_ge(sem("xn2_turned"), o.n + 1)
                    act.activation(xn2_t[:, ds(o.n * SEQ, SEQ)], bank[7][:, 0:256], ACT.Copy)\
                       .then_inc(sem("xn2_t_ready"), 1)
                if m.valid:
                    act.wait_ge(sem("qk0_projected"), m.n + 1)
                    wait(act, sem("scored"), m.n - 1)
                    act.activation(qk0[m.par][:, :], bank[1][:, :], ACT.Copy).then_inc(sem("qk0_ready"), 1)
                    act.wait_ge(sem("v_projected"), m.n + 1)
                    wait(act, sem("attended0"), m.n - 1)
                    act.activation(v0[m.par][:, :], bank[2][:, 0:256], ACT.Copy).then_inc(sem("v0_ready"), 1)
                    if isinstance(s.it, int) and s.n == -1:
                        act.wait_ge(sem("cols_set"), 1)
                    act.wait_ge(sem("k1_projected"), m.n + 1)
                    act.activation(k_hi[:, ds(m.n * SEQ, SEQ)], bank[3][:, 0:256], ACT.Identity,
                                   bias=cols[:, BKC:BKC + 1]).then_inc(sem("k_hi_done"), 1)
                if isinstance(s.it, int) and s.n == -1:
                    act.wait_ge(sem("g_landed"), 64)
                    act.activation(tg[:, :], g_in[:, :], ACT.Tanh).then_inc(sem("tg_set"), 1)
                    act.activation(sig[:, :], clip[:, :], ACT.Exp, scale=-1.0).then_inc(sem("sig_exp"), 1)

            skewed(act, step_a, BATCH, lag=2)

            act.wait_ge(sem("x_inv"), 1)
            act.wait_ge(sem("magic_set"), 1)
            act.wait_ge(sem("xn2_t_ready"), BATCH)
            act.wait_ge(sem("wd_turned"), 1)

            def scale_x(s):
                wait(act, sem("x_rounded"), s.n - 1)
                act.activation(xq_f[s.par][:, :], xn2_t[:, ds(s.n * BLK, BLK)], ACT.Identity,
                               bias=magic[:, 0:1], scale=smalls[:, 1:2]).then_inc(sem("x_scaled"), 1)

            def both_scale_x(s0, s1):
                scale_x(s0)
                scale_x(s1)

            paired(act, both_scale_x, NBLK)

            def silu_block(s):
                for ch in range(CH):
                    w = CHW[ch]
                    k = CH * s.n + ch
                    act.wait_ge(sem("gated"), k + 1)
                    wait(act, sem("h_done"), k - 1)
                    par = (CH * s.c + ch) % 2
                    act.activation(silu[par][0:w, :], bank[2 * ch][0:w, :], ACT.Silu,
                                   scale=gu_scale[0:w, ch:ch + 1]).then_inc(sem("silued"), 1)

            def both_silu(s0, s1):
                silu_block(s0)
                silu_block(s1)

            act.wait_ge(sem("gu_scaled"), 1)
            paired(act, both_silu, NBLK)
            act.wait_ge(sem("h_inv"), 1)

            def finish_ffn(s0, s1):
                for s in (s0, s1):
                    act.activation(h[:, :, ds(s.n * BLK, BLK)], h[:, :, ds(s.n * BLK, BLK)], ACT.Identity,
                                   bias=magic[:, 0:1], scale=smalls[:, 3:4]).then_inc(sem("h_scaled"), 1)
                for s in (s0, s1):
                    act.wait_ge(sem("xn3_turned"), s.n + 1)
                    wait(act, sem("q_projected"), s.n - 1)
                    act.activation(xn3_t[s.par][:, :], bank[2 + s.par][:, :], ACT.Copy).then_inc(sem("xn3_t_ready"), 1)
                for s in (s0, s1):
                    act.wait_ge(sem("q_projected"), s.n + 1)
                    act.activation(q_hi[:, ds(s.n * BLK, BLK)], bank[4 + s.par][:, :], ACT.Identity,
                                   bias=cols[:, BQC:BQC + 1]).then_inc(sem("q_hi_done"), 1)

            paired(act, finish_ffn, NBLK)

            def step_c(s):
                m, o = s + 1, s + (-1)

                def take_q(u):
                    act.wait_ge(sem("q_slotted"), 2 * m.n + u + 1)
                    if u == 0:
                        wait(act, sem("st_done"), 16 * (m.n - 1))
                    act.activation(q_st[m.par][:, 2 * u:2 * u + 2, :], bank[5 + u][:, :]
                                   .rearrange("p (g s) -> p g s", g=2), ACT.Copy).then_inc(sem("q_staged"), 1)

                for k in range(C_SLOTS):
                    if o.valid and k == 0:
                        act.wait_ge(sem("attended"), 4 * o.n + 4)
                        wait(act, sem("on_ready"), o.n)
                        act.activation(av[:, :], bank[4][:, :], ACT.Copy).then_inc(sem("av_ready"), 1)
                    if m.valid and k == 1:
                        take_q(0)
                    if o.valid and k == 3:
                        act.wait_ge(sem("sums_inverted"), o.n + 1)
                        act.activation(inv_wide[:, :, :, :].rearrange("p t u (w c) -> p (t u w) c", c=16),
                                       sums_inv[:, :, :, :].rearrange("p t u w -> p (t u w)").unsqueeze(2)
                                       .broadcast_to([P, 32, 16]), ACT.Copy).then_inc(sem("inv_widened"), 1)
                    if m.valid and k == 5:
                        take_q(1)
                    if o.valid and k == 15:
                        act.wait_ge(sem("xn4_turned"), o.n + 1)
                        act.activation(xt_hi[:, ds(o.n * SEQ, SEQ)], bank[7][:, 0:256], ACT.Copy)\
                           .then_inc(sem("xt_hi_done"), 1)
                    if s.valid and k < 16:
                        quad, j = k // 4, k % 4
                        if j == 0:
                            wait(act, sem("attended"), 4 * s.n + quad - 1)
                        act.wait_ge(sem("st_done"), 16 * s.n + k + 1)
                        act.activation(probs[quad % 2][:, j, :, :], bank[2 + j % 2][:, :]
                                       .rearrange("p (r s) -> p r s", r=2), ACT.Exp, scale=SC1)\
                           .then_inc(sem("exped"), 1)

            act.wait_ge(sem("k_slotted"), 16 * 3 * HEADS)
            skewed(act, step_c, BATCH)

            for k in range(NBLK):
                act.wait_ge(sem("gates_done"), k + 1)
                act.activation(gates_t[:, k * BLK:(k + 1) * BLK], bank[k][0:EXPERTS, :], ACT.Identity,
                               bias=gate_b[:, 0:1]).then_inc(sem("gates_t_ready"), 1)
            act.wait_ge(sem("top_gap"), 1)
            act.activation(soft[:, 1, :], soft[:, 0, :], ACT.Exp).then_inc(sem("top_exp"), 1)
            for k in range(NBLK):
                act.wait_ge(sem("wte_turning"), k + 1)
                act.activation(wte_t[:, k * BLK:(k + 1) * BLK], bank[4 + k][0:EXPERTS, :], ACT.Copy)\
                   .then_inc(sem("wte_turned"), 1)

            def gelus(s):
                for k in range(NBLK):
                    wait(act, sem("y_done"), NBLK * s.n + k - 1)
                    for ch in range(HC):
                        act.wait_ge(sem("hid_done"), HC * (NBLK * s.n + k) + ch + 1)
                        act.activation(hid[k % 2][:, ch, :], bank[ch][:, :], ACT.Gelu,
                                       bias=b1_cols[s.par][:, ch:ch + 1]).then_inc(sem("gelued"), 1)

            def both_gelus(s0, s1):
                gelus(s0)
                gelus(s1)

            paired(act, both_gelus, EXPERTS)

        @block.vector
        def _(dve):
            dve.memset(rows[:, :], 0.0).then_inc(sem("rows_set"), 1)
            def first_norm(k):
                dve.wait_ge(sem(f"x_landed{k}"), 16)
                for i in range(BT):
                    ins = dve.bn_stats(stats[k % 2][:, i, :], x3d[:, BT * k + i, :])
                ins.then_inc(sem("halves_done"), 1)
                dve.wait_ge(sem("halves_done"), k + 1)
                for i in range(BT):
                    ins = dve.bn_aggr(mv1[:, BT * k + i, :], stats[k % 2][:, i, :])
                ins.then_inc(sem("var_done"), 1)

            def set_constants():
                for i in range(2):
                    dve.memset(neg_max_pad[i][:, :, :, :, :].bitcast(F32), 0.0).then_inc(sem("v_pad"), 1)
                for n in ("qhi", "qlo"):
                    dve.memset(sel[n][:, :, :].bitcast(F32), 0.0).then_inc(sem("v_pad"), 1)
                dve.wait_ge(sem("ident_set"), 1)
                dve.wait_ge(sem("v_pad"), 4)
                dve.tensor_copy(ident_b[:, :], ident[:, :]).then_inc(sem("v_const"), 1)
                dve.tensor_copy(ident_r[:, :], ident[:, :]).then_inc(sem("v_const"), 1)
                iv = ident[:, :].rearrange("p (g j e) -> p g j e", g=GROUPS, e=HD)
                for n, slots in (("qhi", Q_HI), ("qlo", Q_LO)):
                    for s in slots:
                        dve.tensor_copy(sel[n][:, :, :].rearrange("p g (j s e) -> p g j s e", j=QUADS, s=4)
                                        [:, :, :, s, :], iv).then_inc(sem("v_const"), 1)
                dve.tensor_copy(sum_rows[:, :], ident[:, :].rearrange("p (w c) -> p w c", c=16)[:, :, HD])\
                   .then_inc(sem("v_const"), 1)

            def ffn_scales():
                dve.wait_ge(sem("sig_exp"), 1)
                dve.tensor_scalar(sig[:, :], sig[:, :], 1.0, QMAX, ALU.add, ALU.mult).then_inc(sem("v_sig"), 1)
                dve.wait_ge(sem("v_sig"), 1)
                dve.reciprocal(sig[:, :], sig[:, :]).then_inc(sem("v_sig"), 1)
                dve.wait_ge(sem("wffn_landed"), 80)
                dve.tensor_reduce(w_amax[:, 0:6], wq_in[:, :, :], AX.X, ALU.max, apply_absolute_value=True)\
                   .then_inc(sem("v_w"), 1)
                dve.tensor_reduce(w_amax[:, 6:7], wd_in[:, :], AX.X, ALU.max, apply_absolute_value=True)\
                   .then_inc(sem("v_w"), 1)
                dve.wait_ge(sem("v_w"), 2)
                dve.tensor_scalar(w_scale[:, 0:7], w_amax[:, 0:7], 1.0 / QMAX, None, ALU.mult).then_inc(sem("v_w"), 1)
                dve.wait_ge(sem("v_w"), 3)
                dve.reciprocal(w_inv[:, 0:7], w_scale[:, 0:7]).then_inc(sem("w_inv_set"), 1)
                dve.tensor_scalar(sd_row[:, :], ident[:, :], w_scale[:, 6:7], None, ALU.mult)\
                   .then_inc(sem("sd_diag"), 1)

            def norm(out, src, par, i):
                return dve.tensor_scalar(out, src, mv[par][:, i, 0:1], rstd[par][:, i:i + 1], ALU.subtract, ALU.mult)

            def halves_of(par, tiles, column0):
                dve.memset(wait_taker[:, par:par + 1], 0.0)
                for i in range(tiles):
                    ins = dve.bn_stats(stats[par][:, i, :], x[:, ds(column0 + i * P, P)])
                ins.then_inc(sem("halves_done"), 1)

            def variances_of(n, par, tiles):
                dve.wait_ge(sem("halves_done"), n)
                dve.memset(wait_taker[:, 2 + par:3 + par], 0.0)
                for i in range(tiles):
                    ins = dve.bn_aggr(mv[par][:, i, :], stats[par][:, i, :])
                ins.then_inc(sem("var_done"), 1)

            def step_a(s):
                m, b, o = s + 1, s + (-1), s + (-2)
                start = isinstance(s.it, int) and s.n == -1
                if m.valid:
                    dve.wait_ge(sem("rstd_done"), LN1 + (1 if start else 4))
                    wait(dve, sem("cx_turned"), m.n - 1)
                    mv1f = mv1[:, :, :].rearrange("p i c -> p (i c)")
                    for i in range(2):
                        ins = dve.tensor_scalar(xn1[m.par][:, i, :], x[:, ds(m.n * SEQ + i * P, P)],
                                                mv1f[:, ds(4 * m.n + 2 * i, 1)], rstd1[:, ds(2 * m.n + i, 1)],
                                                ALU.subtract, ALU.mult)
                    ins.then_inc(sem("xn1_ready"), 1)
                if start:
                    for k in range(1, 4):
                        first_norm(k)
                    dve.wait_ge(sem("cols_turned"), 1)
                    dve.tensor_copy(cols[:, :], bank[6][:, 0:64]).then_inc(sem("cols_set"), 1)
                if s.valid:
                    dve.wait_ge(sem("causal_set"), 2)
                    dve.wait_ge(sem("scored"), s.n + 1)
                    wait(dve, sem("probs0_done"), s.n - 1)
                    dve.scalar_tensor_tensor(scores0[s.par][:, :], bank[4][:, 0:384], SC0, causal[:, :],
                                             ALU.mult, ALU.add).then_inc(sem("masked"), 1)
                if o.valid:
                    dve.wait_ge(sem("rstd_done"), o.n + (LN2 + 1))
                    wait(dve, sem("xn2_turned"), o.n)
                    for i in range(2):
                        ins = norm(xn2[o.par][:, i * P:(i + 1) * P], x[:, ds(o.n * SEQ + i * P, P)], o.par, i)
                    ins.then_inc(sem("xn2_ready"), 1)
                if s.valid:
                    dve.wait_ge(sem("masked"), s.n + 1)
                    dve.tensor_reduce(nmax0[s.par][:, 0:1], scores0[s.par][:, 0:128], AX.X, ALU.max, negate=True)
                    dve.tensor_reduce(nmax0[s.par][:, 1:2], scores0[s.par][:, 128:384], AX.X, ALU.max, negate=True)\
                       .then_inc(sem("nmax0_done"), 1)
                if b.valid:
                    dve.wait_ge(sem("probs0_done"), b.n + 1)
                    dve.reciprocal(rinv0[b.par][:, 0:2], rsum0[b.par][:, :]).then_inc(sem("rinv0_done"), 1)
                if o.valid:
                    dve.wait_ge(sem("xn2_ready"), o.n + 1)
                    dve.tensor_reduce(amax0[:, ds(o.n, 1)], xn2[o.par][:, :], AX.X, ALU.max,
                                      apply_absolute_value=True).then_inc(sem("amax0_part"), 1)
                if b.valid:
                    dve.wait_ge(sem("rinv0_done"), b.n + 1)
                    dve.tensor_scalar(rinv0[b.par][:, 2:4], rinv0[b.par][:, 0:2], tg[:, 0:1], None, ALU.mult)\
                       .then_inc(sem("rg0_done"), 1)
                    dve.wait_ge(sem("rg0_done"), b.n + 1)
                    dve.wait_ge(sem("attended0"), b.n + 1)
                    for i in range(2):
                        ins = dve.scalar_tensor_tensor(x[:, ds(b.n * SEQ + i * P, P)], bank[6][:, i * P:(i + 1) * P],
                                                       rinv0[b.par][:, 2 + i:3 + i], x[:, ds(b.n * SEQ + i * P, P)],
                                                       ALU.mult, ALU.add)
                    ins.then_inc(sem("x1_done"), 1)
                    dve.wait_ge(sem("x1_done"), b.n + 1)
                    halves_of(b.par, 2, b.n * SEQ)
                if m.valid:
                    dve.wait_ge(sem("v0_ready"), m.n + 1)
                    dve.tensor_copy(v1[:, :, :].rearrange("p i n -> p (i n)")[:, ds(m.n * SEQ, SEQ)],
                                    bank[2][:, 256:512]).then_inc(sem("v1_ready"), 1)
                if b.valid:
                    variances_of(b.n + (LN2 + 1), b.par, 2)
                if m.valid:
                    dve.wait_ge(sem("k_hi_done"), m.n + 1)
                    dve.scalar_tensor_tensor(k_lo[:, ds(m.n * SEQ, SEQ)], bank[3][:, 0:256], cols[:, BKC:BKC + 1],
                                             k_hi[:, ds(m.n * SEQ, SEQ)].bitcast(F32), ALU.add, ALU.subtract)\
                       .then_inc(sem("k_split"), 2)
                if start:
                    set_constants()
                    ffn_scales()
                    dve.wait_ge(sem("tg_set"), 1)

            first_norm(0)
            skewed(dve, step_a, BATCH, lag=2)

            dve.wait_ge(sem("wgu_turned"), 1)
            dve.tensor_copy(wgu_t[:, :, :].rearrange("p c n -> p (c n)"), bank[0][:, :].bitcast(BF16)[:, 0:2 * CH * P])\
               .then_inc(sem("ffn_w_ready"), 1)
            dve.wait_ge(sem("wd_turned"), 1)
            wd_ps = bank[1][:, :].bitcast(BF16)
            dve.tensor_copy(wd_t[:, 0:2, :].rearrange("p c n -> p (c n)"), wd_ps[:, 0:2 * P]).then_inc(sem("ffn_w_ready"), 1)
            dve.tensor_copy(wd_t[0:CHW[2], 2, :], wd_ps[0:CHW[2], 2 * P:3 * P]).then_inc(sem("ffn_w_ready"), 1)
            dve.wait_ge(sem("xn2_t_ready"), BATCH)
            dve.wait_ge(sem("amax0_part"), BATCH)
            dve.tensor_reduce(amax0[:, 8:9], amax0[:, 0:8], AX.X, ALU.max).then_inc(sem("amax0_done"), 1)
            dve.wait_ge(sem("v_sig"), 2)
            dve.wait_ge(sem("gmax0"), 1)
            dve.tensor_scalar(smalls[:, 0:1], amax0[:, 9:10], sig[:, 0:1], None, ALU.mult).then_inc(sem("v_sig"), 1)
            dve.wait_ge(sem("v_sig"), 3)
            dve.reciprocal(smalls[:, 1:2], smalls[:, 0:1]).then_inc(sem("x_inv"), 1)
            dve.tensor_scalar(gu_scale[:, :], w_scale[:, 0:6], smalls[:, 0:1], None, ALU.mult)\
               .then_inc(sem("gu_scaled"), 1)
            dve.memset(h[96:128, 2, :], 0.0).then_inc(sem("h_pad"), 1)

            def round_x(s):
                dve.wait_ge(sem("x_scaled"), s.n + 1)
                dve.tensor_scalar(xq_f[s.par][:, :], xq_f[s.par][:, :], MAGIC + QMAX, MAGIC - QMAX - 1.0,
                                  ALU.min, ALU.max).then_inc(sem("x_clipped"), 1)

            def both_round_x(s0, s1):
                round_x(s0)
                round_x(s1)
                for s in (s0, s1):
                    dve.wait_ge(sem("x_clipped"), s.n + 1)
                    dve.tensor_scalar(xq[:, ds(s.n * BLK, BLK)], xq_f[s.par][:, :], MAGIC, None, ALU.subtract)\
                       .then_inc(sem("x_rounded"), 1)

            paired(dve, both_round_x, NBLK)

            def products(s0, s1):
                for s in (s0, s1):
                    for ch in range(CH):
                        w = CHW[ch]
                        k = CH * s.n + ch
                        par = (CH * s.c + ch) % 2
                        dve.wait_ge(sem("upped"), k + 1)
                        dve.wait_ge(sem("silued"), k + 1)
                        dve.scalar_tensor_tensor(h[0:w, ch, ds(s.n * BLK, BLK)], bank[2 * ch + 1][0:w, :],
                                                 gu_scale[0:w, CH + ch:CH + ch + 1], silu[par][0:w, :],
                                                 ALU.mult, ALU.mult).then_inc(sem("h_done"), 1)
                    if s is s1:
                        dve.wait_ge(sem("h_done"), CH * s0.n + CH)
                        dve.tensor_reduce(amax1[:, ds(s0.n, 1)], h[:, :, ds(s0.n * BLK, BLK)], AX.XY, ALU.max,
                                          apply_absolute_value=True).then_inc(sem("amax1_part"), 1)
                dve.wait_ge(sem("h_done"), CH * s1.n + CH)
                dve.tensor_reduce(amax1[:, ds(s1.n, 1)], h[:, :, ds(s1.n * BLK, BLK)], AX.XY, ALU.max,
                                  apply_absolute_value=True).then_inc(sem("amax1_part"), 1)

            dve.wait_ge(sem("h_pad"), 1)
            dve.wait_ge(sem("gu_scaled"), 1)
            paired(dve, products, NBLK)
            dve.wait_ge(sem("amax1_part"), NBLK)
            dve.tensor_reduce(amax1[:, 4:5], amax1[:, 0:4], AX.X, ALU.max).then_inc(sem("amax1_done"), 1)
            dve.wait_ge(sem("gmax1"), 1)
            dve.tensor_scalar(smalls[:, 2:3], amax1[:, 5:6], sig[:, 1:2], None, ALU.mult).then_inc(sem("v_sig"), 1)
            dve.wait_ge(sem("v_sig"), 4)
            dve.reciprocal(smalls[:, 3:4], smalls[:, 2:3]).then_inc(sem("h_inv"), 1)
            dve.tensor_scalar(smalls[:, 4:5], smalls[:, 2:3], tg[:, 2:3], None, ALU.mult).then_inc(sem("v_sig"), 1)
            dve.wait_ge(sem("v_sig"), 5)
            dve.wait_ge(sem("sd_spread"), 1)
            dve.tensor_scalar(sd_all[:, :], bank[7][:, 0:DM], smalls[:, 4:5], None, ALU.mult).then_inc(sem("sd_set"), 1)
            dve.wait_ge(sem("sd_set"), 1)

            def finish_ffn(s0, s1):
                for s in (s0, s1):
                    dve.wait_ge(sem("h_scaled"), s.n + 1)
                    hb = h[:, :, ds(s.n * BLK, BLK)]
                    dve.tensor_scalar(hb, hb, MAGIC + QMAX, MAGIC - QMAX - 1.0, ALU.min, ALU.max)\
                       .then_inc(sem("h_clipped"), 1)
                for s in (s0, s1):
                    dve.wait_ge(sem("h_clipped"), s.n + 1)
                    wait(dve, sem("downed"), s.n - 1)
                    dve.tensor_scalar(hq[s.par][:, :, :], h[:, :, ds(s.n * BLK, BLK)], MAGIC, None, ALU.subtract)\
                       .then_inc(sem("h_rounded"), 1)
                for s in (s0, s1):
                    dve.wait_ge(sem("downed"), s.n + 1)
                    wait(dve, sem("xn3_turned"), s.n - 1)
                    dve.tensor_tensor(down[s.par][:, :].rearrange("p (i d) -> p i d", d=DM),
                                      bank[s.par][:, :].rearrange("p (i d) -> p i d", d=DM),
                                      sd_all[:, :].unsqueeze(1).broadcast_to([P, BT, DM]), ALU.mult)\
                       .then_inc(sem("down_scaled"), 1)
                for s in (s0, s1):
                    dve.wait_ge(sem("down_scaled"), s.n + 1)
                    xb = x[:, ds(s.n * BLK, BLK)]
                    dve.tensor_tensor(xb, down[s.par][:, :], xb, ALU.add).then_inc(sem("x2_done"), 1)
                for s in (s0, s1):
                    dve.wait_ge(sem("x2_done"), s.n + 1)
                    halves_of(s.par, BT, s.n * BLK)
                for s in (s0, s1):
                    variances_of(s.n + (LN3 + 1), s.par, BT)
                for s in (s0, s1):
                    dve.wait_ge(sem("rstd_done"), s.n + (LN3 + 1))
                    for i in range(BT):
                        ins = norm(xn3[s.par][:, i * P:(i + 1) * P], x[:, ds(s.n * BLK + i * P, P)], s.par, i)
                    ins.then_inc(sem("xn3_ready"), 1)
                for s in (s0, s1):
                    dve.wait_ge(sem("q_hi_done"), s.n + 1)
                    dve.scalar_tensor_tensor(q_lo[:, ds(s.n * BLK, BLK)], bank[4 + s.par][:, :], cols[:, BQC:BQC + 1],
                                             q_hi[:, ds(s.n * BLK, BLK)].bitcast(F32), ALU.add, ALU.subtract)\
                       .then_inc(sem("q_split"), 2)

            paired(dve, finish_ffn, NBLK)

            def step_c(s):
                m, o = s + 1, s + (-1)

                def maximum(u):
                    gp, qt, j = u // 8, u // 4 % 2, u % 4
                    dve.wait_ge(sem("s_done"), 16 * m.n + u + 1)
                    if u == 0:
                        wait(dve, sem("max_split"), 2 * m.n - 2)
                    dve.tensor_reduce(nmax[m.par][:, gp, qt, :, j],
                                      bank[u % 2][:, :].rearrange("p (r s) -> p r s", r=2), AX.X, ALU.max,
                                      negate=True).then_inc(sem("s_maxed"), 1)

                def split_maxima(b, gp):
                    i = 2 * b.n + gp
                    pad = neg_max_pad[b.par][:, gp, :, :, :].rearrange("p t g (j c) -> p (t g j) c", c=32)
                    nm = nmax[b.par][:, gp, :, :, :].rearrange("p t g j -> p (t g j)").unsqueeze(2)
                    dve.wait_ge(sem("s_maxed"), 16 * b.n + 8 * gp + 8)
                    wait(dve, sem("max_turned"), i - 3)
                    dve.tensor_copy(pad[:, :, MROW:MROW + 1], nm).then_inc(sem("max_hi"), 1)
                    dve.wait_ge(sem("max_hi"), i + 1)
                    dve.tensor_tensor(pad[:, :, MROW + 1:MROW + 2], nm, pad[:, :, MROW:MROW + 1].bitcast(F32),
                                      ALU.subtract).then_inc(sem("max_split"), 1)

                def shift_q(b, gp):
                    dve.wait_ge(sem("max_turned"), 2 * b.n + gp + 1)
                    qs = q_st[b.par][:, 2 * gp:2 * gp + 2, :]
                    dve.tensor_tensor(qs, bank[5 + gp][:, :].rearrange("p (g s) -> p g s", g=2),
                                      qs.bitcast(F32), ALU.add).then_inc(sem("q_shifted"), 1)

                for k in range(C_SLOTS):
                    if s.valid and k == 0:
                        split_maxima(s, 1)
                    if s.valid and k == 1:
                        shift_q(s, 1)
                    if o.valid and k == 2:
                        dve.wait_ge(sem("sums_turned"), o.n + 1)
                        wait(dve, sem("inv_widened"), o.n)
                        dve.reciprocal(sums_inv[:, :, :, :].rearrange("p t u w -> p (t u w)"), bank[7][:, 0:32])\
                           .then_inc(sem("sums_inverted"), 1)
                    if o.valid and k == 6:
                        dve.wait_ge(sem("inv_spread"), o.n + 1)
                        wait(dve, sem("wo_done"), o.n)
                        dve.tensor_tensor(on[:, :], av[:, :], bank[7][:, :], ALU.mult).then_inc(sem("on_ready"), 1)
                    if o.valid and k == 9:
                        dve.wait_ge(sem("wo_done"), o.n + 1)
                        xb = x[:, ds(o.n * SEQ, SEQ)]
                        dve.scalar_tensor_tensor(xb, bank[7][:, 0:256], tg[:, 1:2], xb, ALU.mult, ALU.add)\
                           .then_inc(sem("x3_done"), 1)
                    if o.valid and k == 10:
                        dve.wait_ge(sem("x3_done"), o.n + 1)
                        halves_of(o.par, 2, o.n * SEQ)
                    if o.valid and k == 11:
                        variances_of(o.n + (LN4 + 1), o.par, 2)
                    if m.valid and k == 11:
                        split_maxima(m, 0)
                    if m.valid and k == 12:
                        shift_q(m, 0)
                    if o.valid and k == 13:
                        dve.wait_ge(sem("rstd_done"), o.n + (LN4 + 1))
                        wait(dve, sem("xn4_turned"), o.n)
                        for i in range(2):
                            ins = norm(xn4[:, i * P:(i + 1) * P], x[:, ds(o.n * SEQ + i * P, P)], o.par, i)
                        ins.then_inc(sem("xn4_ready"), 1)
                    if o.valid and k == 17:
                        dve.wait_ge(sem("xt_hi_done"), o.n + 1)
                        dve.tensor_tensor(xt_lo[:, ds(o.n * SEQ, SEQ)], bank[7][:, 0:256],
                                          xt_hi[:, ds(o.n * SEQ, SEQ)].bitcast(F32), ALU.subtract)\
                           .then_inc(sem("xt_split"), 2)
                    if m.valid and 2 <= k:
                        maximum(k - 2)

            skewed(dve, step_c, BATCH)

            dve.wait_ge(sem("wc_landed"), 16 * (4 + 2 * QUADS + 1))
            dve.tensor_copy(gate_hi[:, :], gate_w[:, :]).then_inc(sem("gw_hi"), 1)
            dve.wait_ge(sem("gw_hi"), 1)
            dve.tensor_tensor(gate_lo[:, :], gate_w[:, :], gate_hi[:, :].bitcast(F32), ALU.subtract)\
               .then_inc(sem("gw_split"), 1)

            def cut_w1(s):
                dve.wait_ge(sem(f"w1_landed{s.par}"), 16 * (s.half + 1))
                wait(dve, sem("hid_done"), HC * NBLK * (s.n - 1))
                wait(dve, sem("gelued"), HC * NBLK * (s.n - 1))
                dve.tensor_copy(b1_cols[s.par][:, :], cols[:, ds(HC * s.n, HC)])
                dve.tensor_copy(w1_hi[s.par][:, :], w1_in[s.par][:, :]).then_inc(sem("w1_cut"), 1)
                dve.wait_ge(sem("w1_cut"), 2 * s.n + 1)
                dve.tensor_tensor(w1_lo[s.par][:, :], w1_in[s.par][:, :], w1_hi[s.par][:, :].bitcast(F32),
                                  ALU.subtract).then_inc(sem("w1_cut"), 1)

            cut_w1(Step(0, 0, EXPERTS))
            dve.wait_ge(sem("gates_turned"), 1)
            dve.tensor_copy(gates[:, :, :], bank[4][:, 0:P].rearrange("p (i e) -> p i e", e=EXPERTS))\
               .then_inc(sem("v_top"), 1)
            dve.wait_ge(sem("v_top"), 1)
            for i in range(TILES):
                ins = dve.max(top[:, i, :], gates[:, i, :])
            ins.then_inc(sem("v_top"), 1)
            dve.wait_ge(sem("v_top"), 2)
            dve.tensor_tensor(soft[:, 0, :], top[:, :, 1], top[:, :, 0], ALU.subtract).then_inc(sem("top_gap"), 1)
            for i in range(TILES):
                ins = dve.max_index(top_i[:, i, :], top[:, i, :], gates[:, i, :])
            ins.then_inc(sem("v_top"), 1)
            dve.wait_ge(sem("top_exp"), 1)
            dve.tensor_scalar(soft[:, 2, :], soft[:, 1, :], 1.0, None, ALU.add).then_inc(sem("v_top"), 1)
            dve.wait_ge(sem("v_top"), 3)
            dve.tensor_copy(top_f[:, :, :], top_i[:, :, 0:2]).then_inc(sem("v_top"), 1)
            dve.wait_ge(sem("v_top"), 4)
            dve.reciprocal(soft[:, 2, :], soft[:, 2, :]).then_inc(sem("v_top"), 1)
            dve.wait_ge(sem("v_top"), 6)
            dve.tensor_tensor(soft[:, 3, :], soft[:, 2, :], soft[:, 1, :], ALU.mult).then_inc(sem("v_top"), 1)
            dve.wait_ge(sem("eidx_set"), 1)
            dve.wait_ge(sem("v_top"), 5)
            full = [P, TILES, EXPERTS]
            for k in range(2):
                dve.tensor_tensor(pick[k][:, :, :], eidx[:, :].unsqueeze(1).broadcast_to(full),
                                  top_f[:, :, k].unsqueeze(2).broadcast_to(full), ALU.is_equal)\
                   .then_inc(sem("v_top"), 1)
            dve.wait_ge(sem("v_top"), 7)
            dve.wait_ge(sem("v_top"), 9)
            for k in range(2):
                dve.tensor_tensor(pick[k][:, :, :], pick[k][:, :, :],
                                  soft[:, 2 + k, :].unsqueeze(2).broadcast_to(full), ALU.mult)\
                   .then_inc(sem("v_top"), 1)
            dve.wait_ge(sem("v_top"), 11)
            dve.tensor_tensor(wte[:, :, :], pick[0][:, :, :], pick[1][:, :, :], ALU.add).then_inc(sem("wte_ready"), 1)
            cut_w1(Step(0, 1, EXPERTS))

            def weigh(s):
                dve.wait_ge(sem(f"wtok_landed{s.par}"), 16 * (s.half + 1))
                for k in range(NBLK):
                    y = NBLK * s.n + k
                    dve.wait_ge(sem("y_done"), y + 1)
                    wait(dve, sem("acc_added"), y - 1)
                    dve.tensor_tensor(ytmp[k % 2][:, :], bank[4 + k % 2][:, :],
                                      w_tok[s.par][:, k * BLK:(k + 1) * BLK], ALU.mult).then_inc(sem("y_weighed"), 1)
                    dve.wait_ge(sem("y_weighed"), y + 1)
                    ab_ = acc[:, k * BLK:(k + 1) * BLK]
                    dve.tensor_tensor(ab_, ab_, ytmp[k % 2][:, :], ALU.add).then_inc(sem("acc_added"), 1)

            dve.wait_ge(sem("acc_zero"), 1)
            for n in range(2):
                weigh(Step(0, n, EXPERTS))
                cut_w1(Step(0, n + 2, EXPERTS))
            with dve.Fori(0, (EXPERTS - 4) // 2) as it:
                for u in range(2):
                    weigh(Step(it, 2 + u, EXPERTS))
                    cut_w1(Step(it, 4 + u, EXPERTS))
            weigh(Step(0, EXPERTS - 2, EXPERTS))
            weigh(Step(0, EXPERTS - 1, EXPERTS))
            for k in range(NBLK):
                dve.wait_ge(sem("out_done"), k + 1)
                xb = x[:, k * BLK:(k + 1) * BLK]
                dve.scalar_tensor_tensor(xb, bank[k][:, :], tg[:, 3:4], xb, ALU.mult, ALU.add)\
                   .then_inc(sem("x_final"), 1)

        @block.tensor
        def _(pe):
            def mm(out, lhsT, rhs, start=True, stop=True, **kw):
                return pe.matmul(out, lhsT, rhs, start=start, stop=stop, **kw)

            pe.wait_ge(sem("ident_set"), 1)

            def step_a(s):
                m, b, o = s + 1, s + (-1), s + (-2)
                start = isinstance(s.it, int) and s.n == -1
                if s.valid:
                    wait(pe, sem("masked"), s.n)
                    pe.wait_ge(sem("qk0_ready"), s.n + 1)
                    mm(bank[4][:, 0:128], qk0[s.par][:, 0:128], qk0[s.par][:, 256:384])
                    mm(bank[4][:, 128:384], qk0[s.par][:, 128:256], qk0[s.par][:, 256:512])\
                        .then_inc(sem("scored"), 1)
                if b.valid:
                    pe.wait_ge(sem("probs0_done"), b.n + 1)
                    wait(pe, sem("probs0_t_ready"), b.n)
                    for i in range(3):
                        ins = pe.transpose(bank[5][:, P * i:P * i + P], probs0[b.par][:, P * i:P * i + P], ident[:, :])
                    ins.then_inc(sem("probs0_turned"), 1)
                if m.valid:
                    pe.wait_ge(sem(f"ctx_landed{m.par}"), 16 * (m.half + 1))
                    pe.wait_ge(sem("xn1_ready"), m.n + 1)
                    wait(pe, sem("cx_ready"), m.n)
                    for i in range(2):
                        pe.transpose(bank[0][:, P * i:P * i + P], ctx_in[m.par][:, i, :], ident[:, :])
                    for i in range(2):
                        ins = pe.transpose(bank[0][:, 256 + P * i:256 + P * i + P], xn1[m.par][:, i, :], ident[:, :])
                    ins.then_inc(sem("cx_turned"), 1)
                if b.valid:
                    pe.wait_ge(sem("probs0_t_ready"), b.n + 1)
                    pe.wait_ge(sem("v0_ready"), b.n + 1)
                    wait(pe, sem("x1_done"), b.n)
                    pt, vv = probs0_t[b.par], v0[b.par]
                    mm(bank[6][:, 0:128], pt[:, 0:128], vv[:, 0:128])
                    mm(bank[6][:, 128:256], pt[:, 128:256], vv[:, 0:128], stop=False)
                    mm(bank[6][:, 128:256], pt[:, 256:384], vv[:, 128:256], start=False).then_inc(sem("attended0"), 1)
                if o.valid:
                    pe.wait_ge(sem("xn2_ready"), o.n + 1)
                    wait(pe, sem("xn2_t_ready"), o.n)
                    for i in range(2):
                        ins = pe.transpose(bank[7][:, P * i:P * i + P], xn2[o.par][:, P * i:P * i + P], ident[:, :])
                    ins.then_inc(sem("xn2_turned"), 1)
                if m.valid:
                    if start:
                        pe.wait_ge(sem("rows_landed"), 48)
                        pe.transpose(bank[6][:, 0:64], rows[:, :], ident[0:64, 0:64]).then_inc(sem("cols_turned"), 1)
                        pe.wait_ge(sem("wa_landed"), 80)
                    ct, xt = cx_t[m.par][:, 0:256], cx_t[m.par][:, 256:512]
                    pe.wait_ge(sem("cx_ready"), m.n + 1)
                    wait(pe, sem("qk0_ready"), m.n)
                    mm(bank[1][:, 0:256], wq0[:, :], ct)
                    mm(bank[1][:, 256:512], wk0[:, :], xt).then_inc(sem("qk0_projected"), 1)
                    wait(pe, sem("v0_ready"), m.n)
                    wait(pe, sem("v1_ready"), m.n)
                    for i in range(2):
                        mm(bank[2][:, P * i:P * i + P], ct[:, P * i:P * i + P], wv0[:, :])
                    for i in range(2):
                        ins = mm(bank[2][:, 256 + P * i:256 + P * i + P], ct[:, P * i:P * i + P], wv1[:, :])
                    ins.then_inc(sem("v_projected"), 1)
                    wait(pe, sem("k_split"), 2 * m.n)
                    mm(bank[3][:, 0:256], wk1[:, :], ct).then_inc(sem("k1_projected"), 1)

            skewed(pe, step_a, BATCH, lag=2)

            pe.wait_ge(sem("w_rounded"), 2)
            pe.wait_ge(sem("v_const"), 6)
            pe.wait_ge(sem("cx_ready"), BATCH)
            pe.wait_ge(sem("qk0_ready"), BATCH)
            wg_ps = bank[0][:, :].bitcast(BF16)
            wd_ps = bank[1][:, :].bitcast(BF16)
            for k in range(2 * CH):
                ins = pe.transpose(wg_ps[:, k * P:(k + 1) * P], w_q8[:, k, :], ident_b[:, :])
            ins.then_inc(sem("wgu_turned"), 1)
            for k in range(CH):
                ins = pe.transpose(wd_ps[0:CHW[k], k * P:k * P + P], wd_q8[:, k * P:k * P + CHW[k]], ident_b[:, :])
            ins.then_inc(sem("wd_turned"), 1)
            pe.wait_ge(sem("sd_diag"), 1)
            pe.wait_ge(sem("ones_set"), 1)
            pe.wait_ge(sem("xn2_t_ready"), BATCH)
            mm(bank[7][:, 0:DM], ones[:, :], sd_row[:, :]).then_inc(sem("sd_spread"), 1)

            pe.wait_ge(sem("ffn_w_ready"), 3)
            pe.wait_ge(sem("v0_ready"), BATCH)
            pe.wait_ge(sem("k_split"), 2 * BATCH)
            pe.wait_ge(sem("masked"), BATCH)
            pe.wait_ge(sem("probs0_t_ready"), BATCH)

            def gate_up(s0, s1):
                for s in (s0, s1):
                    pe.wait_ge(sem("x_rounded"), s.n + 1)
                    for ch in range(CH):
                        w = CHW[ch]
                        wait(pe, sem("silued"), CH * s.n + ch - (CH - 1))
                        mm(bank[2 * ch][0:w, :], wgu_t[:, ch, 0:w], xq[:, ds(s.n * BLK, BLK)])\
                            .then_inc(sem("gated"), 1)
                        wait(pe, sem("h_done"), CH * s.n + ch - (CH - 1))
                        mm(bank[2 * ch + 1][0:w, :], wgu_t[:, CH + ch, 0:w], xq[:, ds(s.n * BLK, BLK)])\
                            .then_inc(sem("upped"), 1)

            paired(pe, gate_up, NBLK)
            pe.wait_ge(sem("h_done"), CH * NBLK)
            pe.wait_ge(sem("wc_landed"), 16 * (4 + 2 * QUADS + 1))

            def finish_ffn(s0, s1):
                for s in (s0, s1):
                    pe.wait_ge(sem("h_rounded"), s.n + 1)
                    wait(pe, sem("down_scaled"), s.n - 1)
                    for i in range(BT):
                        for ch in range(CH):
                            w = CHW[ch]
                            ins = mm(bank[s.par][:, i * P:(i + 1) * P], hq[s.par][0:w, ch, i * P:(i + 1) * P],
                                     wd_t[0:w, ch, :], start=(ch == 0), stop=(ch == CH - 1))
                    ins.then_inc(sem("downed"), 1)
                for s in (s0, s1):
                    pe.wait_ge(sem("xn3_ready"), s.n + 1)
                    wait(pe, sem("xn3_t_ready"), s.n - 1)
                    for i in range(BT):
                        ins = pe.transpose(bank[2 + s.par][:, P * i:P * i + P], xn3[s.par][:, P * i:P * i + P],
                                           ident[:, :])
                    ins.then_inc(sem("xn3_turned"), 1)
                for s in (s0, s1):
                    pe.wait_ge(sem("xn3_t_ready"), s.n + 1)
                    wait(pe, sem("q_split"), 2 * (s.n - 1))
                    mm(bank[4 + s.par][:, :], wq1[:, :], xn3_t[s.par][:, :]).then_inc(sem("q_projected"), 1)

            paired(pe, finish_ffn, NBLK)

            pe.wait_ge(sem("q_split"), 2 * NBLK)

            def step_c(s):
                m, o = s + 1, s + (-1)

                def slot_q(u):
                    wait(pe, sem("q_shifted"), 2 * s.n + u + 1)
                    for gg in range(2):
                        g = 2 * u + gg
                        mm(bank[5 + u][:, gg * SEQ:(gg + 1) * SEQ], sel["qhi"][:, g, :],
                           q_hi[:, ds(m.n * SEQ, SEQ)], stop=False)
                        ins = mm(bank[5 + u][:, gg * SEQ:(gg + 1) * SEQ], sel["qlo"][:, g, :],
                                 q_lo[:, ds(m.n * SEQ, SEQ)], start=False)
                    ins.then_inc(sem("q_slotted"), 1)

                def by_query(u):
                    gp, qt, j = u // 8, u // 4 % 2, u % 4
                    if u % 8 == 0:
                        pe.wait_ge(sem("q_staged"), 2 * m.n + gp + 1)
                        pe.wait_ge(sem(f"k_staged{m.par}{gp}"), 64 * (m.half + 1))
                    wait(pe, sem("s_maxed"), 16 * m.n + u - 1)
                    for r in range(2):
                        g = 2 * gp + r
                        ins = mm(bank[u % 2][:, r * SEQ:(r + 1) * SEQ],
                                 q_st[m.par][:, g, qt * P:(qt + 1) * P], k_quad[m.par][:, j, g, :])
                    ins.then_inc(sem("s_done"), 1)

                def by_key(u):
                    gp, kt, j = u // 8, u // 4 % 2, u % 4
                    if u % 8 == 0:
                        pe.wait_ge(sem("q_shifted"), 2 * s.n + gp + 1)
                    wait(pe, sem("exped"), 16 * s.n + u - 1)
                    for r in range(2):
                        g = 2 * gp + r
                        ins = mm(bank[2 + u % 2][:, r * SEQ:(r + 1) * SEQ],
                                 k_quad[s.par][:, j, g, kt * P:(kt + 1) * P], q_st[s.par][:, g, :])
                    ins.then_inc(sem("st_done"), 1)

                def attend(quad, r):
                    gp, kt = quad // 2, quad % 2
                    if r == 0:
                        pe.wait_ge(sem("exped"), 16 * s.n + 4 * quad + 4)
                    if quad == 0 and r == 0:
                        pe.wait_ge(sem("v_widened"), 4 * s.n + 4)
                        wait(pe, sem("av_ready"), s.n)
                    for j in range(QUADS):
                        c0 = 32 * (2 * (4 * gp + j) + r)
                        ins = mm(bank[4][32 * j:32 * j + 32, gp * SEQ:(gp + 1) * SEQ],
                                 v_st[s.par][:, kt, c0:c0 + 32], probs[quad % 2][:, j, r, :],
                                 start=(kt == 0 and r == 0), stop=(kt == 1 and r == 1),
                                 tile_position=(0, 32 * j))
                    if r == 1:
                        ins.then_inc(sem("attended"), 1)

                def turn_maxima(b, gp):
                    pe.wait_ge(sem("max_split"), 2 * b.n + gp + 1)
                    pe.wait_ge(sem("q_staged"), 2 * b.n + gp + 1)
                    for gg in range(2):
                        for qt in range(2):
                            ins = mm(bank[5 + gp][:, gg * SEQ + qt * P:gg * SEQ + (qt + 1) * P],
                                     neg_max_pad[b.par][:, gp, qt, gg, :], ident_r[:, :])
                    ins.then_inc(sem("max_turned"), 1)

                for k in range(C_SLOTS):
                    if m.valid and k == 0:
                        slot_q(0)
                    if s.valid and k == 1:
                        turn_maxima(s, 1)
                    if o.valid and k == 1:
                        pe.wait_ge(sem("av_ready"), o.n + 1)
                        wait(pe, sem("xt_split"), 2 * o.n)
                        for qt in range(2):
                            for u in range(2):
                                c0 = 16 * qt + 8 * u
                                ins = mm(bank[7][:, c0:c0 + 8], av[:, u * SEQ + qt * P:u * SEQ + (qt + 1) * P],
                                         sum_rows[:, :])
                        ins.then_inc(sem("sums_turned"), 1)
                    if m.valid and k == 4:
                        slot_q(1)
                    if o.valid and k == 5:
                        pe.wait_ge(sem("inv_widened"), o.n + 1)
                        for u in range(2):
                            for qt in range(2):
                                ins = mm(bank[7][:, u * SEQ + qt * P:u * SEQ + (qt + 1) * P], inv_wide[:, qt, u, :],
                                         ident[:, :])
                        ins.then_inc(sem("inv_spread"), 1)
                    if o.valid and k == 8:
                        pe.wait_ge(sem("on_ready"), o.n + 1)
                        for qt in range(2):
                            for u in range(2):
                                ins = mm(bank[7][:, qt * P:(qt + 1) * P],
                                         on[:, u * SEQ + qt * P:u * SEQ + (qt + 1) * P],
                                         we_pad[:, u, :], start=(u == 0), stop=(u == 1))
                        ins.then_inc(sem("wo_done"), 1)
                    if m.valid and k == 12:
                        turn_maxima(m, 0)
                    if o.valid and k == 15:
                        pe.wait_ge(sem("xn4_ready"), o.n + 1)
                        for i in range(2):
                            ins = pe.transpose(bank[7][:, P * i:P * i + P], xn4[:, P * i:P * i + P], ident[:, :])
                        ins.then_inc(sem("xn4_turned"), 1)
                    if s.valid and k < 16:
                        by_key(k)
                    if s.valid and k >= 5 and k % 4 == 1:
                        attend(k // 4 - 1, 0)
                    if m.valid and k >= 2:
                        by_query(k - 2)
                    if s.valid and k >= 5 and k % 4 == 1:
                        attend(k // 4 - 1, 1)

            skewed(pe, step_c, BATCH)

            pe.wait_ge(sem("gw_split"), 1)
            pe.wait_ge(sem("xt_split"), 2 * BATCH)
            for k in range(NBLK):
                cs = slice(k * BLK, (k + 1) * BLK)
                if k == 0:
                    pe.wait_ge(sem("s_maxed"), 16 * BATCH)
                if k == 2:
                    pe.wait_ge(sem("exped"), 16 * BATCH)
                mm(bank[k][0:EXPERTS, :], gate_hi[:, :], xt_hi[:, cs], stop=False)
                mm(bank[k][0:EXPERTS, :], gate_hi[:, :], xt_lo[:, cs], start=False, stop=False)
                mm(bank[k][0:EXPERTS, :], gate_lo[:, :], xt_hi[:, cs], start=False).then_inc(sem("gates_done"), 1)
            pe.wait_ge(sem("av_ready"), BATCH)
            pe.wait_ge(sem("gates_t_ready"), NBLK)
            for i in range(TILES):
                ins = pe.transpose(bank[4][:, EXPERTS * i:EXPERTS * (i + 1)], gates_t[:, i * P:(i + 1) * P],
                                   ident[0:EXPERTS, 0:EXPERTS])
            ins.then_inc(sem("gates_turned"), 1)
            pe.wait_ge(sem("wte_ready"), 1)
            for i in range(TILES):
                k = i // BT
                ins = pe.transpose(bank[4 + k][0:EXPERTS, (i % BT) * P:(i % BT + 1) * P], wte[:, i, :], ident[:, :])
                if i % BT == BT - 1:
                    ins.then_inc(sem("wte_turning"), 1)
            pe.wait_ge(sem("wte_turned"), NBLK)

            def expert(s):
                pe.wait_ge(sem("w1_cut"), 2 * s.n + 2)
                for k in range(NBLK):
                    cs = slice(k * BLK, (k + 1) * BLK)
                    y = NBLK * s.n + k
                    for ch in range(HC):
                        wait(pe, sem("gelued"), HC * y + ch - (HC - 1))
                        wc = slice(ch * P, (ch + 1) * P)
                        mm(bank[ch][:, :], w1_hi[s.par][:, wc], xt_hi[:, cs], stop=False)
                        mm(bank[ch][:, :], w1_hi[s.par][:, wc], xt_lo[:, cs], start=False, stop=False)
                        mm(bank[ch][:, :], w1_lo[s.par][:, wc], xt_hi[:, cs], start=False).then_inc(sem("hid_done"), 1)
                    if k == 0:
                        pe.wait_ge(sem(f"w2_landed{s.par}"), 16 * (s.half + 1))
                    wait(pe, sem("y_weighed"), y - 1)
                    for ch in range(HC):
                        pe.wait_ge(sem("gelued"), HC * y + ch + 1)
                        ins = mm(bank[4 + k % 2][:, :], w2_in[s.par][:, ch, :], hid[k % 2][:, ch, :],
                                 start=(ch == 0), stop=(ch == HC - 1))
                    ins.then_inc(sem("y_done"), 1)

            def both_experts(s0, s1):
                expert(s0)
                expert(s1)

            paired(pe, both_experts, EXPERTS)

            pe.wait_ge(sem("gelued"), HC * NBLK * EXPERTS)
            for k in range(NBLK):
                pe.wait_ge(sem("acc_added"), NBLK * (EXPERTS - 1) + k + 1)
                for i in range(BT):
                    tok = slice(k * BLK + i * P, k * BLK + (i + 1) * P)
                    mm(bank[k][:, i * P:(i + 1) * P], acc[:, tok], ident[:, :], stop=False)
                    ins = mm(bank[k][:, i * P:(i + 1) * P], wte_t[:, tok], b2[:, :], start=False)
                ins.then_inc(sem("out_done"), 1)


_INS = ["x", "ctx_1024", "g_xattn", "g_ffn", "L0_xattn_WK", "L0_xattn_WQ", "L0_xattn_WV", "L0_ffn_clip_x",
        "L0_ffn_clip_down", "L0_ffn_w_gate", "L0_ffn_w_up", "L0_ffn_w_down", "L1_xattn_Wq", "L1_xattn_bq",
        "L1_xattn_Wk", "L1_xattn_bk", "L1_xattn_Wv", "L1_xattn_bv", "L1_xattn_We", "L1_xattn_be",
        "L1_ffn_gate_w", "L1_ffn_gate_b", "L1_ffn_w1", "L1_ffn_b1", "L1_ffn_w2", "L1_ffn_b2"]


def kernel(**inputs):
    import concourse.bacc as bacc
    from concourse.bass_utils import run_bass_kernel_spmd

    nc = bacc.Bacc("TRN2", target_bir_lowering=False, num_devices=1)
    arrays, t = {}, {}
    for name in _INS:
        a = np.ascontiguousarray(inputs[name])
        arrays[f"in_{name}"] = a
        t[name] = nc.dram_tensor(f"in_{name}", a.shape, mybir.dt.from_np(a.dtype), kind="ExternalInput").ap()
    t["out"] = nc.dram_tensor("out_x", (BATCH, SEQ, DM), F32, kind="ExternalOutput").ap()
    flamingo(nc, t)
    r = run_bass_kernel_spmd(nc, [arrays], core_ids=[0])
    return r.results[0]["out_x"]
```

```python
from contextlib import ExitStack

import numpy as np

import concourse.bass as bass
from concourse import mybir

F32, F32R, BF16 = mybir.dt.float32, mybir.dt.float32r, mybir.dt.bfloat16
U32 = mybir.dt.uint32
ACT = mybir.ActivationFunctionType
ALU = mybir.AluOpType
AX = mybir.AxisListType
ds = bass.ds

P = 128
BATCH, SEQ, DM = 8, 256, 128
TOK = BATCH * SEQ
TILES = TOK // P
HEADS, HD = 16, 8
FF0 = 352
CH = 3
CHW = [128, 128, FF0 - 256]
EXPERTS, HID = 8, 512
HC = HID // P
BLK = 512
NBLK = TOK // BLK
BT = BLK // P
LN1, LN2, LN3, LN4 = 0, 4, 4 + BATCH, 4 + BATCH + NBLK

EPS = 1e-5
QMAX = 127.0
MAGIC = 1.5 * 2.0 ** 23
MASKED = -1e30
SC0 = float(1.0 / np.sqrt(np.float32(DM)))
SC1 = float(1.0 / np.sqrt(HD))

QUADS, GROUPS = 4, 4
POOL_CH = (0, 1)
Q_HI, Q_LO = (0, 1), (2,)
K_HI, K_LO = (0, 2), (1,)
QUERY_BANKS = (0, 1, 6)
GATE_BANKS = (0, 1, 2, 6)
C_SLOTS = 18
QUERY_LAG = 1
MROW = 24
EULER = float(np.e)


class Step:

    def __init__(self, it, c, count):
        self.it, self.c, self.count = it, c, count
        self.par = c % 2

    @property
    def n(self):
        return 2 * self.it + self.c

    @property
    def half(self):
        return self.it + self.c // 2

    def __add__(self, k):
        return Step(self.it, self.c + k, self.count)

    @property
    def valid(self):
        return not isinstance(self.it, int) or 0 <= self.n < self.count


def wait(eng, sem, value):
    if not isinstance(value, int) or value > 0:
        eng.wait_ge(sem, value)


def skewed(eng, step, count, lag=1, lead=1):
    first = 2 if lag == 2 else 1
    pairs = (count - lead - first) // 2
    for n in range(-1, first):
        step(Step(0, n, count))
    with eng.Fori(0, pairs) as it:
        for u in range(2):
            step(Step(it, first + u, count))
    for n in range(first + 2 * pairs, count + lag):
        step(Step(0, n, count))


def paired(eng, body, count):
    body(Step(0, 0, count), Step(0, 1, count))
    with eng.Fori(0, (count - 2) // 2) as it:
        body(Step(it, 2, count), Step(it, 3, count))


def is_step(s, n):
    return isinstance(s.it, int) and s.n == n


def over_experts(eng, body):
    for n in range(2):
        body(Step(0, n, EXPERTS))
    with eng.Fori(0, (EXPERTS - 4) // 2) as it:
        for u in range(2):
            body(Step(it, 2 + u, EXPERTS))
    for n in range(EXPERTS - 2, EXPERTS):
        body(Step(0, n, EXPERTS))


def flamingo(nc, t):
    ctx = ExitStack()
    with ctx:
        def sb(name, shape, dt=F32, scope=ctx):
            return scope.enter_context(nc.sbuf_tensor(name, shape, dt))

        sems = {}

        def sem(name):
            if name not in sems:
                sems[name] = ctx.enter_context(nc.semaphore(name))
            return sems[name]

        bank = [ctx.enter_context(nc.psum_tensor(f"bank{i}", [P, 512], F32)) for i in range(8)]

        x = sb("x", [P, TOK])
        ident = sb("ident", [P, P])
        ident_r = sb("ident_r", [P, P], F32R)
        ident_b = sb("ident_b", [P, P], BF16)
        wk0, wq0, wv0 = (sb(n, [P, DM]) for n in ("wk0", "wq0", "wv0"))
        wk1, wq1, wv1 = (sb(n, [P, DM]) for n in ("wk1", "wq1", "wv1"))
        bv1 = sb("bv1", [P, DM])
        rows = sb("rows", [64, P])
        cols = sb("cols", [P, 64])
        B1C, BQC, BKC, B2C = 0, 32, 33, 34
        causal = sb("causal", [P, 384])
        g_in = sb("g_in", [P, 4])
        tg = sb("tg", [P, 4])
        clip = sb("clip", [P, 2])
        sig = sb("sig", [P, 2])
        magic = sb("magic", [P, 1])
        half_neg = sb("half_neg", [P, BT])
        eps = sb("eps_row", [P, BT])
        ones = sb("ones", [P, P])
        sel = {n: sb(f"sel_{n}", [P, GROUPS, P], F32R) for n in ("qhi", "qlo")}
        we_pad = sb("we_pad", [P, 2, DM])
        neg_max_pad = [sb(f"neg_max_pad{i}", [P, 2, 2, 2, P], F32R) for i in range(2)]
        stats = [sb(f"stats{i}", [P, BT, 6]) for i in range(2)]
        mv = [sb(f"mv_{i}", [P, BT, 2]) for i in range(2)]
        var_eps = [sb(f"var_eps{i}", [P, BT]) for i in range(2)]
        rstd = [sb(f"rstd_{i}", [P, BT]) for i in range(2)]
        wait_taker = sb("wait_taker", [P, 4])
        silu_first = sb("silu_first", [P, 1])
        exp_first = sb("exp_first", [P, 1])
        in_quad = sb("in_quad", [P, QUADS])
        mv1 = sb("mv_first", [P, TILES, 2])
        rstd1 = sb("rstd_first", [P, TILES])
        wq_in = sb("wq_in", [P, 2 * CH, DM])
        wd_in = sb("wd_in", [P, FF0])
        w_amax = sb("w_amax", [P, 8])
        w_scale = sb("w_scale", [P, 8])
        w_inv = sb("w_inv", [P, 8])
        wgu_t = sb("wgu_t", [P, 2 * CH, P], BF16)
        wd_t = sb("wd_t", [P, CH, DM], BF16)
        sd_row = sb("sd_row", [P, DM])
        sd_all = sb("sd_all", [P, DM])
        gate_w = sb("gate_w", [P, EXPERTS])
        gate_hi = sb("gate_hi", [P, EXPERTS], F32R)
        gate_lo = sb("gate_lo", [P, EXPERTS], F32R)
        gate_b = sb("gate_b", [EXPERTS, 1])
        xt_hi = sb("xt_hi", [P, TOK], F32R)
        xt_lo = sb("xt_lo", [P, TOK], F32R)
        smalls = sb("smalls", [P, 32])

        w1_in = [sb(f"w1_in{i}", [P, HID]) for i in range(2)]
        w1_hi = [sb(f"w1_hi{i}", [P, HID], F32R) for i in range(2)]
        w1_lo = [sb(f"w1_lo{i}", [P, HID], F32R) for i in range(2)]
        b1_cols = [sb(f"b1_cols{i}", [P, HC]) for i in range(2)]
        w2_in = [sb(f"w2_in{i}", [P, HC, DM]) for i in range(2)]
        w2_hi = [sb(f"w2_hi{i}", [P, HC, DM], F32R) for i in range(2)]
        w2_lo = [sb(f"w2_lo{i}", [P, HC, DM], F32R) for i in range(2)]

        mid = ExitStack()
        v1 = sb("v1", [P, TILES, DM], scope=mid)
        q_hi = sb("q_hi", [P, TOK], F32R, mid)
        q_lo = sb("q_lo", [P, TOK], F32R, mid)
        k_all = sb("k_all", [P, GROUPS, TOK], F32R, mid)

        ab = ExitStack()
        k_hi = sb("k_hi", [P, TOK], F32R, ab)
        k_lo = sb("k_lo", [P, TOK], F32R, ab)
        xn2_t = sb("xn2_t", [P, TOK], scope=ab)
        amax0 = sb("amax0", [P, BATCH + 8], scope=ab)
        a = ExitStack()
        w_tmp = sb("w_tmp", [P, 2 * CH * DM], scope=a)
        w_q8 = sb("w_q8", [P, 2 * CH, DM], BF16, a)
        wd_tmp = sb("wd_tmp", [P, FF0], scope=a)
        wd_q8 = sb("wd_q8", [P, FF0], BF16, a)
        ctx_in = [sb(f"ctx_in{i}", [P, 2, DM], scope=a) for i in range(2)]
        xn1 = [sb(f"xn1_{i}", [P, 2, DM], scope=a) for i in range(2)]
        cx_t = [sb(f"cx_t{i}", [P, 512], scope=a) for i in range(2)]
        qk0 = [sb(f"qk0_{i}", [P, 512], scope=a) for i in range(2)]
        v0 = [sb(f"v0_{i}", [P, 256], scope=a) for i in range(2)]
        scores0 = [sb(f"scores0_{i}", [P, 384], scope=a) for i in range(2)]
        probs0 = [sb(f"probs0_{i}", [P, 384], scope=a) for i in range(2)]
        probs0_t = [sb(f"probs0_t{i}", [P, 384], scope=a) for i in range(2)]
        xn2 = [sb(f"xn2_{i}", [P, 256], scope=a) for i in range(2)]
        nmax0 = [sb(f"nmax0_{i}", [P, 2], scope=a) for i in range(2)]
        rsum0 = [sb(f"rsum0_{i}", [P, 2], scope=a) for i in range(2)]
        rinv0 = [sb(f"rinv0_{i}", [P, 4], scope=a) for i in range(2)]
        a.close()
        b = ExitStack()
        h = sb("h", [P, NBLK * CH * BLK], scope=b)
        xq = sb("xq", [P, TOK], BF16, b)
        silu = xn3_t = [sb(f"silu{i}", [P, BLK], scope=b) for i in range(2)]
        hq = [sb(f"hq{i}", [P, CH, BLK], BF16, b) for i in range(2)]
        down = [sb(f"down{i}", [P, BLK], scope=b) for i in range(2)]
        xn3 = [sb(f"xn3_{i}", [P, BLK], scope=b) for i in range(2)]
        amax1 = sb("amax1", [P, CH * NBLK + 2], scope=b)
        gu_scale = sb("gu_scale", [P, 2 * CH], scope=b)
        b.close()
        ab.close()

        c = ExitStack()
        k_quad = [sb(f"k_quad{i}", [P, QUADS, GROUPS, SEQ], F32R, c) for i in range(2)]
        q_st = [sb(f"q_st{i}", [P, GROUPS, SEQ], F32R, c) for i in range(2)]
        v_st = [sb(f"v_st{i}", [P, 2, BLK], scope=c) for i in range(2)]
        probs = [sb(f"probs{i}", [P, QUADS, 2, SEQ], scope=c) for i in range(2)]
        nmax = [sb(f"nmax{i}", [P, 2, 2, 2, QUADS], scope=c) for i in range(2)]
        av = sb("av", [P, 512], scope=c)
        sums_inv = sb("sums_inv", [P, 2, 2, 8], scope=c)
        inv_wide = sb("inv_wide", [P, 2, 2, P], scope=c)
        on = sb("on", [P, 512], scope=c)
        xn4 = sb("xn4", [P, SEQ], scope=c)
        c.close()
        mid.close()

        d = ctx
        gates_t = sb("gates_t", [EXPERTS, TOK], scope=d)
        gates = sb("gates", [P, TILES, EXPERTS], scope=d)
        top = sb("top", [P, TILES, 8], scope=d)
        top_i = sb("top_i", [P, TILES, 8], U32, d)
        top_f = sb("top_f", [P, TILES, 2], scope=d)
        soft = sb("soft", [P, 4, TILES], scope=d)
        euler = sb("euler", [P, TILES], scope=d)
        eidx = sb("eidx", [P, EXPERTS], scope=d)
        pick = [sb(f"pick{i}", [P, TILES, EXPERTS], scope=d) for i in range(2)]
        wte = sb("wte", [P, TILES, EXPERTS], scope=d)
        wte_t = sb("wte_t", [EXPERTS, TOK], scope=d)
        w_tok = [sb(f"w_tok{i}", [P, TOK], scope=d) for i in range(2)]
        hid = [sb(f"hid{i}", [P, HC, BLK], scope=d) for i in range(2)]
        hid_hi = [sb(f"hid_hi{i}", [P, HC, BLK], F32R, d) for i in range(2)]
        hid_lo = [sb(f"hid_lo{i}", [P, HC, BLK], F32R, d) for i in range(2)]
        ytmp = [sb(f"ytmp{i}", [P, BLK], scope=d) for i in range(2)]
        acc = sb("acc", [P, TOK], scope=d)
        wte_dram = nc.dram_tensor("wte_scratch", (EXPERTS, TOK), F32, kind="Internal").ap()

        x_tiles = t["x"].rearrange("b (i p) d -> p (b i) d", p=P)
        ctx_tiles = t["ctx_1024"].rearrange("b (i p) d -> p (b i) d", p=P)
        out_tiles = t["out"].rearrange("b (i p) d -> p (b i) d", p=P)
        x3d = x[:, :].rearrange("p (i d) -> p i d", d=DM)

        def slot_keys(eng, s):
            src = k_hi if s in K_HI else k_lo
            for g in range(GROUPS):
                for j in range(QUADS):
                    r0 = HD * (4 * g + j)
                    eng.dma_start(k_all[32 * j + 8 * s:32 * j + 8 * s + 8, g, :].bitcast(F32),
                                  src[r0:r0 + 8, :].bitcast(F32)).then_inc(sem(f"k_slotted{s // 2}"), 16)

        def wait_slots(eng):
            eng.wait_ge(sem("k_slotted0"), 2 * 16 * HEADS)
            eng.wait_ge(sem("k_slotted1"), 16 * HEADS)

        block = ctx.enter_context(nc.Block())

        @block.sync
        def _(sp):
            def load_ctx(s):
                wait(sp, sem("cx_turned"), s.n - 1)
                sp.dma_start(ctx_in[s.par][:, :, :], ctx_tiles[:, ds(2 * s.n, 2), :])\
                  .then_inc(sem(f"ctx_landed{s.par}"), 16)

            def load_x(i):
                sp.dma_start(x3d[:, BT * i:BT * i + BT, :], x_tiles[:, BT * i:BT * i + BT, :])\
                  .then_inc(sem(f"x_landed{i}"), 16)

            load_ctx(Step(0, 0, BATCH))
            load_x(0)
            sp.wait_ge(sem("v_zeroed"), 1)
            sp.dma_start(rows[BKC:BKC + 1, :], t["L1_xattn_bk"].rearrange("(o n) -> o n", o=1))\
              .then_inc(sem("rows_landed"), 16)
            sp.dma_start(rows[BQC:BQC + 1, :], t["L1_xattn_bq"].rearrange("(o n) -> o n", o=1))\
              .then_inc(sem("rows_landed"), 16)
            sp.dma_start(rows[B2C:B2C + EXPERTS, :], t["L1_ffn_b2"]).then_inc(sem("rows_landed"), 16)
            sp.dma_start(rows[0:32, :], t["L1_ffn_b1"].rearrange("e (c p) -> (e c) p", p=P))\
              .then_inc(sem("rows_landed"), 16)
            load_ctx(Step(0, 1, BATCH))
            for i in range(1, 4):
                load_x(i)
            sp.dma_start(g_in[:, 0:2], t["g_xattn"].partition_broadcast(P)).then_inc(sem("g_landed"), 16)
            sp.dma_start(g_in[:, 2:4], t["g_ffn"].partition_broadcast(P)).then_inc(sem("g_landed"), 16)
            sp.dma_start(clip[:, 0:1], t["L0_ffn_clip_x"].partition_broadcast(P)).then_inc(sem("g_landed"), 16)
            sp.dma_start(clip[:, 1:2], t["L0_ffn_clip_down"].partition_broadcast(P)).then_inc(sem("g_landed"), 16)
            sp.wait_ge(sem("wq_in_set"), 1)
            for k, name in enumerate(("L0_ffn_w_gate", "L0_ffn_w_up")):
                sp.dma_start(wq_in[:, CH * k:CH * k + 2, :], t[name][0:256, :].rearrange("(c p) n -> p c n", p=P))\
                  .then_inc(sem("wffn_landed"), 16)
                sp.dma_start(wq_in[0:CHW[2], CH * k + 2, :], t[name][256:FF0, :]).then_inc(sem("wffn_landed"), 16)
            sp.dma_start(wd_in[:, :], t["L0_ffn_w_down"]).then_inc(sem("wffn_landed"), 16)
            sp.dma_start(bv1[:, :], t["L1_xattn_bv"].partition_broadcast(P)).then_inc(sem("bv1_landed"), 16)
            with sp.Fori(0, (BATCH - 2) // 2) as it:
                load_ctx(Step(it, 2, BATCH))
                load_ctx(Step(it, 3, BATCH))
            for dst, src in ((wq1, "L1_xattn_Wq"), (gate_w, "L1_ffn_gate_w")):
                sp.dma_start(dst[:, :], t[src]).then_inc(sem("wc_landed"), 16)
            sp.dma_start(gate_b[:, :], t["L1_ffn_gate_b"].rearrange("(n o) -> n o", o=1)).then_inc(sem("wc_landed"), 16)
            def load_expert(s):
                wait(sp, sem("w_cut"), 4 * (s.n - 1))
                sp.dma_start(w1_in[s.par][:, :], t["L1_ffn_w1"][ds(s.n, 1)].rearrange("o p n -> (o p) n"))\
                  .then_inc(sem(f"we_landed{s.par}"), 16)
                sp.dma_start(w2_in[s.par][:, :, :],
                             t["L1_ffn_w2"][ds(s.n, 1)].rearrange("o (c p) n -> p (o c) n", p=P))\
                  .then_inc(sem(f"we_landed{s.par}"), 16)

            load_expert(Step(0, 0, EXPERTS))
            load_expert(Step(0, 1, EXPERTS))
            sp.wait_ge(sem("we_pad_set"), 1)
            we_rows = t["L1_xattn_We"].rearrange("(u r j e) n -> r j e u n", u=2, r=2, j=QUADS, e=HD)
            for r in range(2):
                for j in range(QUADS):
                    p0 = 32 * j + 16 * r
                    sp.dma_start(we_pad[p0:p0 + HD, :, :], we_rows[r, j]).then_inc(sem("wc_landed"), 16)
            sp.dma_start(we_pad[HD:HD + 1, 0, :], t["L1_xattn_be"].rearrange("(o n) -> o n", o=1))\
              .then_inc(sem("wc_landed"), 16)

            sp.wait_ge(sem("k_split"), 2 * BATCH)
            for s in range(2):
                slot_keys(sp, s)

            def stage_k(s, gp):
                wait(sp, sem("st_done"), 16 * s.n - 24 + 8 * gp)
                for j in range(QUADS):
                    r0 = 32 * j
                    sp.dma_start(k_quad[s.par][r0:r0 + MROW, j, 2 * gp:2 * gp + 2, :].bitcast(F32),
                                 k_all[r0:r0 + MROW, 2 * gp:2 * gp + 2, ds(s.n * SEQ, SEQ)].bitcast(F32))\
                      .then_inc(sem(f"k_staged{s.par}{gp}"), 16)

            wait_slots(sp)
            sp.wait_ge(sem("k_quad_set"), QUADS)
            stage_k(Step(0, 0, BATCH), 0)
            stage_k(Step(0, 0, BATCH), 1)
            sp.wait_ge(sem("k_quad_set"), 2 * QUADS)
            stage_k(Step(0, 1, BATCH), 0)
            stage_k(Step(0, 1, BATCH), 1)
            with sp.Fori(0, (BATCH - 2) // 2) as it:
                for u in range(2):
                    stage_k(Step(it, 2 + u, BATCH), 0)
                    stage_k(Step(it, 2 + u, BATCH), 1)

            def load_token_weights(s):
                wait(sp, sem("acc_added"), NBLK * (s.n - 1))
                sp.dma_start(w_tok[s.par][:, :],
                             wte_dram[ds(s.n, 1), :].rearrange("o n -> (o n)").partition_broadcast(P))\
                  .then_inc(sem(f"wtok_landed{s.par}"), 16)

            for k in range(NBLK):
                cs = slice(k * BLK, (k + 1) * BLK)
                sp.wait_ge(sem("wte_turned"), k + 1)
                sp.dma_start(wte_dram[:, cs], wte_t[:, cs]).then_inc(sem("wte_stored"), 16)
                sp.wait_ge(sem("wte_stored"), 16 * (k + 1))
                sp.dma_start(w_tok[0][:, cs], wte_dram[0, cs].partition_broadcast(P))\
                  .then_inc(sem(f"wtok_first{k}"), 16)
            load_token_weights(Step(0, 1, EXPERTS))
            with sp.Fori(0, (EXPERTS - 2) // 2) as it:
                for u in range(2):
                    load_expert(Step(it, 2 + u, EXPERTS))
                    load_token_weights(Step(it, 2 + u, EXPERTS))
            for k in range(NBLK):
                sp.wait_ge(sem("x_final"), k + 1)
                sp.dma_start(out_tiles[:, BT * k:BT * k + BT, :], x3d[:, BT * k:BT * k + BT, :])\
                  .then_inc(sem("stored"), 16)
            sp.wait_ge(sem("stored"), 16 * NBLK)

        @block.gpsimd
        def _(pool):
            pool.memset(ident[:, :], 0.0).then_inc(sem("p_zero"), 1)
            pool.memset(causal[:, :], 0.0).then_inc(sem("p_zero"), 1)
            pool.memset(half_neg[:, :], -0.5).then_inc(sem("p_zero"), 1)
            pool.memset(eps[:, :], EPS).then_inc(sem("p_zero"), 1)
            pool.wait_ge(sem("p_zero"), 4)
            pool.affine_select(out=ident[:, :], in_=ident[:, :], compare_op=ALU.not_equal, fill=1.0,
                               base=0, pattern=[[-1, P]], channel_multiplier=1).then_inc(sem("ident_set"), 1)
            for c0 in (0, 256):
                pool.affine_select(out=causal[:, c0:c0 + P], in_=causal[:, c0:c0 + P], compare_op=ALU.is_ge,
                                   fill=MASKED, base=0, pattern=[[-1, P]], channel_multiplier=1)\
                    .then_inc(sem("consts_set"), 1)
            pool.memset(wq_in[:, :, :], 1.0).then_inc(sem("wq_in_set"), 1)
            pool.memset(magic[:, :], MAGIC).then_inc(sem("consts_set"), 1)
            pool.memset(ones[:, :], 1.0).then_inc(sem("consts_set"), 1)

            def rstd_of(n, mean_var, eps_sum, out, tiles):
                pool.wait_ge(sem("var_done"), n)
                pool.tensor_tensor(eps_sum[:, 0:tiles], mean_var[:, 0:tiles, 1], eps[:, 0:tiles], ALU.add)\
                    .then_inc(sem("eps_added"), 1)
                pool.wait_ge(sem("eps_added"), n)
                pool.tensor_tensor(out[:, 0:tiles], eps_sum[:, 0:tiles], half_neg[:, 0:tiles], ALU.pow)\
                    .then_inc(sem("rstd_done"), 1)

            def rstd_loop(base, tiles, count):
                with pool.Fori(0, count // 2) as it:
                    for u in range(2):
                        rstd_of(2 * it + (base + u + 1), mv[u], var_eps[u], rstd[u], tiles)

            for k in range(TILES // BT):
                rstd_of(LN1 + k + 1, mv1[:, BT * k:BT * k + BT, :], var_eps[k % 2], rstd1[:, BT * k:BT * k + BT], BT)
            pool.memset(we_pad[:, :, :], 0.0).then_inc(sem("we_pad_set"), 1)
            pool.wait_ge(sem("w_inv_set"), 1)
            for k in range(2 * CH):
                pool.tensor_scalar(w_tmp[:, k * DM:(k + 1) * DM], wq_in[:, k, :], w_inv[:, k:k + 1], MAGIC,
                                   ALU.mult, ALU.add).then_inc(sem("p_w"), 1)
            pool.tensor_scalar(wd_tmp[:, :], wd_in[:, :], w_inv[:, 6:7], MAGIC, ALU.mult, ALU.add)\
                .then_inc(sem("p_w"), 1)
            pool.wait_ge(sem("p_w"), 7)
            pool.tensor_scalar(w_tmp[:, :], w_tmp[:, :], MAGIC + QMAX, MAGIC - QMAX - 1.0, ALU.min, ALU.max)\
                .then_inc(sem("p_w"), 1)
            pool.tensor_scalar(wd_tmp[:, :], wd_tmp[:, :], MAGIC + QMAX, MAGIC - QMAX - 1.0, ALU.min, ALU.max)\
                .then_inc(sem("p_w"), 1)
            pool.wait_ge(sem("p_w"), 9)
            pool.tensor_scalar(w_q8[:, :, :].rearrange("p c n -> p (c n)"), w_tmp[:, :], -MAGIC, 1.0,
                               ALU.add, ALU.mult).then_inc(sem("w_rounded"), 1)
            pool.tensor_scalar(wd_q8[:, :], wd_tmp[:, :], -MAGIC, 1.0, ALU.add, ALU.mult)\
                .then_inc(sem("w_rounded"), 1)

            rstd_loop(LN2, 2, BATCH)
            pool.wait_ge(sem("amax0_done"), 1)
            pool.partition_all_reduce(amax0[:, 9:10], amax0[:, 8:9], P, bass.bass_isa.ReduceOp.max)\
                .then_inc(sem("gmax0"), 1)
            pool.wait_ge(sem("k_split"), 2 * BATCH)
            slot_keys(pool, 2)
            pool.wait_ge(sem("amax1_done"), 1)
            na = CH * NBLK
            pool.partition_all_reduce(amax1[:, na + 1:na + 2], amax1[:, na:na + 1], P, bass.bass_isa.ReduceOp.max)\
                .then_inc(sem("gmax1"), 1)
            def add_down(k):
                pool.wait_ge(sem("down_scaled"), k + 1)
                xb = x[:, k * BLK:(k + 1) * BLK]
                pool.tensor_tensor(xb, down[k % 2][:, :], xb, ALU.add).then_inc(sem("x2_done"), 1)

            add_down(0)
            for k in range(NBLK):
                if k + 1 < NBLK:
                    add_down(k + 1)
                rstd_of(LN3 + k + 1, mv[k % 2], var_eps[k % 2], rstd[k % 2], BT)
            pool.wait_ge(sem("q_split"), 2 * NBLK)
            for i in range(2):
                pool.memset(v_st[i][:, :, :], 0.0).then_inc(sem("v_zero"), 1)
                pool.wait_ge(sem("v_zero"), i + 1)
                v4 = v_st[i][:, :, :].rearrange("p i (w r c) -> p i w r c", r=2, c=32)
                pool.memset(v4[:, :, :, 0, 8:16], 1.0).then_inc(sem("v_ones"), 1)
                pool.memset(v4[:, :, :, 1, 24:32], 1.0).then_inc(sem("v_ones"), 1)

            v1f = v1[:, :, :].rearrange("p i n -> p (i n)")

            def widen_v(s):
                wait(pool, sem("attended"), 4 * s.n - 4)
                for i in range(2):
                    for r in range(2):
                        def heads(tile):
                            return tile.rearrange("p (u r j e) -> p r u j e", u=2, r=2, e=HD)[:, r]
                        dst = v_st[s.par][:, i, :].rearrange("p (u j c) -> p u j c", u=2, c=64)
                        pool.tensor_tensor(dst[:, :, :, 48 * r:48 * r + 8],
                                           heads(v1f[:, ds(s.n * SEQ + i * P, P)]), heads(bv1[:, :]), ALU.add)\
                            .then_inc(sem("v_widened"), 1)

            def fourth_norm(b):
                rstd_of(b.n + (LN4 + 1), mv[b.par], var_eps[b.par], rstd[b.par], 2)
                full = [P, 2, P]
                xn = xn4[:, :].rearrange("p (i c) -> p i c", i=2)
                pool.tensor_tensor(xn, x[:, ds(b.n * SEQ, SEQ)].rearrange("p (i c) -> p i c", i=2),
                                   mv[b.par][:, 0:2, 0].unsqueeze(2).broadcast_to(full), ALU.subtract)\
                    .then_inc(sem("xn4_centred"), 1)
                pool.wait_ge(sem("xn4_centred"), b.n + 1)
                pool.wait_ge(sem("rstd_done"), b.n + (LN4 + 1))
                pool.tensor_tensor(xn, xn, rstd[b.par][:, 0:2].unsqueeze(2).broadcast_to(full), ALU.mult)\
                    .then_inc(sem("xn4_ready"), 1)

            pool.wait_ge(sem("bv1_landed"), 16)
            pool.wait_ge(sem("v_ones"), 4)
            widen_v(Step(0, 0, BATCH))
            widen_v(Step(0, 1, BATCH))
            with pool.Fori(0, (BATCH - 2) // 2) as it:
                for u in range(2):
                    widen_v(Step(it, 2 + u, BATCH))
                    fourth_norm(Step(it, u, BATCH))
            fourth_norm(Step(0, BATCH - 2, BATCH))
            pool.wait_ge(sem("attended"), 4 * BATCH)
            pool.iota(eidx[:, :], pattern=[[1, EXPERTS]], base=0, channel_multiplier=0,
                      allow_small_or_imprecise_dtypes=True).then_inc(sem("moe_set"), 1)
            pool.memset(acc[:, :], 0.0).then_inc(sem("moe_set"), 1)
            pool.memset(euler[:, :], EULER).then_inc(sem("moe_set"), 1)
            fourth_norm(Step(0, BATCH - 1, BATCH))

            def low_parts(s, blocks=range(NBLK)):
                for k in blocks:
                    y = NBLK * s.n + k
                    wait(pool, sem("y_done"), y - 1)
                    for ch in POOL_CH:
                        pool.wait_ge(sem("hid_hi_done"), HC * y + ch + 1)
                        pool.tensor_tensor(hid_lo[k % 2][:, ch, :], hid[k % 2][:, ch, :],
                                           hid_hi[k % 2][:, ch, :].bitcast(F32), ALU.subtract)\
                            .then_inc(sem("pool_low"), 1)

            first = Step(0, 0, EXPERTS)
            low_parts(first, range(2))
            pool.wait_ge(sem("moe_set"), 3)
            pool.wait_ge(sem("top_gap"), 1)
            pool.tensor_tensor(soft[:, 1, :], euler[:, :], soft[:, 0, :], ALU.pow).then_inc(sem("top_exp"), 1)
            low_parts(first, range(2, NBLK))
            over_experts(pool, lambda s: None if is_step(s, 0) else low_parts(s))

        @block.scalar
        def _(act):
            for dst, src in ((wq0, "L0_xattn_WQ"), (wk0, "L0_xattn_WK"), (wv0, "L0_xattn_WV"),
                             (wv1, "L1_xattn_Wv"), (wk1, "L1_xattn_Wk")):
                act.dma_start(dst[:, :], t[src]).then_inc(sem("wa_landed"), 16)

            def step_a(s):
                m, b, o = s + 1, s + (-1), s + (-2)
                if b.valid:
                    act.wait_ge(sem("probs0_turned"), b.n + 1)
                    wait(act, sem("attended0"), b.n - 1)
                    act.activation(probs0_t[b.par][:, :], bank[5][:, 0:384], ACT.Copy)\
                       .then_inc(sem("probs0_t_ready"), 1)
                if m.valid:
                    act.wait_ge(sem("cx_turned"), m.n + 1)
                    wait(act, sem("k1_projected"), m.n - 1)
                    act.activation(cx_t[m.par][:, :], bank[0][:, :], ACT.Copy).then_inc(sem("cx_ready"), 1)
                if s.valid:
                    act.wait_ge(sem("nmax0_done"), s.n + 1)
                    wait(act, sem("probs0_turned"), s.n - 1)
                    act.activation(probs0[s.par][:, 0:128], scores0[s.par][:, 0:128], ACT.Exp,
                                   bias=nmax0[s.par][:, 0:1], accum_out=rsum0[s.par][:, 0:1])
                    act.activation(probs0[s.par][:, 128:384], scores0[s.par][:, 128:384], ACT.Exp,
                                   bias=nmax0[s.par][:, 1:2], accum_out=rsum0[s.par][:, 1:2])\
                       .then_inc(sem("probs0_done"), 1)
                if m.valid:
                    act.wait_ge(sem("qk0_projected"), m.n + 1)
                    wait(act, sem("scored"), m.n - 1)
                    act.activation(qk0[m.par][:, :], bank[1][:, :], ACT.Copy).then_inc(sem("qk0_ready"), 1)
                if m.valid:
                    act.wait_ge(sem("v_projected"), m.n + 1)
                    wait(act, sem("attended0"), m.n - 1)
                    act.activation(v0[m.par][:, :], bank[2][:, 0:256], ACT.Copy).then_inc(sem("v0_ready"), 1)
                if o.valid:
                    act.wait_ge(sem("xn2_turned"), o.n + 1)
                    act.activation(xn2_t[:, ds(o.n * SEQ, SEQ)], bank[7][:, 0:256], ACT.Copy)\
                       .then_inc(sem("xn2_t_ready"), 1)
                if m.valid:
                    if isinstance(s.it, int) and s.n == -1:
                        act.wait_ge(sem("cols_set"), 1)
                    act.wait_ge(sem("k1_projected"), m.n + 1)
                    act.activation(k_hi[:, ds(m.n * SEQ, SEQ)], bank[3][:, 0:256], ACT.Identity,
                                   bias=cols[:, BKC:BKC + 1]).then_inc(sem("k_hi_done"), 1)
                if isinstance(s.it, int) and s.n == -1:
                    act.wait_ge(sem("g_landed"), 64)
                    act.activation(tg[:, :], g_in[:, :], ACT.Tanh).then_inc(sem("tg_set"), 1)
                    act.activation(sig[:, :], clip[:, :], ACT.Exp, scale=-1.0).then_inc(sem("sig_exp"), 1)

            skewed(act, step_a, BATCH, lag=2)

            act.wait_ge(sem("consts_set"), 3)
            act.activation(silu_first[:, :], magic[:, :], ACT.Silu)
            act.wait_ge(sem("ffn_w_turned"), 2)
            act.wait_ge(sem("xn2_t_ready"), BATCH)
            act.wait_ge(sem("x_inv"), 1)
            for k in range(NBLK):
                xb = xn2_t[:, k * BLK:(k + 1) * BLK]
                act.activation(xb, xb, ACT.Identity, bias=magic[:, 0:1], scale=smalls[:, 1:2])\
                   .then_inc(sem("x_scaled"), 1)

            def silu_block(s):
                for ch in range(CH):
                    w = CHW[ch]
                    k = CH * s.n + ch
                    act.wait_ge(sem("gated"), k + 1)
                    wait(act, sem("h_done"), k - 1)
                    par = (CH * s.c + ch) % 2
                    act.activation(silu[par][0:w, :], bank[2 * ch][0:w, :], ACT.Silu,
                                   scale=gu_scale[0:w, ch:ch + 1]).then_inc(sem("silued"), 1)

            def both_silu(s0, s1):
                silu_block(s0)
                silu_block(s1)

            act.wait_ge(sem("gu_scaled"), 1)
            paired(act, both_silu, NBLK)
            act.wait_ge(sem("h_inv"), 1)
            for k in range(NBLK):
                for ch in range(CH):
                    w, c0 = CHW[ch], (CH * k + ch) * BLK
                    act.activation(h[0:w, c0:c0 + BLK], h[0:w, c0:c0 + BLK], ACT.Identity,
                                   bias=magic[0:w, 0:1], scale=smalls[0:w, 3:4]).then_inc(sem("h_scaled"), 1)

            def set_k_quad(i):
                for j in range(QUADS):
                    act.activation(k_quad[i][:, j, :, :].rearrange("p g s -> p (g s)"),
                                   in_quad[:, j:j + 1].broadcast_to([P, GROUPS * SEQ]), ACT.Copy)\
                       .then_inc(sem("k_quad_set"), 1)

            wait_slots(act)
            act.wait_ge(sem("v_const"), 1)
            set_k_quad(0)
            for k in range(NBLK):
                act.wait_ge(sem("xn3_turned"), k + 1)
                if k >= 2:
                    act.wait_ge(sem("q_projected"), k - 1)
                act.activation(xn3_t[k % 2][:, :], bank[2 + k % 2][:, :], ACT.Copy).then_inc(sem("xn3_t_ready"), 1)
                act.wait_ge(sem("q_projected"), k + 1)
                act.activation(q_hi[:, k * BLK:(k + 1) * BLK], bank[4 + k % 2][:, :], ACT.Identity,
                               bias=cols[:, BQC:BQC + 1]).then_inc(sem("q_hi_done"), 1)

            def step_c(s):
                m, o = s + 1, s + (-1)

                def take_q(b, u):
                    act.wait_ge(sem("q_slotted"), 2 * b.n + u + 1)
                    wait(act, sem("st_done"), 16 * (b.n - 2) + 8 * (u + 1))
                    act.activation(q_st[b.par][:, 2 * u:2 * u + 2, :], bank[5][:, :]
                                   .rearrange("p (g s) -> p g s", g=2), ACT.Copy).then_inc(sem("q_staged"), 1)

                for k in range(C_SLOTS):
                    if o.valid and k == 0:
                        act.wait_ge(sem("attended"), 4 * o.n + 4)
                        wait(act, sem("on_ready"), o.n)
                        act.activation(av[:, :], bank[4][:, :], ACT.Copy).then_inc(sem("av_ready"), 1)
                    if is_step(s, -1) and k == 1:
                        take_q(m, 0)
                    if o.valid and k == 3:
                        act.wait_ge(sem("sums_inverted"), o.n + 1)
                        act.activation(inv_wide[:, :, :, :].rearrange("p t u (w c) -> p (t u w) c", c=16),
                                       sums_inv[:, :, :, :].rearrange("p t u w -> p (t u w)").unsqueeze(2)
                                       .broadcast_to([P, 32, 16]), ACT.Copy).then_inc(sem("inv_widened"), 1)
                    if is_step(s, BATCH) and k == 2:
                        take_gates(0)
                    if is_step(s, BATCH) and k == 2:
                        take_gates(1)
                        take_gates(2)
                    if m.valid and k == 5:
                        take_q(m, 1)
                        if is_step(s, -1):
                            set_k_quad(1)
                            act.activation(exp_first[:, :], eps[:, 0:1], ACT.Exp)
                    if is_step(s, BATCH) and k == 12:
                        gelu_block(Step(0, 0, EXPERTS), 0)
                    if o.valid and k == 16:
                        act.wait_ge(sem("xn4_turned"), o.n + 1)
                        act.activation(xt_hi[:, ds(o.n * SEQ, SEQ)], bank[7][:, 0:256], ACT.Copy)\
                           .then_inc(sem("xt_hi_done"), 1)
                    if (s + 2).valid and k == 16:
                        take_q(s + 2, 0)
                    if s.valid and k < 16:
                        quad, j = k // 4, k % 4
                        if j == 0:
                            wait(act, sem("attended"), 4 * s.n + quad - 1)
                        act.wait_ge(sem("st_done"), 16 * s.n + k + 1)
                        act.activation(probs[quad % 2][:, j, :, :], bank[2 + j % 2][:, :]
                                       .rearrange("p (r s) -> p r s", r=2), ACT.Exp, scale=SC1)\
                           .then_inc(sem("exped"), 1)

            def take_gates(k):
                act.wait_ge(sem("gates_done"), k + 1)
                act.activation(gates_t[:, k * BLK:(k + 1) * BLK], bank[GATE_BANKS[k]][0:EXPERTS, :], ACT.Identity,
                               bias=gate_b[:, 0:1]).then_inc(sem("gates_t_ready"), 1)

            def gelu_block(s, k):
                y = NBLK * s.n + k
                for ch in range(HC):
                    act.wait_ge(sem("hid_done"), HC * y + ch + 1)
                    if ch in POOL_CH:
                        wait(act, sem("pool_low"), len(POOL_CH) * (y - 1))
                    else:
                        wait(act, sem("dve_low"), (HC - len(POOL_CH)) * (y - 1))
                    act.activation(hid[k % 2][:, ch, :], bank[ch][:, :], ACT.Gelu,
                                   bias=b1_cols[s.par][:, ch:ch + 1]).then_inc(sem("gelued"), 1)

            skewed(act, step_c, BATCH, lead=2)
            take_gates(3)


            def gelus(s):
                for k in range(1 if is_step(s, 0) else 0, NBLK):
                    if is_step(s, 0) and k == 3:
                        act.wait_ge(sem("wte_turning"), 1)
                        for i in range(NBLK):
                            act.activation(wte_t[:, i * BLK:(i + 1) * BLK], bank[7][32 * i:32 * i + EXPERTS, :],
                                           ACT.Copy).then_inc(sem("wte_turned"), 1)
                    gelu_block(s, k)

            over_experts(act, gelus)

        @block.vector
        def _(dve):
            dve.memset(rows[:, :], 0.0).then_inc(sem("v_zeroed"), 1)
            def first_norm(k):
                dve.wait_ge(sem(f"x_landed{k}"), 16)
                for i in range(BT):
                    ins = dve.bn_stats(stats[k % 2][:, i, :], x3d[:, BT * k + i, :])
                ins.then_inc(sem("halves_done"), 1)
                dve.wait_ge(sem("halves_done"), k + 1)
                for i in range(BT):
                    ins = dve.bn_aggr(mv1[:, BT * k + i, :], stats[k % 2][:, i, :])
                ins.then_inc(sem("var_done"), 1)

            def set_constants():
                for i in range(2):
                    dve.memset(neg_max_pad[i][:, :, :, :, :].bitcast(F32), 0.0).then_inc(sem("v_pad"), 1)
                for n in ("qhi", "qlo"):
                    dve.memset(sel[n][:, :, :].bitcast(F32), 0.0).then_inc(sem("v_pad"), 1)
                dve.wait_ge(sem("ident_set"), 1)
                dve.wait_ge(sem("v_pad"), 4)
                dve.tensor_reduce(in_quad[:, :], ident[:, :].rearrange("p (j c) -> p j c", j=QUADS), AX.X, ALU.max)\
                   .then_inc(sem("v_const"), 1)
                dve.tensor_copy(ident_b[:, :], ident[:, :]).then_inc(sem("v_const"), 1)
                dve.tensor_copy(ident_r[:, :], ident[:, :]).then_inc(sem("v_const"), 1)
                iv = ident[:, :].rearrange("p (g j e) -> p g j e", g=GROUPS, e=HD)
                for n, slots in (("qhi", Q_HI), ("qlo", Q_LO)):
                    for s in slots:
                        dve.tensor_copy(sel[n][:, :, :].rearrange("p g (j s e) -> p g j s e", j=QUADS, s=4)
                                        [:, :, :, s, :], iv).then_inc(sem("v_const"), 1)

            def ffn_scales():
                dve.wait_ge(sem("sig_exp"), 1)
                dve.tensor_scalar(sig[:, :], sig[:, :], 1.0, QMAX, ALU.add, ALU.mult).then_inc(sem("v_sig"), 1)
                dve.wait_ge(sem("v_sig"), 1)
                dve.reciprocal(sig[:, :], sig[:, :]).then_inc(sem("v_sig"), 1)
                dve.wait_ge(sem("wffn_landed"), 80)
                dve.tensor_reduce(w_amax[:, 0:6], wq_in[:, :, :], AX.X, ALU.max, apply_absolute_value=True)\
                   .then_inc(sem("v_w"), 1)
                dve.tensor_reduce(w_amax[:, 6:7], wd_in[:, :], AX.X, ALU.max, apply_absolute_value=True)\
                   .then_inc(sem("v_w"), 1)
                dve.wait_ge(sem("v_w"), 2)
                dve.tensor_scalar(w_scale[:, 0:7], w_amax[:, 0:7], 1.0 / QMAX, None, ALU.mult).then_inc(sem("v_w"), 1)
                dve.wait_ge(sem("v_w"), 3)
                dve.reciprocal(w_inv[:, 0:7], w_scale[:, 0:7]).then_inc(sem("w_inv_set"), 1)
                dve.tensor_scalar(sd_row[:, :], ident[:, :], w_scale[:, 6:7], None, ALU.mult)\
                   .then_inc(sem("sd_diag"), 1)

            def norm(out, src, par, i):
                return dve.tensor_scalar(out, src, mv[par][:, i, 0:1], rstd[par][:, i:i + 1], ALU.subtract, ALU.mult)

            def halves_of(par, tiles, column0):
                dve.memset(wait_taker[:, par:par + 1], 0.0)
                for i in range(tiles):
                    ins = dve.bn_stats(stats[par][:, i, :], x[:, ds(column0 + i * P, P)])
                ins.then_inc(sem("halves_done"), 1)

            def variances_of(n, par, tiles):
                dve.wait_ge(sem("halves_done"), n)
                dve.memset(wait_taker[:, 2 + par:3 + par], 0.0)
                for i in range(tiles):
                    ins = dve.bn_aggr(mv[par][:, i, :], stats[par][:, i, :])
                ins.then_inc(sem("var_done"), 1)

            def step_a(s):
                m, b, o = s + 1, s + (-1), s + (-2)
                start = isinstance(s.it, int) and s.n == -1
                if m.valid:
                    dve.wait_ge(sem("rstd_done"), LN1 + (1 if start else 4))
                    wait(dve, sem("cx_turned"), m.n - 1)
                    mv1f = mv1[:, :, :].rearrange("p i c -> p (i c)")
                    for i in range(2):
                        ins = dve.tensor_scalar(xn1[m.par][:, i, :], x[:, ds(m.n * SEQ + i * P, P)],
                                                mv1f[:, ds(4 * m.n + 2 * i, 1)], rstd1[:, ds(2 * m.n + i, 1)],
                                                ALU.subtract, ALU.mult)
                    ins.then_inc(sem("xn1_ready"), 1)
                if start:
                    for k in range(1, 4):
                        first_norm(k)
                    dve.wait_ge(sem("cols_turned"), 1)
                    dve.tensor_copy(cols[:, :], bank[6][:, 0:64]).then_inc(sem("cols_set"), 1)
                if s.valid:
                    dve.wait_ge(sem("consts_set"), 2)
                    dve.wait_ge(sem("scored"), s.n + 1)
                    wait(dve, sem("probs0_done"), s.n - 1)
                    dve.scalar_tensor_tensor(scores0[s.par][:, :], bank[4][:, 0:384], SC0, causal[:, :],
                                             ALU.mult, ALU.add).then_inc(sem("masked"), 1)
                if b.valid:
                    dve.wait_ge(sem("probs0_done"), b.n + 1)
                    dve.reciprocal(rinv0[b.par][:, 0:2], rsum0[b.par][:, :]).then_inc(sem("rinv0_done"), 1)
                if o.valid:
                    dve.wait_ge(sem("rstd_done"), o.n + (LN2 + 1))
                    wait(dve, sem("xn2_turned"), o.n)
                    for i in range(2):
                        ins = norm(xn2[o.par][:, i * P:(i + 1) * P], x[:, ds(o.n * SEQ + i * P, P)], o.par, i)
                    ins.then_inc(sem("xn2_ready"), 1)
                if s.valid:
                    dve.wait_ge(sem("masked"), s.n + 1)
                    dve.tensor_reduce(nmax0[s.par][:, 0:1], scores0[s.par][:, 0:128], AX.X, ALU.max, negate=True)
                    dve.tensor_reduce(nmax0[s.par][:, 1:2], scores0[s.par][:, 128:384], AX.X, ALU.max, negate=True)\
                       .then_inc(sem("nmax0_done"), 1)
                if o.valid:
                    dve.wait_ge(sem("xn2_ready"), o.n + 1)
                    dve.tensor_reduce(amax0[:, ds(o.n, 1)], xn2[o.par][:, :], AX.X, ALU.max,
                                      apply_absolute_value=True).then_inc(sem("amax0_part"), 1)
                if b.valid:
                    dve.wait_ge(sem("rinv0_done"), 2 * b.n + 1)
                    dve.tensor_scalar(rinv0[b.par][:, 2:4], rinv0[b.par][:, 0:2], tg[:, 0:1], None, ALU.mult)\
                       .then_inc(sem("rinv0_done"), 1)
                    dve.wait_ge(sem("rinv0_done"), 2 * b.n + 2)
                    dve.wait_ge(sem("attended0"), b.n + 1)
                    for i in range(2):
                        ins = dve.scalar_tensor_tensor(x[:, ds(b.n * SEQ + i * P, P)], bank[6][:, i * P:(i + 1) * P],
                                                       rinv0[b.par][:, 2 + i:3 + i], x[:, ds(b.n * SEQ + i * P, P)],
                                                       ALU.mult, ALU.add)
                    ins.then_inc(sem("x1_done"), 1)
                    dve.wait_ge(sem("x1_done"), b.n + 1)
                    halves_of(b.par, 2, b.n * SEQ)
                if m.valid:
                    dve.wait_ge(sem("v0_ready"), m.n + 1)
                    dve.tensor_copy(v1[:, :, :].rearrange("p i n -> p (i n)")[:, ds(m.n * SEQ, SEQ)],
                                    bank[2][:, 256:512]).then_inc(sem("v1_ready"), 1)
                if b.valid:
                    variances_of(b.n + (LN2 + 1), b.par, 2)
                if m.valid:
                    dve.wait_ge(sem("k_hi_done"), m.n + 1)
                    dve.scalar_tensor_tensor(k_lo[:, ds(m.n * SEQ, SEQ)], bank[3][:, 0:256], cols[:, BKC:BKC + 1],
                                             k_hi[:, ds(m.n * SEQ, SEQ)].bitcast(F32), ALU.add, ALU.subtract)\
                       .then_inc(sem("k_split"), 2)
                if start:
                    set_constants()
                    ffn_scales()
                    dve.wait_ge(sem("tg_set"), 1)

            dve.memset(amax1[:, :], 0.0).then_inc(sem("v_zeroed"), 1)
            first_norm(0)
            skewed(dve, step_a, BATCH, lag=2)

            dve.wait_ge(sem("ffn_w_turned"), 1)
            dve.tensor_copy(wgu_t[:, :, :].rearrange("p c n -> p (c n)"), bank[0][:, :].bitcast(BF16)[:, 0:2 * CH * P])\
               .then_inc(sem("ffn_w_ready"), 1)
            dve.wait_ge(sem("ffn_w_turned"), 2)
            wd_ps = bank[1][:, :].bitcast(BF16)
            dve.tensor_copy(wd_t[:, 0:2, :].rearrange("p c n -> p (c n)"), wd_ps[:, 0:2 * P]).then_inc(sem("ffn_w_ready"), 1)
            dve.tensor_copy(wd_t[0:CHW[2], 2, :], wd_ps[0:CHW[2], 2 * P:3 * P]).then_inc(sem("ffn_w_ready"), 1)
            dve.wait_ge(sem("xn2_t_ready"), BATCH)
            dve.wait_ge(sem("amax0_part"), BATCH)
            dve.tensor_reduce(amax0[:, 8:9], amax0[:, 0:8], AX.X, ALU.max).then_inc(sem("amax0_done"), 1)
            dve.wait_ge(sem("v_sig"), 2)
            dve.wait_ge(sem("gmax0"), 1)
            dve.tensor_scalar(smalls[:, 0:1], amax0[:, 9:10], sig[:, 0:1], None, ALU.mult).then_inc(sem("v_sig"), 1)
            dve.wait_ge(sem("v_sig"), 3)
            dve.reciprocal(smalls[:, 1:2], smalls[:, 0:1]).then_inc(sem("x_inv"), 1)
            dve.tensor_scalar(gu_scale[:, :], w_scale[:, 0:6], smalls[:, 0:1], None, ALU.mult)\
               .then_inc(sem("gu_scaled"), 1)
            for k in range(NBLK):
                xb = xn2_t[:, k * BLK:(k + 1) * BLK]
                dve.wait_ge(sem("x_scaled"), k + 1)
                dve.tensor_scalar(xb, xb, MAGIC + QMAX, MAGIC - QMAX - 1.0, ALU.min, ALU.max)\
                   .then_inc(sem("x_clipped"), 1)
                dve.wait_ge(sem("x_clipped"), k + 1)
                dve.tensor_scalar(xq[:, k * BLK:(k + 1) * BLK], xb, MAGIC, None, ALU.subtract)\
                   .then_inc(sem("x_rounded"), 1)

            def largest(n, ch):
                dve.wait_ge(sem("h_done"), CH * n + ch + 1)
                dve.tensor_reduce(amax1[0:CHW[ch], ds(CH * n + ch, 1)], h[0:CHW[ch], ds((CH * n + ch) * BLK, BLK)],
                                  AX.X, ALU.max, apply_absolute_value=True).then_inc(sem("amax1_part"), 1)

            def products(s0, s1):
                before = None
                for s in (s0, s1):
                    for ch in range(CH):
                        w = CHW[ch]
                        k = CH * s.n + ch
                        par = (CH * s.c + ch) % 2
                        dve.wait_ge(sem("upped"), k + 1)
                        dve.wait_ge(sem("silued"), k + 1)
                        dve.scalar_tensor_tensor(h[0:w, ds(k * BLK, BLK)], bank[2 * ch + 1][0:w, :],
                                                 gu_scale[0:w, CH + ch:CH + ch + 1], silu[par][0:w, :],
                                                 ALU.mult, ALU.mult).then_inc(sem("h_done"), 1)
                        if before:
                            largest(*before)
                        before = (s.n, ch)
                largest(*before)

            dve.wait_ge(sem("v_zeroed"), 2)
            dve.wait_ge(sem("gu_scaled"), 1)
            paired(dve, products, NBLK)
            na = CH * NBLK
            dve.wait_ge(sem("amax1_part"), na)
            dve.tensor_reduce(amax1[:, na:na + 1], amax1[:, 0:na], AX.X, ALU.max).then_inc(sem("amax1_done"), 1)
            dve.wait_ge(sem("gmax1"), 1)
            dve.tensor_scalar(smalls[:, 2:3], amax1[:, na + 1:na + 2], sig[:, 1:2], None, ALU.mult)\
               .then_inc(sem("v_sig"), 1)
            dve.wait_ge(sem("v_sig"), 4)
            dve.reciprocal(smalls[:, 3:4], smalls[:, 2:3]).then_inc(sem("h_inv"), 1)
            dve.tensor_scalar(smalls[:, 4:5], smalls[:, 2:3], tg[:, 2:3], None, ALU.mult).then_inc(sem("v_sig"), 1)
            dve.wait_ge(sem("v_sig"), 5)
            dve.wait_ge(sem("sd_spread"), 1)
            dve.tensor_scalar(sd_all[:, :], bank[7][:, 0:DM], smalls[:, 4:5], None, ALU.mult).then_inc(sem("sd_set"), 1)

            def round_h(k):
                def clip(ch):
                    w, c0 = CHW[ch], (CH * k + ch) * BLK
                    dve.wait_ge(sem("h_scaled"), CH * k + ch + 1)
                    dve.tensor_scalar(h[0:w, c0:c0 + BLK], h[0:w, c0:c0 + BLK], MAGIC + QMAX, MAGIC - QMAX - 1.0,
                                      ALU.min, ALU.max).then_inc(sem("h_clipped"), 1)

                def less_magic(ch):
                    w, c0 = CHW[ch], (CH * k + ch) * BLK
                    dve.wait_ge(sem("h_clipped"), CH * k + ch + 1)
                    dve.tensor_scalar(hq[k % 2][0:w, ch, :], h[0:w, c0:c0 + BLK], MAGIC, None, ALU.subtract)\
                       .then_inc(sem("h_rounded"), 1)

                if k >= 2:
                    dve.wait_ge(sem("downed"), k - 1)
                clip(0)
                for ch in range(CH):
                    if ch + 1 < CH:
                        clip(ch + 1)
                    less_magic(ch)

            def scale_down(k):
                dve.wait_ge(sem("downed"), k + 1)
                if k == 0:
                    dve.wait_ge(sem("sd_set"), 1)
                else:
                    wait(dve, sem("x2_done"), k - 1)
                dve.tensor_tensor(down[k % 2][:, :].rearrange("p (i d) -> p i d", d=DM),
                                  bank[k % 2][:, :].rearrange("p (i d) -> p i d", d=DM),
                                  sd_all[:, :].unsqueeze(1).broadcast_to([P, BT, DM]), ALU.mult)\
                   .then_inc(sem("down_scaled"), 1)

            def third_stats(k):
                dve.wait_ge(sem("x2_done"), k + 1)
                if k >= 2:
                    dve.wait_ge(sem("xn3_ready"), k - 1)
                for i in range(BT):
                    ins = dve.bn_stats(stats[k % 2][:, i, :], x[:, k * BLK + i * P:k * BLK + (i + 1) * P])
                ins.then_inc(sem("halves_done"), 1)
                dve.wait_ge(sem("halves_done"), LN3 + k + 1)
                for i in range(BT):
                    ins = dve.bn_aggr(mv[k % 2][:, i, :], stats[k % 2][:, i, :])
                ins.then_inc(sem("var_done"), 1)

            def q_low(k):
                dve.wait_ge(sem("q_hi_done"), k + 1)
                cs = slice(k * BLK, (k + 1) * BLK)
                dve.scalar_tensor_tensor(q_lo[:, cs], bank[4 + k % 2][:, :], cols[:, BQC:BQC + 1],
                                         q_hi[:, cs].bitcast(F32), ALU.add, ALU.subtract).then_inc(sem("q_split"), 2)

            def third_norm(k):
                dve.wait_ge(sem("rstd_done"), LN3 + k + 1)
                if k >= 2:
                    dve.wait_ge(sem("xn3_turned"), k - 1)
                for i in range(BT):
                    ins = norm(xn3[k % 2][:, i * P:(i + 1) * P], x[:, k * BLK + i * P:k * BLK + (i + 1) * P], k % 2, i)
                ins.then_inc(sem("xn3_ready"), 1)

            def cut_expert(s):
                dve.wait_ge(sem(f"we_landed{s.par}"), 32 * (s.half + 1))
                wait(dve, sem("y_done"), NBLK * (s.n - 1))
                dve.tensor_copy(b1_cols[s.par][:, :], cols[:, ds(HC * s.n, HC)])
                for k, (w_in, hi, lo) in enumerate((
                        (w1_in[s.par][:, :], w1_hi[s.par][:, :], w1_lo[s.par][:, :]),
                        (w2_in[s.par][:, :, :], w2_hi[s.par][:, :, :], w2_lo[s.par][:, :, :]))):
                    dve.tensor_copy(hi, w_in).then_inc(sem("w_cut"), 1)
                    dve.wait_ge(sem("w_cut"), 4 * s.n + 2 * k + 1)
                    dve.tensor_tensor(lo, w_in, hi.bitcast(F32), ALU.subtract).then_inc(sem("w_cut"), 1)

            dve.wait_ge(sem("wc_landed"), 16 * (3 + 2 * QUADS + 1))
            dve.tensor_copy(gate_hi[:, :], gate_w[:, :]).then_inc(sem("gw_split"), 1)
            dve.wait_ge(sem("gw_split"), 1)
            dve.tensor_tensor(gate_lo[:, :], gate_w[:, :], gate_hi[:, :].bitcast(F32), ALU.subtract)\
               .then_inc(sem("gw_split"), 1)

            round_h(0)
            round_h(1)
            scale_down(0)
            round_h(2)
            scale_down(1)
            third_stats(0)
            round_h(3)
            third_norm(0)
            scale_down(2)
            third_stats(1)
            scale_down(3)
            third_norm(1)
            third_stats(2)
            q_low(0)
            third_stats(3)
            third_norm(2)
            third_norm(3)
            q_low(1)
            q_low(2)
            q_low(3)

            def step_c(s):
                m, o = s + 1, s + (-1)

                def maximum(u):
                    gp, qt, j = u // 8, u // 4 % 2, u % 4
                    dve.wait_ge(sem("s_done"), 16 * m.n + u + 1)
                    if u == 0:
                        wait(dve, sem("max_split"), 2 * m.n - 2)
                    dve.tensor_reduce(nmax[m.par][:, gp, qt, :, j],
                                      bank[QUERY_BANKS[u % 3]][:, :].rearrange("p (r s) -> p r s", r=2), AX.X, ALU.max,
                                      negate=True).then_inc(sem("s_maxed"), 1)

                def split_maxima(b, gp):
                    i = 2 * b.n + gp
                    pad = neg_max_pad[b.par][:, gp, :, :, :].rearrange("p t g (j c) -> p (t g j) c", c=32)
                    nm = nmax[b.par][:, gp, :, :, :].rearrange("p t g j -> p (t g j)").unsqueeze(2)
                    dve.wait_ge(sem("s_maxed"), 16 * b.n + 8 * gp + 8)
                    wait(dve, sem("max_turned"), i - 3)
                    dve.tensor_copy(pad[:, :, MROW:MROW + 1], nm).then_inc(sem("max_hi"), 1)
                    dve.wait_ge(sem("max_hi"), i + 1)
                    dve.tensor_tensor(pad[:, :, MROW + 1:MROW + 2], nm, pad[:, :, MROW:MROW + 1].bitcast(F32),
                                      ALU.subtract).then_inc(sem("max_split"), 1)

                def shift_q(b, gp):
                    dve.wait_ge(sem("max_turned"), 2 * b.n + gp + 1)
                    qs = q_st[b.par][:, 2 * gp:2 * gp + 2, :]
                    dve.tensor_tensor(qs, bank[5][:, :].rearrange("p (g s) -> p g s", g=2),
                                      qs.bitcast(F32), ALU.add).then_inc(sem("q_shifted"), 1)

                for k in range(C_SLOTS):
                    if s.valid and k == 0:
                        split_maxima(s, 1)
                    if s.valid and k == 0:
                        shift_q(s, 1)
                    if o.valid and k == 1:
                        dve.wait_ge(sem("sums_turned"), o.n + 1)
                        wait(dve, sem("inv_widened"), o.n)
                        dve.reciprocal(sums_inv[:, :, :, :].rearrange("p t u w -> p (t u w)"),
                                       bank[7][:, :].rearrange("p (w c) -> p w c", c=16)[:, :, HD])\
                           .then_inc(sem("sums_inverted"), 1)
                    if o.valid and k == 4:
                        dve.wait_ge(sem("inv_spread"), o.n + 1)
                        wait(dve, sem("wo_done"), o.n)
                        dve.tensor_tensor(on[:, :], av[:, :], bank[7][:, :], ALU.mult).then_inc(sem("on_ready"), 1)
                    if is_step(s, BATCH) and k == 2:
                        cut_expert(Step(0, 0, EXPERTS))
                    if is_step(s, BATCH) and k == 8:
                        top_two(0, TILES - BT)
                    if o.valid and k == 8:
                        dve.wait_ge(sem("wo_done"), o.n + 1)
                        xb = x[:, ds(o.n * SEQ, SEQ)]
                        dve.scalar_tensor_tensor(xb, bank[7][:, 0:256], tg[:, 1:2], xb, ALU.mult, ALU.add)\
                           .then_inc(sem("x3_done"), 1)
                    if o.valid and k == 10:
                        dve.wait_ge(sem("x3_done"), o.n + 1)
                        halves_of(o.par, 2, o.n * SEQ)
                    if o.valid and k == 11:
                        variances_of(o.n + (LN4 + 1), o.par, 2)
                    if m.valid and k == 9:
                        split_maxima(m, 0)
                    if m.valid and k == 13:
                        shift_q(m, 0)
                    if is_step(s, BATCH) and k == 16:
                        split_hidden(Step(0, 0, EXPERTS), 0)
                    if o.valid and k == 17:
                        dve.wait_ge(sem("xt_hi_done"), o.n + 1)
                        dve.tensor_tensor(xt_lo[:, ds(o.n * SEQ, SEQ)], bank[7][:, 0:256],
                                          xt_hi[:, ds(o.n * SEQ, SEQ)].bitcast(F32), ALU.subtract)\
                           .then_inc(sem("xt_split"), 2)
                    if m.valid and 0 <= k - QUERY_LAG < 16:
                        maximum(k - QUERY_LAG)

            def top_two(first, last):
                group = 0 if first == 0 else 1
                dve.wait_ge(sem("gates_turned"), group + 1)
                dve.tensor_copy(gates[:, first:last, :],
                                bank[4][:, EXPERTS * first:EXPERTS * last].rearrange("p (i e) -> p i e", e=EXPERTS))\
                   .then_inc(sem("v_gates"), 1)
                dve.wait_ge(sem("v_gates"), 3 * group + 1)
                for i in range(first, last):
                    ins = dve.max(top[:, i, :], gates[:, i, :])
                ins.then_inc(sem("v_gates"), 1)
                dve.wait_ge(sem("v_gates"), 3 * group + 2)
                for i in range(first, last):
                    ins = dve.max_index(top_i[:, i, :], top[:, i, :], gates[:, i, :])
                ins.then_inc(sem("v_gates"), 1)


            def weigh(y, s, k):
                if is_step(s, 0):
                    dve.wait_ge(sem(f"wtok_first{k}"), 16)
                elif k == 0:
                    dve.wait_ge(sem(f"wtok_landed{s.par}"), 16 * (s.half + s.par))
                dve.wait_ge(sem("y_done"), y + 1)
                dve.scalar_tensor_tensor(ytmp[k % 2][:, :], bank[4 + k][:, :], cols[:, ds(B2C + s.n, 1)],
                                         w_tok[s.par][:, k * BLK:(k + 1) * BLK], ALU.add, ALU.mult)\
                   .then_inc(sem("y_weighed"), 1)
                dve.wait_ge(sem("y_weighed"), y + 1)
                ab_ = acc[:, k * BLK:(k + 1) * BLK]
                dve.tensor_tensor(ab_, ab_, ytmp[k % 2][:, :], ALU.add).then_inc(sem("acc_added"), 1)

            def split_hidden(s, k):
                y = NBLK * s.n + k
                wait(dve, sem("y_done"), y - 1)
                for ch in range(HC):
                    dve.wait_ge(sem("gelued"), HC * y + ch + 1)
                    dve.tensor_copy(hid_hi[k % 2][:, ch, :], hid[k % 2][:, ch, :]).then_inc(sem("hid_hi_done"), 1)
                    if ch not in POOL_CH:
                        dve.wait_ge(sem("hid_hi_done"), HC * y + ch + 1)
                        dve.tensor_tensor(hid_lo[k % 2][:, ch, :], hid[k % 2][:, ch, :],
                                          hid_hi[k % 2][:, ch, :].bitcast(F32), ALU.subtract)\
                           .then_inc(sem("dve_low"), 1)

            def split_and_weigh(s):
                for k in range(NBLK):
                    if not (is_step(s, 0) and k < 2):
                        split_hidden(s, k)
                    before = s if k == NBLK - 1 else s + (-1)
                    if before.valid:
                        weigh(NBLK * s.n + k - 3, before, (k + 1) % NBLK)
                    if k == 1 and (s + 1).valid:
                        cut_expert(s + 1)

            skewed(dve, step_c, BATCH, lead=2)
            top_two(TILES - BT, TILES)
            dve.tensor_tensor(soft[:, 0, :], top[:, :, 1], top[:, :, 0], ALU.subtract).then_inc(sem("top_gap"), 1)
            dve.wait_ge(sem("v_gates"), 6)
            dve.tensor_copy(top_f[:, :, :], top_i[:, :, 0:2]).then_inc(sem("v_top"), 1)
            split_hidden(Step(0, 0, EXPERTS), 1)
            dve.wait_ge(sem("top_exp"), 1)
            dve.tensor_scalar(soft[:, 2, :], soft[:, 1, :], 1.0, None, ALU.add).then_inc(sem("v_top"), 1)
            dve.wait_ge(sem("v_top"), 2)
            dve.reciprocal(soft[:, 2, :], soft[:, 2, :]).then_inc(sem("v_top"), 1)
            dve.wait_ge(sem("v_top"), 3)
            dve.tensor_tensor(soft[:, 3, :], soft[:, 2, :], soft[:, 1, :], ALU.mult).then_inc(sem("v_top"), 1)
            dve.wait_ge(sem("moe_set"), 1)
            full = [P, TILES, EXPERTS]
            for k in range(2):
                dve.tensor_tensor(pick[k][:, :, :], eidx[:, :].unsqueeze(1).broadcast_to(full),
                                  top_f[:, :, k].unsqueeze(2).broadcast_to(full), ALU.is_equal)\
                   .then_inc(sem("v_top"), 1)
            dve.wait_ge(sem("v_top"), 6)
            for k in range(2):
                dve.tensor_tensor(pick[k][:, :, :], pick[k][:, :, :],
                                  soft[:, 2 + k, :].unsqueeze(2).broadcast_to(full), ALU.mult)\
                   .then_inc(sem("v_top"), 1)
            dve.wait_ge(sem("v_top"), 8)
            dve.tensor_tensor(wte[:, :, :], pick[0][:, :, :], pick[1][:, :, :], ALU.add).then_inc(sem("wte_ready"), 1)
            dve.wait_ge(sem("moe_set"), 2)
            over_experts(dve, split_and_weigh)
            def add_moe(k):
                dve.wait_ge(sem("out_done"), k + 1)
                xb = x[:, k * BLK:(k + 1) * BLK]
                dve.scalar_tensor_tensor(xb, bank[k][:, :], tg[:, 3:4], xb, ALU.mult, ALU.add)\
                   .then_inc(sem("x_final"), 1)

            for k in range(1, NBLK):
                weigh(NBLK * (EXPERTS - 1) + k, Step(0, EXPERTS - 1, EXPERTS), k)
            for k in range(NBLK):
                add_moe(k)

        @block.tensor
        def _(pe):
            def mm(out, lhsT, rhs, start=True, stop=True, **kw):
                return pe.matmul(out, lhsT, rhs, start=start, stop=stop, **kw)

            pe.wait_ge(sem("ident_set"), 1)

            def step_a(s):
                m, b, o = s + 1, s + (-1), s + (-2)
                start = isinstance(s.it, int) and s.n == -1
                ct, xt = cx_t[m.par][:, 0:256], cx_t[m.par][:, 256:512]
                if s.valid:
                    wait(pe, sem("masked"), s.n)
                    pe.wait_ge(sem("qk0_ready"), s.n + 1)
                    mm(bank[4][:, 0:128], qk0[s.par][:, 0:128], qk0[s.par][:, 256:384])
                    mm(bank[4][:, 128:384], qk0[s.par][:, 128:256], qk0[s.par][:, 256:512])\
                        .then_inc(sem("scored"), 1)
                if b.valid:
                    pe.wait_ge(sem("probs0_done"), b.n + 1)
                    wait(pe, sem("probs0_t_ready"), b.n)
                    for i in range(3):
                        ins = pe.transpose(bank[5][:, P * i:P * i + P], probs0[b.par][:, P * i:P * i + P], ident[:, :])
                    ins.then_inc(sem("probs0_turned"), 1)
                if m.valid:
                    pe.wait_ge(sem(f"ctx_landed{m.par}"), 16 * (m.half + 1))
                    pe.wait_ge(sem("xn1_ready"), m.n + 1)
                    wait(pe, sem("cx_ready"), m.n)
                    for i in range(2):
                        pe.transpose(bank[0][:, P * i:P * i + P], ctx_in[m.par][:, i, :], ident[:, :])
                    for i in range(2):
                        ins = pe.transpose(bank[0][:, 256 + P * i:256 + P * i + P], xn1[m.par][:, i, :], ident[:, :])
                    ins.then_inc(sem("cx_turned"), 1)
                if b.valid:
                    pe.wait_ge(sem("probs0_t_ready"), b.n + 1)
                    pe.wait_ge(sem("v0_ready"), b.n + 1)
                    wait(pe, sem("x1_done"), b.n)
                    pt, vv = probs0_t[b.par], v0[b.par]
                    mm(bank[6][:, 0:128], pt[:, 0:128], vv[:, 0:128])
                    mm(bank[6][:, 128:256], pt[:, 128:256], vv[:, 0:128], stop=False)
                    mm(bank[6][:, 128:256], pt[:, 256:384], vv[:, 128:256], start=False).then_inc(sem("attended0"), 1)
                if o.valid:
                    pe.wait_ge(sem("xn2_ready"), o.n + 1)
                    wait(pe, sem("xn2_t_ready"), o.n)
                    for i in range(2):
                        ins = pe.transpose(bank[7][:, P * i:P * i + P], xn2[o.par][:, P * i:P * i + P], ident[:, :])
                    ins.then_inc(sem("xn2_turned"), 1)
                if m.valid:
                    if start:
                        pe.wait_ge(sem("rows_landed"), 64)
                        pe.transpose(bank[6][:, 0:64], rows[:, :], ident[0:64, 0:64]).then_inc(sem("cols_turned"), 1)
                        pe.wait_ge(sem("wa_landed"), 80)
                    pe.wait_ge(sem("cx_ready"), m.n + 1)
                    wait(pe, sem("qk0_ready"), m.n)
                    mm(bank[1][:, 0:256], wq0[:, :], ct)
                    mm(bank[1][:, 256:512], wk0[:, :], xt).then_inc(sem("qk0_projected"), 1)
                if m.valid:
                    pe.wait_ge(sem("cx_ready"), m.n + 1)
                    wait(pe, sem("v0_ready"), m.n)
                    wait(pe, sem("v1_ready"), m.n)
                    for i in range(2):
                        mm(bank[2][:, P * i:P * i + P], ct[:, P * i:P * i + P], wv0[:, :])
                    for i in range(2):
                        ins = mm(bank[2][:, 256 + P * i:256 + P * i + P], ct[:, P * i:P * i + P], wv1[:, :])
                    ins.then_inc(sem("v_projected"), 1)
                if m.valid:
                    pe.wait_ge(sem("cx_ready"), m.n + 1)
                    wait(pe, sem("k_split"), 2 * m.n)
                    mm(bank[3][:, 0:256], wk1[:, :], ct).then_inc(sem("k1_projected"), 1)

            skewed(pe, step_a, BATCH, lag=2)

            pe.wait_ge(sem("w_rounded"), 2)
            pe.wait_ge(sem("v_const"), 6)
            pe.wait_ge(sem("cx_ready"), BATCH)
            pe.wait_ge(sem("qk0_ready"), BATCH)
            wg_ps = bank[0][:, :].bitcast(BF16)
            wd_ps = bank[1][:, :].bitcast(BF16)
            for k in range(2 * CH):
                ins = pe.transpose(wg_ps[:, k * P:(k + 1) * P], w_q8[:, k, :], ident_b[:, :])
            ins.then_inc(sem("ffn_w_turned"), 1)
            for k in range(CH):
                ins = pe.transpose(wd_ps[0:CHW[k], k * P:k * P + P], wd_q8[:, k * P:k * P + CHW[k]], ident_b[:, :])
            ins.then_inc(sem("ffn_w_turned"), 1)
            pe.wait_ge(sem("sd_diag"), 1)
            pe.wait_ge(sem("consts_set"), 4)
            pe.wait_ge(sem("xn2_t_ready"), BATCH)
            mm(bank[7][:, 0:DM], ones[:, :], sd_row[:, :]).then_inc(sem("sd_spread"), 1)

            pe.wait_ge(sem("ffn_w_ready"), 3)
            pe.wait_ge(sem("v0_ready"), BATCH)
            pe.wait_ge(sem("k_split"), 2 * BATCH)
            pe.wait_ge(sem("masked"), BATCH)
            pe.wait_ge(sem("probs0_t_ready"), BATCH)

            def gate_up(s0, s1):
                for s in (s0, s1):
                    pe.wait_ge(sem("x_rounded"), s.n + 1)
                    for ch in range(CH):
                        w = CHW[ch]
                        wait(pe, sem("silued"), CH * s.n + ch - (CH - 1))
                        mm(bank[2 * ch][0:w, :], wgu_t[:, ch, 0:w], xq[:, ds(s.n * BLK, BLK)])\
                            .then_inc(sem("gated"), 1)
                        wait(pe, sem("h_done"), CH * s.n + ch - (CH - 1))
                        mm(bank[2 * ch + 1][0:w, :], wgu_t[:, CH + ch, 0:w], xq[:, ds(s.n * BLK, BLK)])\
                            .then_inc(sem("upped"), 1)

            paired(pe, gate_up, NBLK)
            pe.wait_ge(sem("h_done"), CH * NBLK)
            pe.wait_ge(sem("wc_landed"), 16 * (3 + 2 * QUADS + 1))

            def down_product(k):
                pe.wait_ge(sem("h_rounded"), CH * (k + 1))
                if k >= 2:
                    pe.wait_ge(sem("down_scaled"), k - 1)
                for i in range(BT):
                    for ch in range(CH):
                        w = CHW[ch]
                        ins = mm(bank[k % 2][:, i * P:(i + 1) * P], hq[k % 2][0:w, ch, i * P:(i + 1) * P],
                                 wd_t[0:w, ch, :], start=(ch == 0), stop=(ch == CH - 1))
                ins.then_inc(sem("downed"), 1)

            def project_q(k):
                pe.wait_ge(sem("xn3_ready"), k + 1)
                if k >= 2:
                    pe.wait_ge(sem("xn3_t_ready"), k - 1)
                for i in range(BT):
                    ins = pe.transpose(bank[2 + k % 2][:, P * i:P * i + P], xn3[k % 2][:, P * i:P * i + P], ident[:, :])
                ins.then_inc(sem("xn3_turned"), 1)
                pe.wait_ge(sem("xn3_t_ready"), k + 1)
                if k >= 2:
                    pe.wait_ge(sem("q_split"), 2 * (k - 1))
                mm(bank[4 + k % 2][:, :], wq1[:, :], xn3_t[k % 2][:, :]).then_inc(sem("q_projected"), 1)

            for k in range(NBLK):
                down_product(k)
            for k in range(NBLK):
                project_q(k)

            pe.wait_ge(sem("q_split"), 2 * NBLK)

            def step_c(s):
                m, o = s + 1, s + (-1)

                def slot_q(b, u):
                    wait(pe, sem("q_shifted"), 2 * b.n - 2 + u + 1)
                    for gg in range(2):
                        g = 2 * u + gg
                        mm(bank[5][:, gg * SEQ:(gg + 1) * SEQ], sel["qhi"][:, g, :],
                           q_hi[:, ds(b.n * SEQ, SEQ)], stop=False)
                        ins = mm(bank[5][:, gg * SEQ:(gg + 1) * SEQ], sel["qlo"][:, g, :],
                                 q_lo[:, ds(b.n * SEQ, SEQ)], start=False)
                    ins.then_inc(sem("q_slotted"), 1)

                def by_query(u):
                    gp, qt, j = u // 8, u // 4 % 2, u % 4
                    if u % 8 == 0:
                        pe.wait_ge(sem("q_staged"), 2 * m.n + gp + 1)
                        pe.wait_ge(sem(f"k_staged{m.par}{gp}"), 64 * (m.half + 1))
                    wait(pe, sem("s_maxed"), 16 * m.n + (u - 2 if u else 0))
                    for r in range(2):
                        g = 2 * gp + r
                        ins = mm(bank[QUERY_BANKS[u % 3]][:, r * SEQ:(r + 1) * SEQ],
                                 q_st[m.par][:, g, qt * P:(qt + 1) * P], k_quad[m.par][:, j, g, :])
                    ins.then_inc(sem("s_done"), 1)

                def by_key(u):
                    gp, kt, j = u // 8, u // 4 % 2, u % 4
                    if u % 8 == 0:
                        pe.wait_ge(sem("q_shifted"), 2 * s.n + gp + 1)
                    wait(pe, sem("exped"), 16 * s.n + u - 1)
                    for r in range(2):
                        g = 2 * gp + r
                        ins = mm(bank[2 + u % 2][:, r * SEQ:(r + 1) * SEQ],
                                 k_quad[s.par][:, j, g, kt * P:(kt + 1) * P], q_st[s.par][:, g, :])
                    ins.then_inc(sem("st_done"), 1)

                def attend(quad, r):
                    gp, kt = quad // 2, quad % 2
                    if r == 0:
                        pe.wait_ge(sem("exped"), 16 * s.n + 4 * quad + 4)
                    if quad == 0 and r == 0:
                        pe.wait_ge(sem("v_widened"), 4 * s.n + 4)
                        wait(pe, sem("av_ready"), s.n)
                    for j in range(QUADS):
                        c0 = 32 * (2 * (4 * gp + j) + r)
                        ins = mm(bank[4][32 * j:32 * j + 32, gp * SEQ:(gp + 1) * SEQ],
                                 v_st[s.par][:, kt, c0:c0 + 32], probs[quad % 2][:, j, r, :],
                                 start=(kt == 0 and r == 0), stop=(kt == 1 and r == 1),
                                 tile_position=(0, 32 * j))
                    if r == 1:
                        ins.then_inc(sem("attended"), 1)

                def turn_maxima(b, gp):
                    pe.wait_ge(sem("max_split"), 2 * b.n + gp + 1)
                    pe.wait_ge(sem("q_staged"), 2 * b.n + (3 if gp and m.valid else 2))
                    for gg in range(2):
                        for qt in range(2):
                            ins = mm(bank[5][:, gg * SEQ + qt * P:gg * SEQ + (qt + 1) * P],
                                     neg_max_pad[b.par][:, gp, qt, gg, :], ident_r[:, :])
                    ins.then_inc(sem("max_turned"), 1)

                for k in range(C_SLOTS):
                    if is_step(s, -1) and k == 0:
                        slot_q(m, 0)
                    if is_step(s, BATCH) and k == 0:
                        project_gates(0)
                    if is_step(s, BATCH) and k == 4:
                        project_gates(1)
                        project_gates(2)
                    if is_step(s, BATCH) and k == 5:
                        turn_gates(0, TILES - BT)
                    if is_step(s, BATCH) and k == 10:
                        hidden(Step(0, 0, EXPERTS), 0)
                    if is_step(s, BATCH) and k == 14:
                        hidden(Step(0, 0, EXPERTS), 1)
                    if s.valid and k == 2:
                        turn_maxima(s, 1)
                    if o.valid and k == 2:
                        pe.wait_ge(sem("av_ready"), o.n + 1)
                        wait(pe, sem("xt_split"), 2 * o.n)
                        for qt in range(2):
                            for u in range(2):
                                c0 = (2 * qt + u) * P
                                ins = pe.transpose(bank[7][:, c0:c0 + P],
                                                   av[:, u * SEQ + qt * P:u * SEQ + (qt + 1) * P], ident[:, :])
                        ins.then_inc(sem("sums_turned"), 1)
                    if m.valid and k == 4:
                        slot_q(m, 1)
                    if (s + 2).valid and k == 16:
                        slot_q(s + 2, 0)
                    if o.valid and k == 5:
                        pe.wait_ge(sem("inv_widened"), o.n + 1)
                        for u in range(2):
                            for qt in range(2):
                                ins = mm(bank[7][:, u * SEQ + qt * P:u * SEQ + (qt + 1) * P], inv_wide[:, qt, u, :],
                                         ident[:, :])
                        ins.then_inc(sem("inv_spread"), 1)
                    if o.valid and k == 8:
                        pe.wait_ge(sem("on_ready"), o.n + 1)
                        for qt in range(2):
                            for u in range(2):
                                ins = mm(bank[7][:, qt * P:(qt + 1) * P],
                                         on[:, u * SEQ + qt * P:u * SEQ + (qt + 1) * P],
                                         we_pad[:, u, :], start=(u == 0), stop=(u == 1))
                        ins.then_inc(sem("wo_done"), 1)
                    if m.valid and k == 12:
                        turn_maxima(m, 0)
                    if o.valid and k == 16:
                        pe.wait_ge(sem("xn4_ready"), o.n + 1)
                        for i in range(2):
                            ins = pe.transpose(bank[7][:, P * i:P * i + P], xn4[:, P * i:P * i + P], ident[:, :])
                        ins.then_inc(sem("xn4_turned"), 1)
                    if s.valid and k < 16:
                        by_key(k)
                    if m.valid and 0 <= k - QUERY_LAG < 16:
                        by_query(k - QUERY_LAG)
                    if s.valid and k >= 4 + 1 and k % 4 == 1:
                        attend(k // 4 - 1, 0)
                        attend(k // 4 - 1, 1)

            def project_gates(k):
                cs = slice(k * BLK, (k + 1) * BLK)
                if k == 0:
                    pe.wait_ge(sem("gw_split"), 2)
                    pe.wait_ge(sem("s_maxed"), 16 * BATCH)
                    pe.wait_ge(sem("exped"), 16 * BATCH)
                pe.wait_ge(sem("xt_split"), 2 * (2 * k + 2))
                mm(bank[GATE_BANKS[k]][0:EXPERTS, :], gate_hi[:, :], xt_hi[:, cs], stop=False)
                mm(bank[GATE_BANKS[k]][0:EXPERTS, :], gate_hi[:, :], xt_lo[:, cs], start=False, stop=False)
                mm(bank[GATE_BANKS[k]][0:EXPERTS, :], gate_lo[:, :], xt_hi[:, cs], start=False).then_inc(sem("gates_done"), 1)

            def turn_gates(first, last):
                pe.wait_ge(sem("av_ready"), BATCH)
                pe.wait_ge(sem("gates_t_ready"), last // BT)
                if first:
                    pe.wait_ge(sem("v_gates"), 1)
                for i in range(first, last):
                    ins = pe.transpose(bank[4][:, EXPERTS * i:EXPERTS * (i + 1)], gates_t[:, i * P:(i + 1) * P],
                                       ident[0:EXPERTS, 0:EXPERTS])
                ins.then_inc(sem("gates_turned"), 1)

            def hidden(s, k):
                y = NBLK * s.n + k
                cs = slice(k * BLK, (k + 1) * BLK)
                if k == 0:
                    pe.wait_ge(sem("w_cut"), 4 * s.n + 4)
                for ch in range(HC):
                    wait(pe, sem("gelued"), HC * y + ch - (HC - 1))
                    wc = slice(ch * P, (ch + 1) * P)
                    mm(bank[ch][:, :], w1_hi[s.par][:, wc], xt_hi[:, cs], stop=False)
                    mm(bank[ch][:, :], w1_hi[s.par][:, wc], xt_lo[:, cs], start=False, stop=False)
                    mm(bank[ch][:, :], w1_lo[s.par][:, wc], xt_hi[:, cs], start=False).then_inc(sem("hid_done"), 1)

            def output(s, k):
                y = NBLK * s.n + k
                out = bank[4 + k][:, :]
                wait(pe, sem("y_weighed"), y - 3)
                if is_step(s, 0):
                    pe.wait_ge(sem("v_gates"), 4)
                    if k == NBLK - 1:
                        pe.wait_ge(sem("wte_turned"), NBLK)
                for ch in range(HC):
                    hi, lo = hid_hi[k % 2][:, ch, :], hid_lo[k % 2][:, ch, :]
                    pe.wait_ge(sem("hid_hi_done"), HC * y + ch + 1)
                    mm(out, w2_hi[s.par][:, ch, :], hi, start=(ch == 0), stop=False)
                    mm(out, w2_lo[s.par][:, ch, :], hi, start=False, stop=False)
                    if ch in POOL_CH:
                        pe.wait_ge(sem("pool_low"), len(POOL_CH) * y + POOL_CH.index(ch) + 1)
                    else:
                        pe.wait_ge(sem("dve_low"), (HC - len(POOL_CH)) * y + ch - len(POOL_CH) + 1)
                    ins = mm(out, w2_hi[s.par][:, ch, :], lo, start=False, stop=(ch == HC - 1))
                ins.then_inc(sem("y_done"), 1)

            skewed(pe, step_c, BATCH, lead=2)
            project_gates(3)
            turn_gates(TILES - BT, TILES)

            def turn_weights():
                pe.wait_ge(sem("wte_ready"), 1)
                for i in range(TILES):
                    k, p0 = i // BT, 32 * (i // BT)
                    ins = mm(bank[7][p0:p0 + EXPERTS, (i % BT) * P:(i % BT + 1) * P], wte[:, i, :],
                             ident[:, :], tile_position=(0, p0))
                ins.then_inc(sem("wte_turning"), 1)

            def expert(s):
                for k in range(NBLK):
                    if k == NBLK - 1:
                        if (s + 1).valid:
                            hidden(s + 1, 0)
                    elif not (is_step(s, 0) and k == 0):
                        hidden(s, k + 1)
                    if is_step(s, 0) and k == 2:
                        turn_weights()
                    output(s, k)

            over_experts(pe, expert)

            pe.wait_ge(sem("gelued"), HC * NBLK * EXPERTS)
            for k in range(NBLK):
                pe.wait_ge(sem("acc_added"), NBLK * (EXPERTS - 1) + k + 1)
                for i in range(BT):
                    tok = slice(k * BLK + i * P, k * BLK + (i + 1) * P)
                    ins = pe.transpose(bank[k][:, i * P:(i + 1) * P], acc[:, tok], ident[:, :])
                ins.then_inc(sem("out_done"), 1)


_INS = ["x", "ctx_1024", "g_xattn", "g_ffn", "L0_xattn_WK", "L0_xattn_WQ", "L0_xattn_WV", "L0_ffn_clip_x",
        "L0_ffn_clip_down", "L0_ffn_w_gate", "L0_ffn_w_up", "L0_ffn_w_down", "L1_xattn_Wq", "L1_xattn_bq",
        "L1_xattn_Wk", "L1_xattn_bk", "L1_xattn_Wv", "L1_xattn_bv", "L1_xattn_We", "L1_xattn_be",
        "L1_ffn_gate_w", "L1_ffn_gate_b", "L1_ffn_w1", "L1_ffn_b1", "L1_ffn_w2", "L1_ffn_b2"]


def kernel(**inputs):
    import concourse.bacc as bacc
    from concourse.bass_utils import run_bass_kernel_spmd

    nc = bacc.Bacc("TRN2", target_bir_lowering=False, num_devices=1)
    arrays, t = {}, {}
    for name in _INS:
        a = np.ascontiguousarray(inputs[name])
        arrays[f"in_{name}"] = a
        t[name] = nc.dram_tensor(f"in_{name}", a.shape, mybir.dt.from_np(a.dtype), kind="ExternalInput").ap()
    t["out"] = nc.dram_tensor("out_x", (BATCH, SEQ, DM), F32, kind="ExternalOutput").ap()
    flamingo(nc, t)
    r = run_bass_kernel_spmd(nc, [arrays], core_ids=[0])
    return r.results[0]["out_x"]
```
